# Optimizing a Trainium2 kernel written in Bass

```python
import numpy as np
import jax
import jax.numpy as jnp

def _softmax(x, axis=-1):
    return jax.nn.softmax(x, axis=axis)

def _gelu(x):
    return jax.nn.gelu(x, approximate=True)

def _silu(x):
    return jax.nn.silu(x)

def _sigmoid(x):
    return jax.nn.sigmoid(x)

def _layernorm(x, axis=-1, eps=1e-05):
    m = jnp.mean(x, axis=axis, keepdims=True)
    v = jnp.var(x, axis=axis, keepdims=True)
    return (x - m) / jnp.sqrt(v + eps)

def _scatter_add(tgt, idx, src, axis=0):
    return tgt.at[idx].add(src)

def _segment_sum(src, seg, n):
    return jax.ops.segment_sum(src, seg, n)
kernel_name = 'mk_prb_d2_jaxref_r8_f192ae'

def setup_inputs(seed: int=0):
    np.random.seed(seed)
    _w = jnp.asarray

    def _L0_attn_setup():
        import jax, jax.numpy as jnp
        import numpy as np
        key = jax.random.key(seed)
        ks = jax.random.split(key, 5)
        B, S, D = (1, 512, 256)
        H, Dh = (16, 128)
        scale = 1.0 / np.sqrt(D).astype(np.float32)
        return {'x': jax.random.normal(ks[0], (B, S, D), dtype=jnp.float32), 'W_K': jax.random.normal(ks[1], (H, Dh, D), dtype=jnp.float32) * scale, 'W_Q': jax.random.normal(ks[2], (H, Dh, D), dtype=jnp.float32) * scale, 'W_V': jax.random.normal(ks[3], (H, Dh, D), dtype=jnp.float32) * scale, 'W_O': jax.random.normal(ks[4], (D, H * Dh), dtype=jnp.float32) * scale}
    _L0_attn_in = _L0_attn_setup()

    def _L0_ffn_setup():
        import jax, jax.numpy as jnp
        import numpy as np

        def binarize_weight(w):
            alpha = jnp.mean(jnp.abs(w), axis=tuple(range(1, w.ndim)), keepdims=True)
            bw = jnp.where(w >= 0, 1.0, -1.0) * alpha
            return jax.lax.stop_gradient(bw - w) + w
        key = jax.random.key(seed)
        k1, k2, k3 = jax.random.split(key, 3)
        in_features, out_features = (256, 256)
        x = jax.random.normal(k1, (8, 256, in_features), dtype=jnp.float32)
        std = np.sqrt(2.0 / out_features).astype(np.float32)
        weight = jax.random.normal(k2, (out_features, in_features), dtype=jnp.float32) * std
        bias = jax.random.normal(k3, (out_features,), dtype=jnp.float32) * 0.01
        return {'x': x, 'weight': weight, 'bias': bias}
    _L0_ffn_in = _L0_ffn_setup()

    def _L1_attn_setup():
        import jax, jax.numpy as jnp
        import numpy as np
        from jax import lax
        H, P, N, G, K, CHUNK = (64, 64, 128, 1, 4, 32)
        D_MODEL = 256
        D_INNER = H * P
        CONV_DIM = D_INNER + 2 * G * N
        EPS = 1e-05

        def _mamba2_forward(hidden_states, in_proj_w, conv_w, conv_b, dt_bias, A_log, D_param, norm_w, out_proj_w):
            b, l, _ = hidden_states.shape
            c = l // CHUNK
            proj = hidden_states @ in_proj_w
            gate = proj[..., :D_INNER]
            hbc = proj[..., D_INNER:D_INNER + CONV_DIM]
            dt = proj[..., D_INNER + CONV_DIM:]
            xt = hbc.transpose(0, 2, 1)
            y = lax.conv_general_dilated(xt, conv_w[:, None, :], window_strides=(1,), padding=[(K - 1, 0)], feature_group_count=CONV_DIM, dimension_numbers=('NCH', 'OIH', 'NCH'))
            hbc = jax.nn.silu(y + conv_b[None, :, None]).transpose(0, 2, 1)
            per_g = D_INNER // G
            hg = hbc.reshape(b, l, G, per_g + 2 * N)
            x = hg[..., :per_g].reshape(b, l, H, P)
            Bm = hg[..., per_g:per_g + N]
            Cm = hg[..., per_g + N:]
            hpg = H // G
            Bh = jnp.repeat(Bm, hpg, axis=2)
            Ch = jnp.repeat(Cm, hpg, axis=2)
            dt = jax.nn.softplus(dt + dt_bias)
            A = -jnp.exp(A_log)
            x_c = x.reshape(b, c, CHUNK, H, P)
            B_c = Bh.reshape(b, c, CHUNK, H, N)
            C_c = Ch.reshape(b, c, CHUNK, H, N)
            dt_c = dt.reshape(b, c, CHUNK, H)
            dA = dt_c * A[None, None, None, :]
            cum = jnp.cumsum(dA, axis=2)
            diff = cum[:, :, :, None, :] - cum[:, :, None, :, :]
            i = jnp.arange(CHUNK)
            mask = i[:, None] >= i[None, :]
            decay = jnp.exp(jnp.where(mask[None, None, :, :, None], diff, -jnp.inf))
            scores = jnp.einsum('bcihn,bcjhn->bcijh', C_c, B_c) * decay * dt_c[:, :, None, :, :]
            Y_diag = jnp.einsum('bcijh,bcjhp->bcihp', scores, x_c)
            decay_states = jnp.exp(cum[:, :, -1:, :] - cum)
            states = jnp.einsum('bclh,bclhn,bclhp->bchpn', decay_states * dt_c, B_c, x_c)
            chunk_decay = jnp.exp(cum[:, :, -1, :])

            def step(prev, inp):
                st, cd = inp
                new = cd[:, :, None, None] * prev + st
                return (new, prev)
            init = jnp.zeros((b, H, P, N), hidden_states.dtype)
            _, prev_states = lax.scan(step, init, (jnp.moveaxis(states, 1, 0), jnp.moveaxis(chunk_decay, 1, 0)))
            prev_states = jnp.moveaxis(prev_states, 0, 1)
            state_decay_out = jnp.exp(cum)
            Y_off = jnp.einsum('bclhn,bchpn,bclh->bclhp', C_c, prev_states, state_decay_out)
            yh = (Y_diag + Y_off).reshape(b, l, H, P) + D_param[None, None, :, None] * x
            yr = yh.reshape(b, l, D_INNER)
            hidden = yr * jax.nn.silu(gate)
            var = jnp.mean(hidden * hidden, axis=-1, keepdims=True)
            hidden = hidden * lax.rsqrt(var + EPS) * norm_w
            return hidden @ out_proj_w
        key = jax.random.key(seed)
        ks = jax.random.split(key, 6)
        s = lambda k, shape, scale: jax.random.normal(k, shape, jnp.float32) * scale
        return {'hidden_states': s(ks[0], (2, 256, D_MODEL), 1.0), 'in_proj_w': s(ks[1], (D_MODEL, D_INNER + CONV_DIM + H), D_MODEL ** (-0.5)), 'conv_w': s(ks[2], (CONV_DIM, K), K ** (-0.5)), 'conv_b': jnp.zeros((CONV_DIM,), jnp.float32), 'dt_bias': jnp.ones((H,), jnp.float32), 'A_log': jnp.log(jnp.arange(1, H + 1, dtype=jnp.float32)), 'D_param': jnp.ones((H,), jnp.float32), 'norm_w': jnp.ones((D_INNER,), jnp.float32), 'out_proj_w': s(ks[3], (D_INNER, D_MODEL), D_INNER ** (-0.5))}
    _L1_attn_in = _L1_attn_setup()

    def _L1_ffn_setup():
        import jax, jax.numpy as jnp
        import numpy as np
        HIDDEN = 256
        INTER = 704
        B, S = (2, 256)

        def _ternary(key, shape):
            return jax.random.randint(key, shape, -1, 2).astype(jnp.float32)
        key = jax.random.key(seed)
        ks = jax.random.split(key, 7)
        x = jax.random.normal(ks[0], (B, S, HIDDEN), dtype=jnp.float32)
        gate_w = _ternary(ks[1], (INTER, HIDDEN))
        up_w = _ternary(ks[2], (INTER, HIDDEN))
        down_w = _ternary(ks[3], (HIDDEN, INTER))
        gate_s = jax.random.uniform(ks[4], (INTER,), minval=0.01, maxval=0.1, dtype=jnp.float32)
        up_s = jax.random.uniform(ks[5], (INTER,), minval=0.01, maxval=0.1, dtype=jnp.float32)
        down_s = jax.random.uniform(ks[6], (HIDDEN,), minval=0.01, maxval=0.1, dtype=jnp.float32)
        return {'x': x, 'gate_w': gate_w, 'up_w': up_w, 'down_w': down_w, 'gate_s': gate_s, 'up_s': up_s, 'down_s': down_s}
    _L1_ffn_in = _L1_ffn_setup()
    _d = {'L0_attn_x': _L0_attn_in['x'], 'L0_attn_W_K': _L0_attn_in['W_K'], 'L0_attn_W_Q': _L0_attn_in['W_Q'], 'L0_attn_W_V': _L0_attn_in['W_V'], 'L0_attn_W_O': _L0_attn_in['W_O'], 'L0_ffn_weight': _L0_ffn_in['weight'], 'L0_ffn_bias': _L0_ffn_in['bias'], 'L1_attn_in_proj_w': _L1_attn_in['in_proj_w'], 'L1_attn_conv_w': _L1_attn_in['conv_w'], 'L1_attn_conv_b': _L1_attn_in['conv_b'], 'L1_attn_dt_bias': _L1_attn_in['dt_bias'], 'L1_attn_A_log': _L1_attn_in['A_log'], 'L1_attn_D_param': _L1_attn_in['D_param'], 'L1_attn_norm_w': _L1_attn_in['norm_w'], 'L1_attn_out_proj_w': _L1_attn_in['out_proj_w'], 'L1_ffn_gate_w': _L1_ffn_in['gate_w'], 'L1_ffn_up_w': _L1_ffn_in['up_w'], 'L1_ffn_down_w': _L1_ffn_in['down_w'], 'L1_ffn_gate_s': _L1_ffn_in['gate_s'], 'L1_ffn_up_s': _L1_ffn_in['up_s'], 'L1_ffn_down_s': _L1_ffn_in['down_s']}
    _x0 = _d['L0_attn_x']
    _d['L0_attn_x'] = jax.random.normal(jax.random.fold_in(jax.random.key(seed), 1), (4, 512, 256), dtype=_x0.dtype)
    del _x0
    return _d

def reference(L0_attn_x, L0_attn_W_K, L0_attn_W_Q, L0_attn_W_V, L0_attn_W_O, L0_ffn_weight, L0_ffn_bias, L1_attn_in_proj_w, L1_attn_conv_w, L1_attn_conv_b, L1_attn_dt_bias, L1_attn_A_log, L1_attn_D_param, L1_attn_norm_w, L1_attn_out_proj_w, L1_ffn_gate_w, L1_ffn_up_w, L1_ffn_down_w, L1_ffn_gate_s, L1_ffn_up_s, L1_ffn_down_s):

    def _L0_attn_ref(x, W_K, W_Q, W_V, W_O):
        import jax, jax.numpy as jnp
        import numpy as np
        b, pos, d_model = x.shape
        d_head = W_K.shape[1]
        k = jnp.einsum('ihd,bpd->biph', W_K, x)
        q = jnp.einsum('ihd,bpd->biph', W_Q, x)
        v = jnp.einsum('ihd,bpd->biph', W_V, x)
        scores = jnp.einsum('biph,biqh->biqp', k, q)
        mask = jnp.tril(jnp.ones((pos, pos), dtype=x.dtype))
        masked = scores * mask - jnp.float32(10000000000.0) * (1.0 - mask)
        attn = jax.nn.softmax(masked / jnp.sqrt(jnp.float32(d_head)), axis=-1)
        z = jnp.einsum('biqp,biph->biqh', attn, v)
        z_flat = jnp.transpose(z, (0, 2, 1, 3)).reshape(b, pos, -1)
        out = jnp.einsum('df,bqf->bqd', W_O, z_flat)
        return out

    def _L0_ffn_ref(x, weight, bias):
        import jax, jax.numpy as jnp
        import numpy as np

        def binarize_weight(w):
            alpha = jnp.mean(jnp.abs(w), axis=tuple(range(1, w.ndim)), keepdims=True)
            bw = jnp.where(w >= 0, 1.0, -1.0) * alpha
            return jax.lax.stop_gradient(bw - w) + w
        bw = binarize_weight(weight)
        return jnp.einsum('bsi,oi->bso', x, bw) + bias

    def _L1_attn_ref(hidden_states, in_proj_w, conv_w, conv_b, dt_bias, A_log, D_param, norm_w, out_proj_w):
        import jax, jax.numpy as jnp
        import numpy as np
        from jax import lax
        H, P, N, G, K, CHUNK = (64, 64, 128, 1, 4, 32)
        D_MODEL = 256
        D_INNER = H * P
        CONV_DIM = D_INNER + 2 * G * N
        EPS = 1e-05

        def _mamba2_forward(hidden_states, in_proj_w, conv_w, conv_b, dt_bias, A_log, D_param, norm_w, out_proj_w):
            b, l, _ = hidden_states.shape
            c = l // CHUNK
            proj = hidden_states @ in_proj_w
            gate = proj[..., :D_INNER]
            hbc = proj[..., D_INNER:D_INNER + CONV_DIM]
            dt = proj[..., D_INNER + CONV_DIM:]
            xt = hbc.transpose(0, 2, 1)
            y = lax.conv_general_dilated(xt, conv_w[:, None, :], window_strides=(1,), padding=[(K - 1, 0)], feature_group_count=CONV_DIM, dimension_numbers=('NCH', 'OIH', 'NCH'))
            hbc = jax.nn.silu(y + conv_b[None, :, None]).transpose(0, 2, 1)
            per_g = D_INNER // G
            hg = hbc.reshape(b, l, G, per_g + 2 * N)
            x = hg[..., :per_g].reshape(b, l, H, P)
            Bm = hg[..., per_g:per_g + N]
            Cm = hg[..., per_g + N:]
            hpg = H // G
            Bh = jnp.repeat(Bm, hpg, axis=2)
            Ch = jnp.repeat(Cm, hpg, axis=2)
            dt = jax.nn.softplus(dt + dt_bias)
            A = -jnp.exp(A_log)
            x_c = x.reshape(b, c, CHUNK, H, P)
            B_c = Bh.reshape(b, c, CHUNK, H, N)
            C_c = Ch.reshape(b, c, CHUNK, H, N)
            dt_c = dt.reshape(b, c, CHUNK, H)
            dA = dt_c * A[None, None, None, :]
            cum = jnp.cumsum(dA, axis=2)
            diff = cum[:, :, :, None, :] - cum[:, :, None, :, :]
            i = jnp.arange(CHUNK)
            mask = i[:, None] >= i[None, :]
            decay = jnp.exp(jnp.where(mask[None, None, :, :, None], diff, -jnp.inf))
            scores = jnp.einsum('bcihn,bcjhn->bcijh', C_c, B_c) * decay * dt_c[:, :, None, :, :]
            Y_diag = jnp.einsum('bcijh,bcjhp->bcihp', scores, x_c)
            decay_states = jnp.exp(cum[:, :, -1:, :] - cum)
            states = jnp.einsum('bclh,bclhn,bclhp->bchpn', decay_states * dt_c, B_c, x_c)
            chunk_decay = jnp.exp(cum[:, :, -1, :])

            def step(prev, inp):
                st, cd = inp
                new = cd[:, :, None, None] * prev + st
                return (new, prev)
            init = jnp.zeros((b, H, P, N), hidden_states.dtype)
            _, prev_states = lax.scan(step, init, (jnp.moveaxis(states, 1, 0), jnp.moveaxis(chunk_decay, 1, 0)))
            prev_states = jnp.moveaxis(prev_states, 0, 1)
            state_decay_out = jnp.exp(cum)
            Y_off = jnp.einsum('bclhn,bchpn,bclh->bclhp', C_c, prev_states, state_decay_out)
            yh = (Y_diag + Y_off).reshape(b, l, H, P) + D_param[None, None, :, None] * x
            yr = yh.reshape(b, l, D_INNER)
            hidden = yr * jax.nn.silu(gate)
            var = jnp.mean(hidden * hidden, axis=-1, keepdims=True)
            hidden = hidden * lax.rsqrt(var + EPS) * norm_w
            return hidden @ out_proj_w
        return _mamba2_forward(hidden_states, in_proj_w, conv_w, conv_b, dt_bias, A_log, D_param, norm_w, out_proj_w)

    def _L1_ffn_ref(x, gate_w, up_w, down_w, gate_s, up_s, down_s):
        import jax, jax.numpy as jnp
        import numpy as np
        HIDDEN = 256
        INTER = 704
        B, S = (2, 256)

        def _ternary(key, shape):
            return jax.random.randint(key, shape, -1, 2).astype(jnp.float32)
        b, s, h = x.shape
        xf = x.reshape(b * s, h)
        g = jnp.einsum('th,ih->ti', xf, gate_w) * gate_s
        u = jnp.einsum('th,ih->ti', xf, up_w) * up_s
        hdn = jax.nn.silu(g) * u
        out = jnp.einsum('ti,hi->th', hdn, down_w) * down_s
        return out.reshape(b, s, -1)
    x = L0_attn_x
    xn = _layernorm(x, axis=-1)
    x = x + _L0_attn_ref(xn, L0_attn_W_K, L0_attn_W_Q, L0_attn_W_V, L0_attn_W_O) + _L0_ffn_ref(xn, L0_ffn_weight, L0_ffn_bias)
    xn = _layernorm(x, axis=-1)
    x = x + _L1_attn_ref(xn, L1_attn_in_proj_w, L1_attn_conv_w, L1_attn_conv_b, L1_attn_dt_bias, L1_attn_A_log, L1_attn_D_param, L1_attn_norm_w, L1_attn_out_proj_w) + _L1_ffn_ref(xn, L1_ffn_gate_w, L1_ffn_up_w, L1_ffn_down_w, L1_ffn_gate_s, L1_ffn_up_s, L1_ffn_down_s)
    return x

_drawn_inputs = setup_inputs


def setup_inputs(seed=0):
    import zlib

    import numpy as np

    out = dict(_drawn_inputs(seed))
    spreads = {'L1_attn_conv_b': (0.0, 0.1),
     'L1_attn_dt_bias': (1.0, 0.2),
     'L1_attn_D_param': (1.0, 0.2),
     'L1_attn_norm_w': (1.0, 0.2)}
    factors = {'L0_ffn_bias': 5.161}
    for name, (base, spread) in spreads.items():
        noise = np.random.default_rng([zlib.crc32(name.encode()), seed]).standard_normal(out[name].shape)
        drawn = base * np.exp(spread * noise) if base else spread * noise
        out[name] = jnp.asarray(drawn.astype(out[name].dtype))
    for name, factor in factors.items():
        out[name] = (out[name] * factor).astype(out[name].dtype)
    return out
```

```python
from contextlib import ExitStack

import concourse.bass as bass
from concourse import mybir

F32 = mybir.dt.float32
BF16 = mybir.dt.bfloat16
ALU = mybir.AluOpType
ACT = mybir.ActivationFunctionType
AX_X = mybir.AxisListType.X

P = 128
EPS = 1e-5
TAPS = 4


def two_layers(nc, x, wqkv, wo_t, w0, b0, w_pair, w_out, w_bc, w_dt, conv_par, dt_bias, a_log,
               d_col, norm_col, gate_t, up_t, down_t, gate_s, up_s, down_s, out):
    NB, S, D = x.shape
    NH = wqkv.shape[0]
    NT = S // P
    KT = D // P
    NPAIR = w_pair.shape[0]
    MH = dt_bias.shape[0]
    HD = P // 2
    F = gate_t.shape[2]
    FT = -(-F // P)
    FR = F - (FT - 1) * P
    SCALE = float(P) ** -0.5
    W = NT * P
    assert W == 512 and D == 256 and NH % 2 == 0 and NPAIR % 2 == 0 and NT == 4

    P_AT = {3: 0, 2: 512, 0: 896, 1: 1024}
    PT_AT = {0: 0, 1: 512, 3: 896, 2: 1024}
    NP = 1280
    FEEDS = [(a, c) for a in range(NT) for c in range(a + 1, NT)]

    with ExitStack() as ctx:
        def sb(name, shape, dt=F32):
            return ctx.enter_context(nc.sbuf_tensor(name, shape, dt))

        def sem(name):
            return ctx.enter_context(nc.semaphore(name))

        bank = [ctx.enter_context(nc.psum_tensor(f"bank{i}", [P, 512], F32)) for i in range(8)]

        ident = sb("ident", [P, P])
        ident_bf = sb("ident_bf", [P, P], BF16)
        causal_bf = sb("causal_bf", [P, P], BF16)
        upto = sb("upto", [P, P])
        after = sb("after", [P, P])
        ones = sb("ones", [P, P])
        minus_half = sb("minus_half", [P, NT])
        wo_sb = sb("wo_sb", [P, NH, D])
        w0_sb = sb("w0_sb", [P, KT, D])
        w0_abs = sb("w0_abs", [P, KT])
        w0_sign = sb("w0_sign", [P, KT, D])
        w0_t = sb("w0_t", [P, KT, D])
        b0_bc = sb("b0_bc", [P, D])
        wout_sb = sb("wout_sb", [P, NPAIR, D])
        wbc_sb = sb("wbc_sb", [P, KT, 2 * P])
        wdt_sb = sb("wdt_sb", [P, KT, MH])
        conv_sb = sb("conv_sb", [P, NPAIR + 2, TAPS + 1])
        dtb_bc = sb("dtb_bc", [P, MH])
        exp_a = sb("exp_a", [P, MH])
        d_sb = sb("d_sb", [P, NPAIR])
        norm_sb = sb("norm_sb", [P, NPAIR])
        gw_sb = sb("gw_sb", [P, KT, F])
        uw_sb = sb("uw_sb", [P, KT, F])
        dw_sb = sb("dw_sb", [P, FT, D])
        gs_sb = sb("gs_sb", [P, FT])
        us_sb = sb("us_sb", [P, FT])
        ds_bc = sb("ds_bc", [P, D])

        x_sb = sb("x_sb", [P, NT, D])
        xn = sb("xn", [P, NT, D])
        xn_t = sb("xn_t", [P, KT, W])
        spacer = sb("spacer", [P, 1])
        stats = sb("stats", [P, NT, 6])
        meanvar = sb("meanvar", [P, NT, 2])
        var_eps = sb("var_eps", [P, NT])
        rstd = sb("rstd", [P, NT])
        wh = sb("wh", [P, 2, 3, KT, P])
        neg_max = sb("neg_max", [P, 2, NT])
        bias = sb("bias", [P, 2, NT])
        total = sb("total", [P, 2, NT])
        inv_total = sb("inv_total", [P, 2, NT])
        shared = sb("shared", [P, NH * W])
        z_t = shared[:].rearrange("p (h w) -> p h w", h=NH)
        n_mix, n_xw = 4 * NT * P, len(FEEDS) * P
        mix = shared[:, 0:n_mix].rearrange("p (a h w) -> p a h w", a=2, h=2)
        steps = shared[:, n_mix:2 * n_mix].rearrange("p (a h c i) -> p a h c i", a=2, h=2, c=NT)
        x_w = shared[:, 2 * n_mix:2 * n_mix + n_xw].rearrange("p (f q) -> p f q", f=len(FEEDS))
        f_hid = shared[:, 2 * n_mix + n_xw:2 * n_mix + n_xw + FT * W].rearrange("p (f w) -> p f w", f=FT)
        x2 = sb("x2", [P, NT, D])

        place = sb("place", [P, 6 * W + 3 * NP])
        q_t = place[:, 0:2 * W].rearrange("p (a w) -> p a w", a=2)
        k_t = place[:, 2 * W:4 * W].rearrange("p (a w) -> p a w", a=2)
        v_sb = place[:, 4 * W:6 * W].rearrange("p (a t e) -> p a t e", a=2, t=NT)
        prob = place[:, 6 * W:6 * W + 2 * NP].rearrange("p (a n) -> p a n", a=2)
        prob_t = place[:, 6 * W + 2 * NP:6 * W + 3 * NP]
        xs = place[:, 0:2 * W].rearrange("p (a w) -> p a w", a=2)
        gate = place[:, 2 * W:4 * W].rearrange("p (a w) -> p a w", a=2)
        x_dt = place[:, 4 * W:6 * W].rearrange("p (a t q) -> p a t q", a=2, t=NT)
        hid = place[:, 6 * W:8 * W].rearrange("p (a w) -> p a w", a=2)
        grow, y_x, y_all, square = (place[:, (8 + i) * W:(9 + i) * W] for i in range(4))

        wp = sb("wp", [P, 2, 2, KT, P])
        conv_acc = sb("conv_acc", [P, W])
        conv_th = sb("conv_th", [P, W])
        gate_th = sb("gate_th", [P, W])
        b_t = sb("b_t", [P, W])
        c_t = sb("c_t", [P, W])
        b_sb = sb("b_sb", [P, NT, P])
        cb = sb("cb", [P, NT, P])
        dt_raw = sb("dt_raw", [P, NT, MH])
        dt_tmp = sb("dt_tmp", [P, NT, MH])
        dt_sb = sb("dt_sb", [P, NT, MH])
        da = sb("da", [P, NT, MH])
        dec = sb("dec", [P, len(FEEDS), MH])
        state = sb("state", [P, NT - 1, P])
        y_in = sb("y_in", [P, W])
        sumsq = sb("sumsq", [P, W])
        ms_eps = sb("ms_eps", [P, NT])
        rms = sb("rms", [P, NT])
        f_half = sb("f_half", [P, 2, W])
        f_th = sb("f_th", [P, 2, W])
        f_silu = sb("f_silu", [P, W])
        res = xn
        y_out = sb("y_out", [P, NT, D])

        s_loads = sem("loads")
        s_consts = sem("consts")
        s_x_in = sem("x_in")
        s_wh_in0 = sem("wh_in0")
        s_wh_in1 = sem("wh_in1")
        s_wp_in0 = sem("wp_in0")
        s_wp_in1 = sem("wp_in1")
        s_stored = sem("stored")
        s_xnt_half = sem("xnt_half")
        s_setup_sign = sem("setup_sign")
        s_setup_act = sem("setup_act")
        s_setup_dve = sem("setup_dve")
        s_setup_pe = sem("setup_pe")
        s_ln_stats = sem("ln_stats")
        s_ln_var = sem("ln_var")
        s_ln_rstd = sem("ln_rstd")
        s_ln_xn = sem("ln_xn")
        s_ln_turned = sem("ln_turned")
        s_ln_xnt = sem("ln_xnt")
        s_x_bias = sem("x_bias")
        s_q_done = sem("q_done")
        s_k_done = sem("k_done")
        s_v_done = sem("v_done")
        s_q_ev = sem("q_ev")
        s_k_ev = sem("k_ev")
        s_v_ev = sem("v_ev")
        s_scores_done = sem("scores_done")
        s_max_done = sem("max_done")
        s_bias_done = sem("bias_done")
        s_exp_done = sem("exp_done")
        s_inv_done = sem("inv_done")
        s_norm_done = sem("norm_done")
        s_turned_a = sem("turned_a")
        s_turned_b = sem("turned_b")
        s_turned_c = sem("turned_c")
        s_pt_a = sem("pt_a")
        s_pt_b = sem("pt_b")
        s_pt_c = sem("pt_c")
        s_z_done = sem("z_done")
        s_z_ev = sem("z_ev")
        s_attn_out = sem("attn_out")
        s_x2_done = sem("x2_done")
        s_dt_done = sem("dt_done")
        s_dt_biased = sem("dt_biased")
        s_dt_absed = sem("dt_absed")
        s_dt_exp = sem("dt_exp")
        s_dt_ln = sem("dt_ln")
        s_dt_ready = sem("dt_ready")
        s_da_ready = sem("da_ready")
        s_bc_done = sem("bc_done")
        s_tap0 = sem("tap0")
        s_tap1 = sem("tap1")
        s_tap2 = sem("tap2")
        s_taps_done = sem("taps_done")
        s_conv_tanh = sem("conv_tanh")
        s_conv_silu = sem("conv_silu")
        s_b_turned = sem("b_turned")
        s_b_ev = sem("b_ev")
        s_cb_done = sem("cb_done")
        s_cb_ev = sem("cb_ev")
        s_dec_done = sem("dec_done")
        s_dec_ready = sem("dec_ready")
        s_gate_done = sem("gate_done")
        s_xc_done = sem("xc_done")
        s_gate_tanh = sem("gate_tanh")
        s_gate_ready = sem("gate_ready")
        s_steps_ready = sem("steps_ready")
        s_seg0_done = sem("seg0_done")
        s_seg1_done = sem("seg1_done")
        s_mix_exp0 = sem("mix_exp0")
        s_mix_exp1 = sem("mix_exp1")
        s_mix_ready = sem("mix_ready")
        s_x_turned = sem("x_turned")
        s_xdt_ready = sem("xdt_ready")
        s_xw_ready = sem("xw_ready")
        s_state_done = sem("state_done")
        s_state_ev = sem("state_ev")
        s_grow_done = sem("grow_done")
        s_grow_ev = sem("grow_ev")
        s_off_done = sem("off_done")
        s_off_scaled = sem("off_scaled")
        s_skip_done = sem("skip_done")
        s_diag_done = sem("diag_done")
        s_y_ready = sem("y_ready")
        s_hid_ready = sem("hid_ready")
        s_squared = sem("squared")
        s_summed = sem("summed")
        s_projected = sem("projected")
        s_ss_done = sem("ss_done")
        s_ms_ready = sem("ms_ready")
        s_rms_ready = sem("rms_ready")
        s_ffn_gate = sem("ffn_gate")
        s_ffn_up = sem("ffn_up")
        s_ffn_scaled = sem("ffn_scaled")
        s_ffn_tanh = sem("ffn_tanh")
        s_ffn_silu = sem("ffn_silu")
        s_ffn_hid = sem("ffn_hid")
        s_ffn_out = sem("ffn_out")
        s_res_ready = sem("res_ready")
        s_y_done = sem("y_done")
        wh_in, wp_in = (s_wh_in0, s_wh_in1), (s_wp_in0, s_wp_in1)

        PE_CREDITS = ((s_z_done, 1), (s_state_done, 1), (s_off_done, 1), (s_projected, 2), (s_ss_done, 1),
                      (s_v_done, 2), (s_xc_done, 2), (s_grow_done, 2))
        ACT_CREDITS = ((s_v_ev, 1), (s_exp_done, 1), (s_pt_a, 1), (s_state_ev, 1), (s_grow_ev, 1))
        DVE_CREDITS = ((s_k_ev, 1), (s_pt_b, 1), (s_z_ev, 1), (s_x2_done, 1), (s_gate_ready, 1), (s_conv_silu, 1),
                       (s_off_scaled, 1), (s_y_ready, 1), (s_hid_ready, 1), (s_ffn_hid, 1), (s_y_done, 1))
        POOL_CREDITS = ((s_squared, 2), (s_stored, 16))

        block = ctx.enter_context(nc.Block())
        N_LOADS = 18
        NCONST = 9

        @block.sync
        def _(sp):
            resident = [
                (wo_sb[:], wo_t), (w0_sb[:], w0), (b0_bc[:], b0.unsqueeze(0).to_broadcast([P, D])),
                (wout_sb[:], w_out), (wbc_sb[:], w_bc), (wdt_sb[:], w_dt), (conv_sb[:], conv_par),
                (dtb_bc[:], dt_bias.unsqueeze(0).to_broadcast([P, MH])),
                (exp_a[:], a_log.unsqueeze(0).to_broadcast([P, MH])),
                (d_sb[:], d_col), (norm_sb[:], norm_col), (gw_sb[:], gate_t), (uw_sb[:], up_t),
                (dw_sb[:, 0:FT - 1, :], down_t[0:(FT - 1) * P, :].rearrange("(f p) d -> p f d", p=P)),
                (dw_sb[0:FR, FT - 1, :], down_t[(FT - 1) * P:F, :]),
                (gs_sb[:], gate_s), (us_sb[:], up_s),
                (ds_bc[:], down_s.unsqueeze(0).to_broadcast([P, D])),
            ]
            assert len(resident) == N_LOADS
            for dst, src in resident:
                sp.dma_start(dst, src).then_inc(s_loads, 16)
            with sp.Fori(0, NB) as b:
                sp.wait_ge(s_x2_done, b + 1)
                sp.dma_start(x_sb[:], x[bass.ds(b, 1), :, :].rearrange("b (t p) d -> p (b t) d", p=P)).then_inc(s_x_in, 16)
                with sp.Fori(0, NH // 2) as i:
                    for par in range(2):
                        n = b * NH + i * 2 + par
                        sp.wait_ge(s_v_done, n + 1)
                        sp.dma_start(wh[:, par, :, :, :], wqkv[bass.ds(i * 2 + par, 1), :, :, :, :].rearrange("h p m k d -> p (h m) k d")).then_inc(wh_in[par], 16)
                with sp.Fori(0, NPAIR // 2) as i:
                    for par in range(2):
                        n = b * NPAIR + i * 2 + par
                        sp.wait_ge(s_xc_done, n + 1)
                        sp.dma_start(wp[:, par, :, :, :], w_pair[bass.ds(i * 2 + par, 1), :, :, :, :].rearrange("h p m k d -> p (h m) k d")).then_inc(wp_in[par], 16)
                sp.wait_ge(s_y_done, b + 2)
                sp.dma_start(out[bass.ds(b, 1), :, :].rearrange("b (t p) d -> p (b t) d", p=P), y_out[:]).then_inc(s_stored, 16)
            sp.wait_ge(s_stored, 16 * NB + 16)

        @block.gpsimd
        def _(pool):
            for free, n in POOL_CREDITS:
                pool.sem_inc(free, n)
            pool.memset(ident[:], 0.0).then_inc(s_consts, 1)
            pool.memset(upto[:], 1.0).then_inc(s_consts, 1)
            pool.memset(after[:], 1.0).then_inc(s_consts, 1)
            pool.memset(ones[:], 1.0).then_inc(s_consts, 1)
            pool.memset(causal_bf[:], 0.0).then_inc(s_consts, 1)
            pool.memset(minus_half[:], -0.5).then_inc(s_consts, 1)
            pool.memset(ident_bf[:], 0.0).then_inc(s_consts, 1)
            pool.memset(y_in[:, 0:P], 0.0).then_inc(s_consts, 1)
            pool.wait_ge(s_consts, 8)
            for t in (ident, ident_bf):
                pool.affine_select(out=t[:], in_=t[:], compare_op=ALU.not_equal, fill=1.0, base=0,
                                   pattern=[[-1, P]], channel_multiplier=1)
            pool.affine_select(out=upto[:], in_=upto[:], compare_op=ALU.is_ge, fill=0.0, base=0,
                               pattern=[[1, P]], channel_multiplier=-1)
            pool.affine_select(out=after[:], in_=after[:], compare_op=ALU.is_ge, fill=0.0, base=-1,
                               pattern=[[-1, P]], channel_multiplier=1)
            pool.affine_select(out=causal_bf[:], in_=causal_bf[:], compare_op=ALU.is_ge, fill=-1e10, base=0,
                               pattern=[[-1, P]], channel_multiplier=1).then_inc(s_consts, 1)

            def rstd_of(k):
                pool.wait_ge(s_ln_var, k + 1)
                pool.tensor_tensor(rstd[:], var_eps[:], minus_half[:], ALU.pow).then_inc(s_ln_rstd, 1)

            def build_steps(b, n, par):
                N = b * NPAIR + n
                pool.wait_ge(s_grow_done, N + 1)
                for h in range(2):
                    col = da[:, :, bass.ds(n * 2 + h, 1)].to_broadcast([P, NT, P])
                    ins = pool.tensor_tensor(steps[:, par, h, :, :], upto[:].unsqueeze(1).to_broadcast([P, NT, P]), col, ALU.mult)
                ins.then_inc(s_steps_ready, 1)

            def weigh_x(b, n, par):
                N = b * NPAIR + n
                pool.wait_ge(s_xdt_ready, N + 1)
                pool.wait_ge(s_state_done, N + 1)
                at = 0
                for a in range(NT - 1):
                    k = NT - 1 - a
                    o = x_w[:, at:at + k, :].rearrange("p k (h q) -> p k h q", h=2)
                    i0 = x_dt[:, par, a, :].rearrange("p (h q) -> p h q", h=2).unsqueeze(1).to_broadcast([P, k, 2, HD])
                    i1 = dec[:, at:at + k, bass.ds(n * 2, 2)].unsqueeze(3).to_broadcast([P, k, 2, HD])
                    ins = pool.tensor_tensor(o, i0, i1, ALU.mult)
                    at += k
                ins.then_inc(s_xw_ready, 1)

            def add_squares(b, n, par):
                N = b * NPAIR + n
                pool.wait_ge(s_hid_ready, N + 2)
                pool.wait_ge(s_summed, N + b + 1)
                pool.tensor_tensor(square[:], hid[:, par, :], hid[:, par, :], ALU.mult).then_inc(s_squared, 1)
                pool.wait_ge(s_squared, N + 3)
                pool.tensor_tensor(sumsq[:], sumsq[:], square[:], ALU.add).then_inc(s_summed, 1)

            with pool.Fori(0, NB) as b:
                rstd_of(b * 2)
                pool.wait_ge(s_ln_xn, b * 2 + 1)
                pool.wait_ge(s_loads, 16 * N_LOADS)
                pool.tensor_tensor(x_sb[:], x_sb[:], b0_bc[:].unsqueeze(1).to_broadcast([P, NT, D]), ALU.add).then_inc(s_x_bias, 1)
                pool.wait_ge(s_ss_done, b + 1)
                rstd_of(b * 2 + 1)
                pool.memset(sumsq[:], 0.0).then_inc(s_summed, 1)
                pool.wait_ge(s_da_ready, b + 1)
                build_steps(b, 0, 0)
                pool.wait_ge(s_consts, NCONST)
                pool.wait_ge(s_dec_ready, b + 1)

                def pair(n, par, more):
                    if more:
                        build_steps(b, n + 1, 1 - par)
                    weigh_x(b, n, par)
                    add_squares(b, n, par)

                with pool.Fori(0, NPAIR // 2 - 1) as i:
                    for par in range(2):
                        pair(i * 2 + par, par, True)
                pair(NPAIR - 2, 0, True)
                pair(NPAIR - 1, 1, False)
                pool.wait_ge(s_ms_ready, b + 1)
                pool.tensor_tensor(rms[:], ms_eps[:], minus_half[:], ALU.pow).then_inc(s_rms_ready, 1)

        @block.tensor
        def _(pe):
            for free, n in PE_CREDITS:
                pe.sem_inc(free, n)
            mm = pe.matmul
            pe.wait_ge(s_consts, NCONST)
            pe.wait_ge(s_setup_dve, 3)
            for o in range(KT):
                for k in range(KT):
                    ins = pe.transpose(bank[0][:, k * D + o * P:k * D + (o + 1) * P], w0_sb[:, o, k * P:(k + 1) * P], ident[:])
            ins.then_inc(s_setup_pe, 1)
            pe.wait_ge(s_setup_dve, 4)

            def turn_norm(k):
                pe.wait_ge(s_ln_xn, k + 1)
                for d in range(KT):
                    for t in range(NT):
                        ins = pe.transpose(bank[d][:, t * P:(t + 1) * P], xn[:, t, d * P:(d + 1) * P], ident[:])
                ins.then_inc(s_ln_turned, 1)
                pe.wait_ge(s_ln_xnt, k + 1)
                pe.wait_ge(s_xnt_half, k + 1)

            def project_qk(b, h, par):
                N = b * NH + h
                pe.wait_ge(wh_in[par], (N - par + 2) * 8)
                pe.wait_ge(s_v_ev, N + 1)
                for k in range(KT):
                    ins = mm(bank[0][:], lhsT=wh[:, par, 0, k, :], rhs=xn_t[:, k, :], start=(k == 0), stop=(k == KT - 1))
                ins.then_inc(s_q_done, 1)
                pe.wait_ge(s_k_ev, N + 1)
                for k in range(KT):
                    ins = mm(bank[1][:], lhsT=wh[:, par, 1, k, :], rhs=xn_t[:, k, :], start=(k == 0), stop=(k == KT - 1))
                ins.then_inc(s_k_done, 1)

            def project_v(b, h, par):
                N = b * NH + h
                pe.wait_ge(s_q_ev, N + 1)
                for t in range(NT):
                    for k in range(KT):
                        ins = mm(bank[0][:, t * P:(t + 1) * P], lhsT=xn_t[:, k, t * P:(t + 1) * P],
                                 rhs=wh[:, par, 2, k, :], start=(k == 0), stop=(k == KT - 1))
                ins.then_inc(s_v_done, 1)

            def score(b, h, par):
                N = b * NH + h
                pe.wait_ge(s_k_ev, N + 2)
                pe.wait_ge(s_exp_done, N + 1)
                for q, bk, at in ((3, 2, 0), (2, 3, 0), (0, 3, 384), (1, 4, 0)):
                    w = (q + 1) * P
                    mm(bank[bk][:, at:at + w], lhsT=q_t[:, par, q * P:(q + 1) * P], rhs=k_t[:, par, 0:w], start=True, stop=True)
                    mm(bank[bk][:, at + w - P:at + w], lhsT=ident_bf[:], rhs=causal_bf[:], start=False, stop=True,
                       skip_group_check=True).then_inc(s_scores_done, 1)

            def turn_probs(b, h, par):
                N = b * NH + h
                pe.wait_ge(s_norm_done, N + 1)
                pe.wait_ge(s_pt_a, N + 1)
                for q in range(NT):
                    ins = pe.transpose(bank[5][:, q * P:(q + 1) * P], prob[:, par, P_AT[q]:P_AT[q] + P], ident[:])
                ins.then_inc(s_turned_a, 1)
                pe.wait_ge(s_pt_b, N + 1)
                for k, q in ((1, 1), (1, 2), (1, 3), (3, 3)):
                    at = PT_AT[k] - PT_AT[1] + (q - k) * P
                    ins = pe.transpose(bank[6][:, at:at + P], prob[:, par, P_AT[q] + k * P:P_AT[q] + (k + 1) * P], ident[:])
                ins.then_inc(s_turned_b, 1)
                pe.wait_ge(s_z_ev, N + 1)
                for q in (2, 3):
                    ins = pe.transpose(bank[7][:, (q - 2) * P:(q - 1) * P], prob[:, par, P_AT[q] + 2 * P:P_AT[q] + 3 * P], ident[:])
                ins.then_inc(s_turned_c, 1)

            def weigh_values(b, h, par):
                N = b * NH + h
                pe.wait_ge(s_pt_a, N + 2)
                pe.wait_ge(s_pt_b, N + 2)
                pe.wait_ge(s_pt_c, N + 1)
                pe.wait_ge(s_v_ev, N + 2)
                for k in range(NT):
                    ins = mm(bank[7][:, k * P:W], lhsT=v_sb[:, par, k, :], rhs=prob_t[:, PT_AT[k]:PT_AT[k] + W - k * P],
                             start=(k == 0), stop=True, skip_group_check=True)
                ins.then_inc(s_z_done, 1)

            def out_tile(banks, t):
                return bank[banks[t // 2]][:, (t % 2) * D:(t % 2 + 1) * D]

            def attention_out(b):
                pe.wait_ge(s_z_ev, (b + 1) * NH + 1)
                for t in range(NT):
                    for h in range(NH):
                        mm(out_tile((0, 1), t), lhsT=z_t[:, h, t * P:(t + 1) * P], rhs=wo_sb[:, h, :],
                           start=(h == 0), stop=False)
                    for k in range(KT):
                        ins = mm(out_tile((0, 1), t), lhsT=xn_t[:, k, t * P:(t + 1) * P], rhs=w0_t[:, k, :],
                                 start=False, stop=(k == KT - 1))
                ins.then_inc(s_attn_out, 1)

            def mamba_start(b):
                for i in range(2):
                    for k in range(KT):
                        ins = mm(bank[i][:], lhsT=wbc_sb[:, k, i * P:(i + 1) * P], rhs=xn_t[:, k, :], start=(k == 0), stop=(k == KT - 1))
                    ins.then_inc(s_bc_done, 1)
                for t in range(NT):
                    for k in range(KT):
                        ins = mm(bank[2][:, t * MH:(t + 1) * MH], lhsT=xn_t[:, k, t * P:(t + 1) * P], rhs=wdt_sb[:, k, :],
                                 start=(k == 0), stop=(k == KT - 1))
                ins.then_inc(s_dt_done, 1)
                pe.wait_ge(s_da_ready, b + 1)
                for i, (a, c) in enumerate(FEEDS):
                    o = bank[5][:, i * MH:(i + 1) * MH]
                    ins = mm(o, lhsT=after[:], rhs=da[:, a, :], start=True, stop=(c == a + 1))
                    for m in range(a + 1, c):
                        ins = mm(o, lhsT=ones[:], rhs=da[:, m, :], start=False, stop=(m == c - 1))
                ins.then_inc(s_dec_done, 1)
                pe.wait_ge(s_conv_silu, b * (NPAIR + 2) + 3)
                for t in range(NT):
                    ins = pe.transpose(bank[4][:, t * P:(t + 1) * P], b_t[:, t * P:(t + 1) * P], ident[:])
                ins.then_inc(s_b_turned, 1)
                for t in range(NT):
                    ins = mm(bank[3][:, t * P:(t + 1) * P], lhsT=b_t[:, t * P:(t + 1) * P], rhs=c_t[:, t * P:(t + 1) * P],
                             start=True, stop=True)
                ins.then_inc(s_cb_done, 1)

            def project_pair(b, n, par):
                N = b * NPAIR + n
                pe.wait_ge(wp_in[par], (N - par + 2) * 8)
                pe.wait_ge(s_gate_ready, N + 1)
                for k in range(KT):
                    ins = mm(bank[0][:], lhsT=wp[:, par, 0, k, :], rhs=xn_t[:, k, :], start=(k == 0), stop=(k == KT - 1))
                ins.then_inc(s_gate_done, 1)
                pe.wait_ge(s_taps_done, N + b * 2 + 2)
                for k in range(KT):
                    ins = mm(bank[1][:], lhsT=wp[:, par, 1, k, :], rhs=xn_t[:, k, :], start=(k == 0), stop=(k == KT - 1))
                ins.then_inc(s_xc_done, 1)

            def segments(b, n, par):
                N = b * NPAIR + n
                pe.wait_ge(s_steps_ready, N + 1)
                pe.wait_ge(s_grow_ev, N + 1)
                mm(bank[3][:], lhsT=after[:], rhs=steps[:, par, 0, :, :].rearrange("p c i -> p (c i)"), start=True, stop=True).then_inc(s_seg0_done, 1)
                pe.wait_ge(s_off_scaled, N + 1)
                mm(bank[4][:], lhsT=after[:], rhs=steps[:, par, 1, :, :].rearrange("p c i -> p (c i)"), start=True, stop=True).then_inc(s_seg1_done, 1)

            def turn_x(b, n, par):
                N = b * NPAIR + n
                pe.wait_ge(s_conv_silu, N + b * 2 + 4)
                pe.wait_ge(s_state_ev, N + 1)
                for t in range(NT):
                    ins = pe.transpose(bank[2][:, t * P:(t + 1) * P], xs[:, par, t * P:(t + 1) * P], ident[:])
                ins.then_inc(s_x_turned, 1)

            def make_states(b, n, par):
                N = b * NPAIR + n
                pe.wait_ge(s_xw_ready, N + 1)
                for c in range(1, NT):
                    into = [i for i, f in enumerate(FEEDS) if f[1] == c]
                    for i in into:
                        ins = mm(bank[2][:, (c - 1) * P:c * P], lhsT=b_sb[:, FEEDS[i][0], :], rhs=x_w[:, i, :],
                                 start=(i == into[0]), stop=(i == into[-1]))
                ins.then_inc(s_state_done, 1)

            def grown(b, n, par):
                N = b * NPAIR + n
                pe.wait_ge(s_mix_exp0, N + 1)
                for h in range(2):
                    ins = mm(bank[3][h * HD:(h + 1) * HD, 0:W - P], lhsT=ones[:, 0:HD],
                             rhs=steps[:, par, h, 1:NT, :].rearrange("p c i -> p (c i)"), start=True, stop=True)
                ins.then_inc(s_grow_done, 1)

            def off_block(b, n, par):
                N = b * NPAIR + n
                pe.wait_ge(s_mix_exp1, N + 1)
                pe.wait_ge(s_state_ev, N + 2)
                for c in range(1, NT):
                    ins = mm(bank[4][:, (c - 1) * P:c * P], lhsT=state[:, c - 1, :], rhs=c_t[:, c * P:(c + 1) * P], start=True, stop=True)
                ins.then_inc(s_off_done, 1)

            def in_block(b, n, par):
                N = b * NPAIR + n
                pe.wait_ge(s_mix_ready, N + 1)
                pe.wait_ge(s_xdt_ready, N + 1)
                pe.wait_ge(s_y_ready, N + 1)
                for c in range(NT):
                    for h in range(2):
                        ins = mm(bank[5][h * HD:(h + 1) * HD, c * P:(c + 1) * P], lhsT=x_dt[:, par, c, h * HD:(h + 1) * HD],
                                 rhs=mix[:, par, h, c * P:(c + 1) * P], start=True, stop=True)
                ins.then_inc(s_diag_done, 1)

            def project_out(b, n, par, first, last):
                N = b * NPAIR + n
                pe.wait_ge(s_hid_ready, N + 2)
                for t in range(NT):
                    ins = mm(out_tile((6, 7), t), lhsT=hid[:, par, t * P:(t + 1) * P],
                             rhs=wout_sb[:, n if isinstance(n, int) else bass.ds(n, 1), :],
                             start=(first and t % 2 == 0), stop=last, skip_group_check=True)
                ins.then_inc(s_projected, 1)

            def ffn(b):
                for f in range(FT):
                    m = P if f < FT - 1 else FR
                    o = (f % 2) * 2
                    N = b * FT + f
                    if f >= 2:
                        pe.wait_ge(s_ffn_hid, N)
                    for k in range(KT):
                        ins = mm(bank[o][0:m, :], lhsT=gw_sb[:, k, f * P:f * P + m], rhs=xn_t[:, k, :], start=(k == 0), stop=(k == KT - 1))
                    ins.then_inc(s_ffn_gate, 1)
                    for k in range(KT):
                        ins = mm(bank[o + 1][0:m, :], lhsT=uw_sb[:, k, f * P:f * P + m], rhs=xn_t[:, k, :], start=(k == 0), stop=(k == KT - 1))
                    ins.then_inc(s_ffn_up, 1)

            def ffn_down(b):
                pe.wait_ge(s_ffn_hid, (b + 1) * FT + 1)
                for t in range(NT):
                    for f in range(FT):
                        m = P if f < FT - 1 else FR
                        ins = mm(out_tile((4, 5), t), lhsT=f_hid[0:m, f, t * P:(t + 1) * P], rhs=dw_sb[0:m, f, :],
                                 start=(f == 0), stop=(f == FT - 1))
                ins.then_inc(s_ffn_out, 1)

            with pe.Fori(0, NB) as b:
                pe.wait_ge(s_y_done, b + 1)
                turn_norm(b * 2)
                project_qk(b, 0, 0)
                project_v(b, 0, 0)
                score(b, 0, 0)

                def head(h, par, more):
                    if more:
                        project_qk(b, h + 1, 1 - par)
                    turn_probs(b, h, par)
                    if more:
                        project_v(b, h + 1, 1 - par)
                        score(b, h + 1, 1 - par)
                    weigh_values(b, h, par)

                with pe.Fori(0, NH // 2 - 1) as i:
                    for par in range(2):
                        head(i * 2 + par, par, True)
                head(NH - 2, 0, True)
                head(NH - 1, 1, False)
                attention_out(b)

                turn_norm(b * 2 + 1)
                mamba_start(b)
                pe.wait_ge(s_cb_ev, b + 1)
                pe.wait_ge(s_b_ev, b + 1)
                pe.wait_ge(s_dec_ready, b + 1)
                project_pair(b, 0, 0)

                def pair(n, par, more, first=False, last=False):
                    segments(b, n, par)
                    turn_x(b, n, par)
                    if more:
                        project_pair(b, n + 1, 1 - par)
                    make_states(b, n, par)
                    grown(b, n, par)
                    off_block(b, n, par)
                    in_block(b, n, par)
                    if not first:
                        project_out(b, n - 1, 1 - par, False, False)

                def first_out():
                    project_out(b, 0, 0, True, False)

                pair(0, 0, True, first=True)
                segments(b, 1, 1)
                turn_x(b, 1, 1)
                project_pair(b, 2, 0)
                make_states(b, 1, 1)
                grown(b, 1, 1)
                off_block(b, 1, 1)
                in_block(b, 1, 1)
                first_out()
                with pe.Fori(1, NPAIR // 2 - 1) as i:
                    for par in range(2):
                        pair(i * 2 + par, par, True)
                pair(NPAIR - 2, 0, True)
                pair(NPAIR - 1, 1, False)
                project_out(b, NPAIR - 1, 1, False, True)
                pe.wait_ge(s_summed, (b + 1) * (NPAIR + 1))
                for t in range(NT):
                    ins = mm(bank[4][:, t:t + 1], lhsT=sumsq[:, t * P:(t + 1) * P], rhs=ones[:, 0:1], start=True, stop=True)
                ins.then_inc(s_ss_done, 1)
                ffn(b)
                pe.wait_ge(s_ms_ready, b + 1)
                ffn_down(b)

        @block.scalar
        def _(act):
            for free, n in ACT_CREDITS:
                act.sem_inc(free, n)
            A = act.activation
            act.wait_ge(s_loads, 16 * N_LOADS)
            A(exp_a[:], exp_a[:], ACT.Exp).then_inc(s_setup_act, 1)

            def copy_out(dst, src, done):
                A(dst, src, ACT.Copy).then_inc(done, 1)

            def q_out(b, h, par):
                act.wait_ge(s_q_done, b * NH + h + 1)
                copy_out(q_t[:, par, :], bank[0][:], s_q_ev)

            def v_out(b, h, par):
                act.wait_ge(s_v_done, b * NH + h + 3)
                copy_out(v_sb[:, par, :, :].rearrange("p t d -> p (t d)"), bank[0][:], s_v_ev)

            def exps(b, h, par):
                N = b * NH + h
                act.wait_ge(s_bias_done, N + 1)
                for q, bk, at in ((3, 2, 0), (2, 3, 0), (0, 3, 384), (1, 4, 0)):
                    w = (q + 1) * P
                    ins = A(prob[:, par, P_AT[q]:P_AT[q] + w], bank[bk][:, at:at + w], ACT.Exp,
                            bias=bias[:, par, q:q + 1], scale=SCALE, accum_out=total[:, par, q:q + 1])
                ins.then_inc(s_exp_done, 1)

            def probs_out(b, h, par):
                N = b * NH + h
                act.wait_ge(s_turned_a, N + 1)
                act.wait_ge(s_z_done, N + 1)
                copy_out(prob_t[:, 0:512], bank[5][:], s_pt_a)
                act.wait_ge(s_turned_c, N + 1)
                copy_out(prob_t[:, 1024:NP], bank[7][:, 0:256], s_pt_c)

            def gate_tanh(b, n, par):
                N = b * NPAIR + n
                act.wait_ge(s_gate_done, N + 1)
                act.wait_ge(s_gate_ready, N + 1)
                A(gate_th[:], bank[0][:], ACT.Tanh, scale=0.5).then_inc(s_gate_tanh, 1)

            def tap_now(k, ch, src):
                act.wait_ge(s_conv_silu, k + 1)
                A(conv_acc[:], src, ACT.Identity, bias=conv_sb[:, ch, TAPS:TAPS + 1],
                  scale=conv_sb[:, ch, TAPS - 1:TAPS]).then_inc(s_tap0, 1)

            def conv_tanh(k):
                act.wait_ge(s_taps_done, k + 1)
                A(conv_th[:], conv_acc[:], ACT.Tanh).then_inc(s_conv_tanh, 1)

            def pair_conv_start(b, n):
                act.wait_ge(s_xc_done, b * NPAIR + n + 3)
                tap_now(b * (NPAIR + 2) + 2 + n, n if isinstance(n, int) else bass.ds(n, 1), bank[1][:])

            act.wait_ge(s_setup_dve, 5)

            with act.Fori(0, NB) as b:
                act.wait_ge(s_ln_turned, b * 2 + 1)
                copy_out(xn_t[:, 0, :], bank[0][:], s_xnt_half)
                q_out(b, 0, 0)
                v_out(b, 0, 0)
                exps(b, 0, 0)

                def head(h, par, more):
                    if more:
                        q_out(b, h + 1, 1 - par)
                    probs_out(b, h, par)
                    if more:
                        v_out(b, h + 1, 1 - par)
                        exps(b, h + 1, 1 - par)

                with act.Fori(0, NH // 2 - 1) as i:
                    for par in range(2):
                        head(i * 2 + par, par, True)
                head(NH - 2, 0, True)
                head(NH - 1, 1, False)

                act.wait_ge(s_ln_turned, b * 2 + 2)
                copy_out(xn_t[:, 0, :], bank[0][:], s_xnt_half)
                K = b * (NPAIR + 2)
                act.wait_ge(s_bc_done, b * 2 + 1)
                tap_now(K, NPAIR, bank[0][:])
                conv_tanh(K)
                act.wait_ge(s_bc_done, b * 2 + 2)
                tap_now(K + 1, NPAIR + 1, bank[1][:])
                conv_tanh(K + 1)
                act.wait_ge(s_dt_absed, b + 1)
                A(dt_sb[:], dt_tmp[:], ACT.Exp, scale=-1.0).then_inc(s_dt_exp, 1)
                act.wait_ge(s_dt_exp, b + 1)
                A(dt_tmp[:], dt_sb[:], ACT.Ln, bias=1.0).then_inc(s_dt_ln, 1)
                act.wait_ge(s_dec_done, b + 1)
                A(dec[:].rearrange("p f h -> p (f h)"), bank[5][:, 0:len(FEEDS) * MH], ACT.Exp).then_inc(s_dec_ready, 1)
                act.wait_ge(s_b_turned, b + 1)
                copy_out(b_sb[:].rearrange("p t n -> p (t n)"), bank[4][:], s_b_ev)
                gate_tanh(b, 0, 0)
                pair_conv_start(b, 0)
                conv_tanh(K + 2)

                def pair(n, par, more):
                    N = b * NPAIR + n
                    act.wait_ge(s_seg0_done, N + 1)
                    A(mix[:, par, 0, :], bank[3][:], ACT.Exp).then_inc(s_mix_exp0, 1)
                    act.wait_ge(s_seg1_done, N + 1)
                    A(mix[:, par, 1, :], bank[4][:], ACT.Exp).then_inc(s_mix_exp1, 1)
                    if more:
                        gate_tanh(b, n + 1, 1 - par)
                        pair_conv_start(b, n + 1)
                    act.wait_ge(s_state_done, N + 2)
                    act.wait_ge(s_off_done, N + 1)
                    copy_out(state[:].rearrange("p c q -> p (c q)"), bank[2][:, 0:W - P], s_state_ev)
                    act.wait_ge(s_grow_done, N + 3)
                    act.wait_ge(s_off_scaled, N + 1)
                    A(grow[:, 0:W - P], bank[3][:, 0:W - P], ACT.Exp).then_inc(s_grow_ev, 1)
                    if more:
                        conv_tanh(K + n + 3)

                with act.Fori(0, NPAIR // 2 - 1) as i:
                    for par in range(2):
                        pair(i * 2 + par, par, True)
                pair(NPAIR - 2, 0, True)
                pair(NPAIR - 1, 1, False)
                for f in range(FT):
                    m = P if f < FT - 1 else FR
                    o = (f % 2) * 2
                    N = b * FT + f
                    act.wait_ge(s_ffn_gate, N + 1)
                    if f >= 2:
                        act.wait_ge(s_ffn_hid, N)
                    A(f_half[0:m, f % 2, :], bank[o][0:m, :], ACT.Copy, scale=gs_sb[0:m, f:f + 1]).then_inc(s_ffn_scaled, 1)
                    A(f_th[0:m, f % 2, :], bank[o][0:m, :], ACT.Tanh, scale=gs_sb[0:m, f:f + 1]).then_inc(s_ffn_tanh, 1)

        @block.vector
        def _(dve):
            for free, n in DVE_CREDITS:
                dve.sem_inc(free, n)
            stt = dve.scalar_tensor_tensor
            tt = dve.tensor_tensor
            ts = dve.tensor_scalar
            dve.wait_ge(s_loads, 16 * N_LOADS)
            dve.tensor_reduce(w0_abs[:], w0_sb[:], AX_X, ALU.add, apply_absolute_value=True).then_inc(s_setup_dve, 1)
            ts(w0_sign[:], w0_sb[:], 0.0, 2.0, ALU.is_ge, ALU.mult).then_inc(s_setup_dve, 1)
            dve.wait_ge(s_setup_dve, 2)
            ts(w0_sign[:], w0_sign[:], -1.0, 1.0 / D, ALU.add, ALU.mult).then_inc(s_setup_sign, 1)
            dve.wait_ge(s_setup_sign, 1)
            for o in range(KT):
                ins = stt(out=w0_t[:, o, :], in0=w0_sign[:, o, :], scalar=w0_abs[:, o:o + 1], in1=w0_sb[:, o, :], op0=ALU.mult, op1=ALU.subtract)
            ins.then_inc(s_setup_sign, 1)
            dve.wait_ge(s_setup_sign, 2)
            tt(w0_sb[:], w0_t[:], w0_sb[:], ALU.add).then_inc(s_setup_dve, 1)
            dve.wait_ge(s_setup_pe, 1)
            dve.tensor_copy(w0_t[:].rearrange("p k d -> p (k d)"), bank[0][:]).then_inc(s_setup_dve, 1)
            ts(conv_sb[:], conv_sb[:], 0.5, None, ALU.mult)
            ts(gs_sb[:], gs_sb[:], 0.5, None, ALU.mult)
            tt(wout_sb[:], wout_sb[:], norm_sb[:].unsqueeze(2).to_broadcast([P, NPAIR, D]), ALU.mult)
            tt(dw_sb[:, 0:FT - 1, :], dw_sb[:, 0:FT - 1, :], ds_bc[:].unsqueeze(1).to_broadcast([P, FT - 1, D]), ALU.mult)
            tt(dw_sb[0:FR, FT - 1, :], dw_sb[0:FR, FT - 1, :], ds_bc[0:FR, :], ALU.mult).then_inc(s_setup_dve, 1)
            dve.wait_ge(s_setup_dve, 5)

            def layernorm(k, src):
                for t in range(NT):
                    ins = dve.bn_stats(stats[:, t, :], src[:, t, :])
                ins.then_inc(s_ln_stats, 1)
                dve.wait_ge(s_ln_stats, k * 2 + 1)
                dve.memset(spacer[:], 0.0)
                for t in range(NT):
                    ins = dve.bn_aggr(meanvar[:, t, :], stats[:, t, :])
                ins.then_inc(s_ln_stats, 1)
                dve.wait_ge(s_ln_stats, k * 2 + 2)
                ts(var_eps[:], meanvar[:, :, 1:2].rearrange("p t o -> p (t o)"), EPS, None, ALU.add).then_inc(s_ln_var, 1)
                dve.wait_ge(s_ln_rstd, k + 1)
                for t in range(NT):
                    ins = ts(xn[:, t, :], src[:, t, :], meanvar[:, t, 0:1], rstd[:, t:t + 1], ALU.subtract, ALU.mult)
                ins.then_inc(s_ln_xn, 1)
                dve.wait_ge(s_ln_turned, k + 1)
                dve.tensor_copy(xn_t[:, 1, :], bank[1][:]).then_inc(s_ln_xnt, 1)

            def k_out(b, h, par):
                dve.wait_ge(s_k_done, b * NH + h + 1)
                dve.wait_ge(s_q_ev, b * NH + h + 1)
                dve.tensor_copy(k_t[:, par, :], bank[1][:]).then_inc(s_k_ev, 1)

            def maxima(b, h, par):
                N = b * NH + h
                for j, (q, bk, at) in enumerate(((3, 2, 0), (2, 3, 0), (0, 3, 384), (1, 4, 0))):
                    w = (q + 1) * P
                    dve.wait_ge(s_scores_done, N * NT + (j + 1 if bk != 3 else 3))
                    ins = dve.tensor_reduce(neg_max[:, par, q:q + 1], bank[bk][:, at:at + w], AX_X, ALU.max, negate=True)
                ins.then_inc(s_max_done, 1)
                dve.wait_ge(s_max_done, N + 1)
                ts(bias[:, par, :], neg_max[:, par, :], SCALE, None, ALU.mult).then_inc(s_bias_done, 1)

            def normalise(b, h, par):
                N = b * NH + h
                dve.wait_ge(s_exp_done, N + 2)
                dve.reciprocal(inv_total[:, par, :], total[:, par, :]).then_inc(s_inv_done, 1)
                dve.wait_ge(s_inv_done, N + 1)
                for q in range(NT):
                    pr = prob[:, par, P_AT[q]:P_AT[q] + (q + 1) * P]
                    ins = ts(pr, pr, inv_total[:, par, q:q + 1], None, ALU.mult)
                ins.then_inc(s_norm_done, 1)

            def pair_gate(b, n, par):
                N = b * NPAIR + n
                dve.wait_ge(s_gate_tanh, N + 1)
                stt(out=gate[:, par, :], in0=gate_th[:], scalar=1.0, in1=bank[0][:], op0=ALU.add, op1=ALU.mult).then_inc(s_gate_ready, 1)

            def conv_taps(k, ch, src):
                dve.wait_ge(s_tap0, k + 1)
                for back, done in ((1, s_tap1), (2, s_tap2), (3, s_taps_done)):
                    if back > 1:
                        dve.wait_ge((s_tap1, s_tap2)[back - 2], k + 1)
                    stt(out=conv_acc[:, back:W], in0=src[:, 0:W - back], scalar=conv_sb[:, ch, TAPS - 1 - back:TAPS - back],
                        in1=conv_acc[:, back:W], op0=ALU.mult, op1=ALU.add).then_inc(done, 1)

            def conv_end(k, dst):
                dve.wait_ge(s_conv_tanh, k + 1)
                stt(out=dst, in0=conv_th[:], scalar=1.0, in1=conv_acc[:], op0=ALU.add, op1=ALU.mult).then_inc(s_conv_silu, 1)

            def wide(t):
                return t[:].rearrange("p t h -> p (t h)")

            with dve.Fori(0, NB) as b:
                dve.wait_ge(s_x_in, (b + 1) * 16)
                layernorm(b * 2, x_sb)
                k_out(b, 0, 0)
                maxima(b, 0, 0)
                normalise(b, 0, 0)

                def head(h, par, more):
                    N = b * NH + h
                    if more:
                        k_out(b, h + 1, 1 - par)
                    dve.wait_ge(s_turned_b, N + 1)
                    dve.wait_ge(s_z_done, N + 1)
                    dve.tensor_copy(prob_t[:, 512:1024], bank[6][:]).then_inc(s_pt_b, 1)
                    if more:
                        maxima(b, h + 1, 1 - par)
                    dve.wait_ge(s_z_done, N + 2)
                    dst = z_t[:, h, :] if isinstance(h, int) else z_t[:, bass.ds(h, 1), :].rearrange("p h w -> p (h w)")
                    dve.tensor_copy(dst, bank[7][:]).then_inc(s_z_ev, 1)
                    if more:
                        normalise(b, h + 1, 1 - par)

                with dve.Fori(0, NH // 2 - 1) as i:
                    for par in range(2):
                        head(i * 2 + par, par, True)
                head(NH - 2, 0, True)
                head(NH - 1, 1, False)

                dve.wait_ge(s_attn_out, b + 1)
                dve.wait_ge(s_x_bias, b + 1)
                for i in range(2):
                    ins = tt(x2[:, 2 * i:2 * i + 2, :].rearrange("p t d -> p (t d)"), bank[i][:],
                             x_sb[:, 2 * i:2 * i + 2, :].rearrange("p t d -> p (t d)"), ALU.add)
                ins.then_inc(s_x2_done, 1)
                dve.wait_ge(s_x2_done, b + 2)

                layernorm(b * 2 + 1, x2)
                K = b * (NPAIR + 2)
                dve.wait_ge(s_dt_done, b + 1)
                tt(dt_raw[:], bank[2][:, 0:NT * MH].rearrange("p (t h) -> p t h", t=NT),
                   dtb_bc[:].unsqueeze(1).to_broadcast([P, NT, MH]), ALU.add).then_inc(s_dt_biased, 1)
                dve.wait_ge(s_dt_biased, b + 1)
                stt(out=wide(dt_tmp), in0=wide(dt_raw), scalar=-1.0, in1=wide(dt_raw), op0=ALU.mult, op1=ALU.max).then_inc(s_dt_absed, 1)
                conv_taps(K, NPAIR, bank[0])
                conv_end(K, b_t[:])
                conv_taps(K + 1, NPAIR + 1, bank[1])
                conv_end(K + 1, c_t[:])
                dve.wait_ge(s_dt_ln, b + 1)
                stt(out=wide(dt_sb), in0=wide(dt_raw), scalar=0.0, in1=wide(dt_tmp), op0=ALU.max, op1=ALU.add).then_inc(s_dt_ready, 1)
                dve.wait_ge(s_dt_ready, b + 1)
                stt(out=da[:], in0=dt_sb[:], scalar=-1.0, in1=exp_a[:].unsqueeze(1).to_broadcast([P, NT, MH]),
                    op0=ALU.mult, op1=ALU.mult).then_inc(s_da_ready, 1)
                dve.wait_ge(s_cb_done, b + 1)
                tt(cb[:], bank[3][:].rearrange("p (t i) -> p t i", t=NT), upto[:].unsqueeze(1).to_broadcast([P, NT, P]), ALU.mult).then_inc(s_cb_ev, 1)
                dve.wait_ge(s_cb_ev, b + 1)
                pair_gate(b, 0, 0)
                conv_taps(K + 2, 0, bank[1])
                conv_end(K + 2, xs[:, 0, :])

                def pair(n, par, more):
                    N = b * NPAIR + n
                    dve.wait_ge(s_hid_ready, N + 1)
                    dve.wait_ge(s_x_turned, N + 1)
                    tt(x_dt[:, par, :, :].rearrange("p t (h q) -> p t h q", h=2),
                       bank[2][:].rearrange("p (t h q) -> p t h q", t=NT, h=2),
                       dt_sb[:, :, bass.ds(n * 2, 2)].unsqueeze(3).to_broadcast([P, NT, 2, HD]), ALU.mult).then_inc(s_xdt_ready, 1)
                    dve.wait_ge(s_mix_exp0, N + 1)
                    tt(mix[:, par, 0, :], mix[:, par, 0, :], cb[:].rearrange("p t i -> p (t i)"), ALU.mult)
                    dve.wait_ge(s_mix_exp1, N + 1)
                    tt(mix[:, par, 1, :], mix[:, par, 1, :], cb[:].rearrange("p t i -> p (t i)"), ALU.mult).then_inc(s_mix_ready, 1)
                    if more:
                        pair_gate(b, n + 1, 1 - par)
                        conv_taps(K + n + 3, n + 1 if isinstance(n, int) else bass.ds(n + 1, 1), bank[1])
                    dve.wait_ge(s_off_done, N + 2)
                    dve.wait_ge(s_grow_ev, N + 2)
                    tt(y_in[:, P:W], bank[4][:, 0:W - P], grow[:, 0:W - P], ALU.mult).then_inc(s_off_scaled, 1)
                    if more:
                        conv_end(K + n + 3, xs[:, 1 - par, :])
                    dve.wait_ge(s_off_scaled, N + 2)
                    stt(out=y_x[:], in0=xs[:, par, :], scalar=d_sb[:, n:n + 1] if isinstance(n, int) else d_sb[:, bass.ds(n, 1)],
                        in1=y_in[:], op0=ALU.mult, op1=ALU.add).then_inc(s_skip_done, 1)
                    dve.wait_ge(s_diag_done, N + 1)
                    dve.wait_ge(s_skip_done, N + 1)
                    tt(y_all[:], bank[5][:], y_x[:], ALU.add).then_inc(s_y_ready, 1)
                    dve.wait_ge(s_y_ready, N + 2)
                    dve.wait_ge(s_projected, N + 1)
                    dve.wait_ge(s_squared, N + 1)
                    tt(hid[:, par, :], y_all[:], gate[:, par, :], ALU.mult).then_inc(s_hid_ready, 1)

                with dve.Fori(0, NPAIR // 2 - 1) as i:
                    for par in range(2):
                        pair(i * 2 + par, par, True)
                pair(NPAIR - 2, 0, True)
                pair(NPAIR - 1, 1, False)
                dve.wait_ge(s_ss_done, b + 2)
                ts(ms_eps[:], bank[4][:, 0:NT], 1.0 / (NPAIR * P), 4 * EPS, ALU.mult, ALU.add).then_inc(s_ms_ready, 1)
                for f in range(FT):
                    m = P if f < FT - 1 else FR
                    o = (f % 2) * 2
                    N = b * FT + f
                    dve.wait_ge(s_ffn_tanh, N + 1)
                    dve.wait_ge(s_ffn_hid, N + 1)
                    stt(out=f_silu[0:m, :], in0=f_th[0:m, f % 2, :], scalar=1.0, in1=f_half[0:m, f % 2, :], op0=ALU.add, op1=ALU.mult).then_inc(s_ffn_silu, 1)
                    dve.wait_ge(s_ffn_silu, N + 1)
                    dve.wait_ge(s_ffn_up, N + 1)
                    stt(out=f_hid[0:m, f, :], in0=bank[o + 1][0:m, :], scalar=us_sb[0:m, f:f + 1], in1=f_silu[0:m, :], op0=ALU.mult, op1=ALU.mult).then_inc(s_ffn_hid, 1)
                dve.wait_ge(s_ffn_out, b + 1)
                for i in range(2):
                    ins = tt(res[:, 2 * i:2 * i + 2, :].rearrange("p t d -> p (t d)"), bank[4 + i][:],
                             x2[:, 2 * i:2 * i + 2, :].rearrange("p t d -> p (t d)"), ALU.add)
                ins.then_inc(s_res_ready, 1)
                dve.wait_ge(s_res_ready, b + 1)
                dve.wait_ge(s_rms_ready, b + 1)
                dve.wait_ge(s_projected, (b + 1) * NPAIR + 2)
                dve.wait_ge(s_stored, b * 16 + 16)
                for t in range(NT):
                    ins = stt(out=y_out[:, t, :], in0=bank[6 + t // 2][:, (t % 2) * D:(t % 2 + 1) * D], scalar=rms[:, t:t + 1],
                              in1=res[:, t, :], op0=ALU.mult, op1=ALU.add)
                ins.then_inc(s_y_done, 1)


def kernel(**inputs):
    import numpy as np
    import concourse.bacc as bacc
    from concourse.bass_utils import run_bass_kernel_spmd as run

    a = {k: np.asarray(v) for k, v in inputs.items()}

    def tiles(w_t):
        return w_t.reshape(-1, P, w_t.shape[1]).transpose(1, 0, 2)

    NH, DH, D = a["L0_attn_W_Q"].shape
    qkv = np.stack([a[f"L0_attn_W_{c}"] for c in "QKV"])
    qkv = qkv.reshape(3, NH, DH, D // P, P).transpose(1, 4, 0, 3, 2)
    w_in = a["L1_attn_in_proj_w"]
    inner = a["L1_attn_norm_w"].shape[0]
    pairs = inner // P
    both = np.stack([w_in[:, 0:inner], w_in[:, inner:2 * inner]])
    both = both.reshape(2, D // P, P, pairs, P).transpose(3, 2, 0, 1, 4)
    conv = np.concatenate([a["L1_attn_conv_w"], a["L1_attn_conv_b"][:, None]], axis=1)
    F = a["L1_ffn_gate_w"].shape[0]
    ft = -(-F // P)

    def column(v):
        c = np.zeros((ft * P,), v.dtype)
        c[:F] = v
        return c.reshape(ft, P).T

    per_head = inner // a["L1_attn_D_param"].shape[0]
    arrays = {
        "x": a["L0_attn_x"],
        "wqkv": qkv,
        "wo_t": a["L0_attn_W_O"].T.reshape(NH, DH, D).transpose(1, 0, 2),
        "w0": tiles(a["L0_ffn_weight"]),
        "b0": a["L0_ffn_bias"],
        "w_pair": both,
        "w_out": tiles(a["L1_attn_out_proj_w"]),
        "w_bc": tiles(w_in[:, 2 * inner:2 * inner + 2 * P]),
        "w_dt": tiles(w_in[:, 2 * inner + 2 * P:]),
        "conv_par": conv.reshape(pairs + 2, P, -1).transpose(1, 0, 2),
        "dt_bias": a["L1_attn_dt_bias"],
        "a_log": a["L1_attn_A_log"],
        "d_col": np.repeat(a["L1_attn_D_param"], per_head).reshape(pairs, P).T,
        "norm_col": a["L1_attn_norm_w"].reshape(pairs, P).T,
        "gate_t": tiles(a["L1_ffn_gate_w"].T),
        "up_t": tiles(a["L1_ffn_up_w"].T),
        "down_t": a["L1_ffn_down_w"].T,
        "gate_s": column(a["L1_ffn_gate_s"]),
        "up_s": column(a["L1_ffn_up_s"]),
        "down_s": a["L1_ffn_down_s"],
    }
    nc = bacc.Bacc("TRN2", target_bir_lowering=False, num_devices=1)
    fed, aps = {}, {}
    for name, v in arrays.items():
        v = np.ascontiguousarray(v)
        fed[f"in_{name}"] = v
        aps[name] = nc.dram_tensor(f"in_{name}", v.shape, mybir.dt.from_np(v.dtype), kind="ExternalInput").ap()
    aps["out"] = nc.dram_tensor("out_0", arrays["x"].shape, F32, kind="ExternalOutput").ap()
    two_layers(nc, **aps)
    return run(nc, [fed], core_ids=[0]).results[0]["out_0"]
```

```python
from contextlib import ExitStack

import concourse.bass as bass
from concourse import mybir

F32 = mybir.dt.float32
BF16 = mybir.dt.bfloat16
F32R = mybir.dt.float32r
ALU = mybir.AluOpType
ACT = mybir.ActivationFunctionType
AX_X = mybir.AxisListType.X

P = 128
EPS = 1e-5
TAPS = 4


def two_layers(nc, x, wqkv, wo_t, w0, b0, w_pair, w_out, w_bc, w_dt, conv_par, dt_bias, a_log,
               d_col, norm_col, gate_t, up_t, down_t, gate_s, up_s, down_s, out):
    NB, S, D = x.shape
    NH = wqkv.shape[0]
    NT = S // P
    KT = D // P
    NPAIR = w_pair.shape[0]
    MH = dt_bias.shape[0]
    HD = P // 2
    F = gate_t.shape[2]
    FT = -(-F // P)
    FR = F - (FT - 1) * P
    SCALE = float(P) ** -0.5
    W = NT * P
    assert FT == 6 and 2 * MH == P and W == 512 and D == 256 and NH % 2 == 0 and NPAIR % 2 == 0 and NT == 4

    P_AT = {3: 0, 2: 512, 0: 896, 1: 1024}
    PT_AT = {0: 0, 1: 512, 3: 896, 2: 1024}
    NP = 1280
    FEEDS = [(a, c) for a in range(NT) for c in range(a + 1, NT)]

    with ExitStack() as ctx:
        def sb(name, shape, dt=F32):
            return ctx.enter_context(nc.sbuf_tensor(name, shape, dt))

        def sem(name):
            return ctx.enter_context(nc.semaphore(name))

        bank = [ctx.enter_context(nc.psum_tensor(f"bank{i}", [P, 512], F32)) for i in range(8)]

        ident = sb("ident", [P, P])
        ident_bf = sb("ident_bf", [P, P], BF16)
        causal_bf = sb("causal_bf", [P, P], BF16)
        upto = sb("upto", [P, P])
        after = sb("after", [P, P])
        ones = sb("ones", [P, P])
        minus_half = sb("minus_half", [P, NT])
        wo_sb = sb("wo_sb", [P, NH, D])
        w0_sb = sb("w0_sb", [P, KT, D])
        w0_abs = sb("w0_abs", [P, KT])
        w0_sign = sb("w0_sign", [P, KT, D])
        w0_t = sb("w0_t", [P, KT, D])
        b0_bc = sb("b0_bc", [P, D])
        wbc_sb = sb("wbc_sb", [P, KT, 2 * P])
        wdt_sb = sb("wdt_sb", [P, KT, MH])
        conv_sb = sb("conv_sb", [P, NPAIR + 2, TAPS + 1])
        dtb_bc = sb("dtb_bc", [P, MH])
        exp_a = sb("exp_a", [P, MH])
        d_sb = sb("d_sb", [P, NPAIR])
        norm_sb = sb("norm_sb", [P, NPAIR])
        gw_sb = sb("gw_sb", [P, KT, F])
        uw_sb = sb("uw_sb", [P, KT, F])
        dw_sb = sb("dw_sb", [P, FT, D])
        gs_sb = sb("gs_sb", [P, FT])
        us_sb = sb("us_sb", [P, FT])
        ds_bc = sb("ds_bc", [P, D])

        x_sb = sb("x_sb", [P, NT, D])
        xn = sb("xn", [P, NT, D])
        xn_t = sb("xn_t", [P, KT, W])
        spacer = sb("spacer", [P, 1])
        stats = sb("stats", [P, NT, 6])
        meanvar = sb("meanvar", [P, NT, 2])
        var_eps = sb("var_eps", [P, NT])
        rstd = sb("rstd", [P, NT])
        raw = sb("raw", [P, 2, 3 * KT * P])
        w_r = sb("w_r", [P, 2, 2, 3, KT, P], F32R)
        w_r_flat = [[w_r[:, a, i, :, :, :].rearrange("p m k e -> p (m k e)") for i in range(2)] for a in range(2)]
        raw_out = sb("raw_out", [P, 2, D])
        wo_r = sb("wo_r", [P, 2, 2, D], F32R)
        xn_r = sb("xn_r", [P, 2, KT, W], F32R)
        neg_max = sb("neg_max", [P, 2, NT])
        bias = sb("bias", [P, 2, NT])
        total = sb("total", [P, 2, NT])
        inv_total = sb("inv_total", [P, 2, NT])
        shared = sb("shared", [P, NH * W])
        z_t = shared[:].rearrange("p (h w) -> p h w", h=NH)
        n_mix, n_xw, n_ffn = 4 * NT * P, len(FEEDS) * P, FT * W
        mix = shared[:, 0:n_mix].rearrange("p (a h w) -> p a h w", a=2, h=2)
        x_w = shared[:, n_mix:n_mix + n_xw].rearrange("p (f q) -> p f q", f=len(FEEDS))
        f_hid = shared[:, n_mix + n_xw:n_mix + n_xw + n_ffn].rearrange("p (f w) -> p f w", f=FT)
        f_at = n_mix + n_xw + n_ffn
        f_th = shared[:, f_at:f_at + 2 * W].rearrange("p (a w) -> p a w", a=2)
        f_silu = shared[:, f_at + 2 * W:f_at + 4 * W].rearrange("p (a w) -> p a w", a=2)
        x2 = sb("x2", [P, NT, D])

        place = sb("place", [P, 11 * W])
        prob = place[:, 0:2 * NP].rearrange("p (a n) -> p a n", a=2)
        xs = place[:, 0:2 * W].rearrange("p (a w) -> p a w", a=2)
        gate = place[:, 2 * W:4 * W].rearrange("p (a w) -> p a w", a=2)
        x_dt = place[:, 4 * W:6 * W].rearrange("p (a t q) -> p a t q", a=2, t=NT)
        hid, y, square = (place[:, i * W:(i + 1) * W] for i in (6, 9, 10))
        grow = place[:, 7 * W:9 * W].rearrange("p (a w) -> p a w", a=2)
        place_r = sb("place_r", [P, 8 * W + 2 * NP], F32R)
        q_r = place_r[:, 0:2 * W].rearrange("p (i w) -> p i w", i=2)
        k_r = place_r[:, 2 * W:4 * W].rearrange("p (i w) -> p i w", i=2)
        v_r = place_r[:, 4 * W:8 * W].rearrange("p (a i t e) -> p a i t e", a=2, i=2, t=NT)
        prob_r = place_r[:, 8 * W:8 * W + 2 * NP].rearrange("p (i n) -> p i n", i=2)
        hid_r = place_r[:, 0:4 * W].rearrange("p (a i w) -> p a i w", a=2, i=2)

        conv_acc = sb("conv_acc", [P, W])
        conv_th = sb("conv_th", [P, W])
        gate_th = sb("gate_th", [P, W])
        b_t = sb("b_t", [P, W])
        c_t = sb("c_t", [P, W])
        b_sb = sb("b_sb", [P, NT, P])
        cb = sb("cb", [P, NT, P])
        dt_raw = sb("dt_raw", [P, NT, MH])
        dt_tmp = sb("dt_tmp", [P, NT, MH])
        dt_sb = sb("dt_sb", [P, NT, MH])
        da = sb("da", [P, NT, 2, MH])
        dec = sb("dec", [P, len(FEEDS), MH])
        cum = place[:, 9 * W:10 * W]
        cum_r = sb("cum_r", [2 * MH, W], F32R)
        pick = sb("pick", [P, 2, 2], F32R)
        cum_neg = sb("cum_neg", [P, NT, MH])
        state = sb("state", [P, NT - 1, P])
        y_in = sb("y_in", [P, W])
        sumsq = sb("sumsq", [P, W])
        ms_eps = sb("ms_eps", [P, NT])
        rms = sb("rms", [P, NT])

        s_loads = sem("loads")
        s_consts = sem("consts")
        s_x_in = sem("x_in")
        s_stored = sem("stored")
        s_xnt_half = sem("xnt_half")
        s_setup_sign = sem("setup_sign")
        s_setup_act = sem("setup_act")
        s_setup_dve = sem("setup_dve")
        s_setup_pe = sem("setup_pe")
        s_ln_stats = sem("ln_stats")
        s_ln_var = sem("ln_var")
        s_ln_rstd = sem("ln_rstd")
        s_ln_xn = sem("ln_xn")
        s_ln_turned = sem("ln_turned")
        s_ln_xnt = sem("ln_xnt")
        s_x_bias = sem("x_bias")
        s_q_done = sem("q_done")
        s_k_done = sem("k_done")
        s_q_ev = sem("q_ev")
        s_k_ev = sem("k_ev")
        s_v_ev = sem("v_ev")
        s_scores_done = sem("scores_done")
        s_max_done = sem("max_done")
        s_bias_done = sem("bias_done")
        s_exp_done = sem("exp_done")
        s_inv_done = sem("inv_done")
        s_norm_done = sem("norm_done")
        s_turned_a = sem("turned_a")
        s_turned_b = sem("turned_b")
        s_turned_c = sem("turned_c")
        s_pt_a = sem("pt_a")
        s_pt_b = sem("pt_b")
        s_pt_c = sem("pt_c")
        s_z_done = sem("z_done")
        s_z_ev = sem("z_ev")
        s_attn_out = sem("attn_out")
        s_x2_done = sem("x2_done")
        s_dt_done = sem("dt_done")
        s_dt_biased = sem("dt_biased")
        s_dt_absed = sem("dt_absed")
        s_dt_exp = sem("dt_exp")
        s_dt_ln = sem("dt_ln")
        s_dt_ready = sem("dt_ready")
        s_da_ready = sem("da_ready")
        s_bc_done = sem("bc_done")
        s_tap0 = sem("tap0")
        s_tap1 = sem("tap1")
        s_tap2 = sem("tap2")
        s_taps_done = sem("taps_done")
        s_conv_tanh = sem("conv_tanh")
        s_conv_silu = sem("conv_silu")
        s_b_turned = sem("b_turned")
        s_b_ev = sem("b_ev")
        s_cb_done = sem("cb_done")
        s_cb_ev = sem("cb_ev")
        s_dec_done = sem("dec_done")
        s_dec_ready = sem("dec_ready")
        s_xc_done = sem("xc_done")
        s_gate_tanh = sem("gate_tanh")
        s_gate_ready = sem("gate_ready")
        s_mix_exp0 = sem("mix_exp0")
        s_mix_exp1 = sem("mix_exp1")
        s_mix_ready = sem("mix_ready")
        s_x_turned = sem("x_turned")
        s_xdt_ready = sem("xdt_ready")
        s_xw_ready = sem("xw_ready")
        s_state_done = sem("state_done")
        s_state_ev = sem("state_ev")
        s_grow_ev = sem("grow_ev")
        s_off_done = sem("off_done")
        s_off_scaled = sem("off_scaled")
        s_skip_done = sem("skip_done")
        s_diag_done = sem("diag_done")
        s_y_ready = sem("y_ready")
        s_hid_ready = sem("hid_ready")
        s_squared = sem("squared")
        s_summed = sem("summed")
        s_projected = sem("projected")
        s_ss_done = sem("ss_done")
        s_ms_ready = sem("ms_ready")
        s_rms_ready = sem("rms_ready")
        s_ffn_gate = sem("ffn_gate")
        s_ffn_up = sem("ffn_up")
        s_ffn_tanh = sem("ffn_tanh")
        s_ffn_silu = sem("ffn_silu")
        s_ffn_hid = sem("ffn_hid")
        s_ffn_out = sem("ffn_out")
        s_res_ready = sem("res_ready")
        s_y_done = sem("y_done")
        s_xn_hi = sem("xn_hi")
        s_xn_lo = sem("xn_lo")
        s_w_hi = sem("w_hi")
        s_w_ready = sem("w_ready")
        s_w_used = sem("w_used")
        s_out_hi = sem("out_hi")
        s_out_ready = sem("out_ready")
        s_q_hi = sem("q_hi")
        s_k_hi = sem("k_hi")
        s_v_hi = sem("v_hi")
        s_pt_a_hi = sem("pt_a_hi")
        s_pt_b_hi = sem("pt_b_hi")
        s_pt_c_hi = sem("pt_c_hi")
        s_cum_done = sem("cum_done")
        s_cum_ev = sem("cum_ev")
        s_cum_hi = sem("cum_hi")
        s_cum_split = sem("cum_split")
        s_cum_turned = sem("cum_turned")
        s_cum_neg_ready = sem("cum_neg_ready")
        s_pick_ready = sem("pick_ready")
        s_cum_spread = sem("cum_spread")
        s_cum0_done = sem("cum0_done")
        s_cum1_done = sem("cum1_done")
        s_hid_hi = sem("hid_hi")
        s_hid_split = sem("hid_split")
        s_w_in0 = sem("w_in0")
        s_w_in1 = sem("w_in1")
        s_out_in0 = sem("out_in0")
        s_out_in1 = sem("out_in1")
        w_in, out_in = (s_w_in0, s_w_in1), (s_out_in0, s_out_in1)

        PE_CREDITS = ((s_z_done, 1), (s_state_done, 1), (s_off_done, 1), (s_projected, 2), (s_ss_done, 1), (s_w_used, 2))
        ACT_CREDITS = ((s_exp_done, 1), (s_state_ev, 1), (s_mix_exp1, 1))
        DVE_CREDITS = ((s_k_ev, 1), (s_v_ev, 1), (s_pt_a, 1), (s_pt_b, 1), (s_z_ev, 1), (s_x2_done, 1), (s_gate_ready, 1),
                       (s_conv_silu, 1), (s_off_scaled, 1), (s_y_ready, 1), (s_hid_ready, 1),
                       (s_ffn_silu, 2), (s_ffn_hid, 2), (s_y_done, 1), (s_out_ready, 2))
        POOL_CREDITS = ((s_hid_split, 1), (s_squared, 1), (s_w_ready, 2), (s_stored, 16))
        SLOTS = NH + NPAIR

        block = ctx.enter_context(nc.Block())
        FFN_BANKS = ((3, 4), (5, 7))
        N_LOADS = 17
        NCONST = 9

        @block.sync
        def _(sp):
            resident = [
                (wo_sb[:], wo_t), (w0_sb[:], w0), (b0_bc[:], b0.unsqueeze(0).to_broadcast([P, D])),
                (wbc_sb[:], w_bc), (wdt_sb[:], w_dt), (conv_sb[:], conv_par),
                (dtb_bc[:], dt_bias.unsqueeze(0).to_broadcast([P, MH])),
                (exp_a[:], a_log.unsqueeze(0).to_broadcast([P, MH])),
                (d_sb[:], d_col), (norm_sb[:], norm_col), (gw_sb[:], gate_t), (uw_sb[:], up_t),
                (dw_sb[:, 0:FT - 1, :], down_t[0:(FT - 1) * P, :].rearrange("(f p) d -> p f d", p=P)),
                (dw_sb[0:FR, FT - 1, :], down_t[(FT - 1) * P:F, :]),
                (gs_sb[:], gate_s), (us_sb[:], up_s),
                (ds_bc[:], down_s.unsqueeze(0).to_broadcast([P, D])),
            ]
            assert len(resident) == N_LOADS
            for dst, src in resident:
                sp.dma_start(dst, src).then_inc(s_loads, 16)
            with sp.Fori(0, NB) as b:
                sp.wait_ge(s_x2_done, b * NT + 1)
                sp.dma_start(x_sb[:], x[bass.ds(b, 1), :, :].rearrange("b (t p) d -> p (b t) d", p=P)).then_inc(s_x_in, 16)
                with sp.Fori(0, NH // 2) as i:
                    for par in range(2):
                        sp.wait_ge(s_w_ready, b * SLOTS + i * 2 + par + 1)
                        sp.dma_start(raw[:, par, :], wqkv[bass.ds(i * 2 + par, 1), :, :].rearrange("h p w -> p (h w)")).then_inc(w_in[par], 16)
                with sp.Fori(0, NPAIR // 2) as i:
                    for par in range(2):
                        sp.wait_ge(s_w_ready, b * SLOTS + NH + i * 2 + par + 1)
                        sp.dma_start(raw[:, par, 0:2 * D], w_pair[bass.ds(i * 2 + par, 1), :, :].rearrange("h p w -> p (h w)")).then_inc(w_in[par], 16)
                        sp.wait_ge(s_out_ready, b * NPAIR + i * 2 + par + 1)
                        sp.dma_start(raw_out[:, par, :], w_out[bass.ds(i * 2 + par, 1), :, :].rearrange("h p d -> p (h d)")).then_inc(out_in[par], 16)
                sp.wait_ge(s_y_done, b + 2)
                sp.dma_start(out[bass.ds(b, 1), :, :].rearrange("b (t p) d -> p (b t) d", p=P), x2[:]).then_inc(s_stored, 16)
            sp.wait_ge(s_stored, 16 * NB + 16)

        @block.gpsimd
        def _(pool):
            for free, n in POOL_CREDITS:
                pool.sem_inc(free, n)
            pool.memset(ident[:], 0.0).then_inc(s_consts, 1)
            pool.memset(upto[:], 1.0).then_inc(s_consts, 1)
            pool.memset(after[:], 1.0).then_inc(s_consts, 1)
            pool.memset(ones[:], 1.0).then_inc(s_consts, 1)
            pool.memset(causal_bf[:], 0.0).then_inc(s_consts, 1)
            pool.memset(minus_half[:], -0.5).then_inc(s_consts, 1)
            pool.memset(ident_bf[:], 0.0).then_inc(s_consts, 1)
            pool.memset(y_in[:, 0:P], 0.0).then_inc(s_consts, 1)
            pool.wait_ge(s_consts, 8)
            for t in (ident, ident_bf):
                pool.affine_select(out=t[:], in_=t[:], compare_op=ALU.not_equal, fill=1.0, base=0,
                                   pattern=[[-1, P]], channel_multiplier=1)
            pool.affine_select(out=upto[:], in_=upto[:], compare_op=ALU.is_ge, fill=0.0, base=0,
                               pattern=[[1, P]], channel_multiplier=-1)
            pool.affine_select(out=after[:], in_=after[:], compare_op=ALU.is_ge, fill=0.0, base=-1,
                               pattern=[[-1, P]], channel_multiplier=1)
            pool.affine_select(out=causal_bf[:], in_=causal_bf[:], compare_op=ALU.is_ge, fill=-1e10, base=0,
                               pattern=[[-1, P]], channel_multiplier=1).then_inc(s_consts, 1)

            def rstd_of(g, t0, t1):
                pool.wait_ge(s_ln_var, g + 1)
                pool.tensor_tensor(rstd[:, t0:t1], var_eps[:, t0:t1], minus_half[:, t0:t1], ALU.pow).then_inc(s_ln_rstd, 1)

            def split_low(slot, par, width):
                pool.wait_ge(s_w_hi, slot + 1)
                pool.tensor_tensor(w_r_flat[par][1][:, 0:width], raw[:, par, 0:width],
                                   w_r_flat[par][0][:, 0:width].bitcast(F32), ALU.subtract).then_inc(s_w_ready, 1)

            def weigh_x(b, n, par):
                N = b * NPAIR + n
                pool.wait_ge(s_xdt_ready, N + 1)
                pool.wait_ge(s_state_done, N + 1)
                at = 0
                for a in range(NT - 1):
                    k = NT - 1 - a
                    o = x_w[:, at:at + k, :].rearrange("p k (h q) -> p k h q", h=2)
                    i0 = x_dt[:, par, a, :].rearrange("p (h q) -> p h q", h=2).unsqueeze(1).to_broadcast([P, k, 2, HD])
                    i1 = dec[:, at:at + k, bass.ds(n * 2, 2)].unsqueeze(3).to_broadcast([P, k, 2, HD])
                    ins = pool.tensor_tensor(o, i0, i1, ALU.mult)
                    at += k
                ins.then_inc(s_xw_ready, 1)

            def pick_heads(b, n, par):
                pool.tensor_tensor(pick[:, par, :], ident[:, bass.ds(n * 2, 2)], ident[:, bass.ds(n * 2 + MH, 2)],
                                   ALU.add).then_inc(s_pick_ready, 1)

            def hid_low(b, n, par):
                pool.wait_ge(s_hid_hi, b * NPAIR + n + 1)
                pool.tensor_tensor(hid_r[:, par, 1, :], hid, hid_r[:, par, 0, :].bitcast(F32), ALU.subtract).then_inc(s_hid_split, 1)

            def add_squares(b, n):
                N = b * NPAIR + n
                pool.wait_ge(s_squared, N + 2)
                pool.wait_ge(s_summed, N + b + 1)
                pool.tensor_tensor(sumsq[:], sumsq[:], square, ALU.add).then_inc(s_summed, 1)

            with pool.Fori(0, NB) as b:
                rstd_of(b * 3, 0, NT)
                split_low(b * SLOTS, 0, 3 * D)
                split_low(b * SLOTS + 1, 1, 3 * D)
                pool.wait_ge(s_ln_xn, b * 3 + 1)
                pool.wait_ge(s_loads, 16 * N_LOADS)
                pool.tensor_tensor(x_sb[:], x_sb[:], b0_bc[:].unsqueeze(1).to_broadcast([P, NT, D]), ALU.add).then_inc(s_x_bias, 1)
                with pool.Fori(1, NH // 2) as i:
                    for par in range(2):
                        split_low(b * SLOTS + i * 2 + par, par, 3 * D)
                pool.wait_ge(s_ss_done, b + 1)
                rstd_of(b * 3 + 1, 0, NT - 1)
                pool.memset(sumsq[:], 0.0).then_inc(s_summed, 1)
                rstd_of(b * 3 + 2, NT - 1, NT)
                pick_heads(b, 0, 0)
                pick_heads(b, 1, 1)
                pool.wait_ge(s_xn_hi, b * 2 + 2)
                pool.tensor_tensor(xn_r[:, 1, :, :], xn_t[:], xn_r[:, 0, :, :].bitcast(F32), ALU.subtract).then_inc(s_xn_lo, 1)
                split_low(b * SLOTS + NH, 0, 2 * D)
                split_low(b * SLOTS + NH + 1, 1, 2 * D)

                def pair(n, par, more, first=False):
                    weigh_x(b, n, par)
                    if more:
                        pick_heads(b, n + 2, par)
                    if not first:
                        hid_low(b, n - 1, 1 - par)
                    if more:
                        split_low(b * SLOTS + NH + n + 2, par, 2 * D)
                    if not first:
                        add_squares(b, n - 1)

                pool.wait_ge(s_dec_ready, b + 1)
                pair(0, 0, True, first=True)
                pair(1, 1, True)
                with pool.Fori(1, NPAIR // 2 - 1) as i:
                    for par in range(2):
                        pair(i * 2 + par, par, True)
                pair(NPAIR - 2, 0, False)
                pair(NPAIR - 1, 1, False)
                hid_low(b, NPAIR - 1, 1)
                add_squares(b, NPAIR - 1)
                pool.wait_ge(s_ms_ready, b + 1)
                pool.tensor_tensor(rms[:], ms_eps[:], minus_half[:], ALU.pow).then_inc(s_rms_ready, 1)

        @block.tensor
        def _(pe):
            for free, n in PE_CREDITS:
                pe.sem_inc(free, n)
            mm = pe.matmul

            def mm3(out, w, m, start, stop, **kw):
                for i, (a, b) in enumerate(((0, 1), (1, 0), (0, 0))):
                    ins = mm(out, lhsT=w(a), rhs=m(b), start=(start and i == 0), stop=(stop and i == 2), **kw)
                return ins

            pe.wait_ge(s_consts, NCONST)
            pe.wait_ge(s_setup_dve, 3)
            for o in range(KT):
                for k in range(KT):
                    ins = pe.transpose(bank[0][:, k * D + o * P:k * D + (o + 1) * P], w0_sb[:, o, k * P:(k + 1) * P], ident[:])
            ins.then_inc(s_setup_pe, 1)
            pe.wait_ge(s_setup_dve, 4)

            def turn_norm(g, tiles):
                pe.wait_ge(s_ln_xn, g + 1)
                for d in range(KT):
                    for t in tiles:
                        ins = pe.transpose(bank[d][:, t * P:(t + 1) * P], xn[:, t, d * P:(d + 1) * P], ident[:])
                return ins

            def project(o, par, m):
                for k in range(KT):
                    ins = mm3(o, lambda i: w_r[:, par, i, m, k, :], lambda i: xn_r[:, i, k, :], k == 0, k == KT - 1)
                return ins

            def project_qk(b, h, par):
                N = b * NH + h
                pe.wait_ge(s_w_ready, b * SLOTS + h + 3)
                pe.wait_ge(s_v_ev, N + 1)
                project(bank[0][:], par, 0).then_inc(s_q_done, 1)
                pe.wait_ge(s_k_ev, N + 1)
                project(bank[1][:], par, 1).then_inc(s_k_done, 1)

            def project_v(b, h, par):
                N = b * NH + h
                pe.wait_ge(s_q_ev, N + 1)
                for t in range(NT):
                    for k in range(KT):
                        ins = mm3(bank[0][:, t * P:(t + 1) * P], lambda i: xn_r[:, i, k, t * P:(t + 1) * P],
                                  lambda i: w_r[:, par, i, 2, k, :], k == 0, k == KT - 1)
                ins.then_inc(s_w_used, 1)

            def score(b, h, par):
                N = b * NH + h
                pe.wait_ge(s_q_ev, N + 1)
                pe.wait_ge(s_k_ev, N + 2)
                pe.wait_ge(s_exp_done, N + 1)
                for q, bk, at in ((3, 2, 0), (2, 3, 0), (0, 3, 384), (1, 4, 0)):
                    w = (q + 1) * P
                    mm3(bank[bk][:, at:at + w], lambda i: q_r[:, i, q * P:(q + 1) * P], lambda i: k_r[:, i, 0:w], True, True)
                    mm(bank[bk][:, at + w - P:at + w], lhsT=ident_bf[:], rhs=causal_bf[:], start=False, stop=True,
                       skip_group_check=True).then_inc(s_scores_done, 1)

            def turn_probs(b, h, par):
                N = b * NH + h
                pe.wait_ge(s_norm_done, N + 1)
                pe.wait_ge(s_pt_a, N + 1)
                for q in range(NT):
                    ins = pe.transpose(bank[5][:, q * P:(q + 1) * P], prob[:, par, P_AT[q]:P_AT[q] + P], ident[:])
                ins.then_inc(s_turned_a, 1)
                pe.wait_ge(s_pt_b, N + 1)
                for k, q in ((1, 1), (1, 2), (1, 3), (3, 3)):
                    at = PT_AT[k] - PT_AT[1] + (q - k) * P
                    ins = pe.transpose(bank[6][:, at:at + P], prob[:, par, P_AT[q] + k * P:P_AT[q] + (k + 1) * P], ident[:])
                ins.then_inc(s_turned_b, 1)
                pe.wait_ge(s_z_ev, N + 1)
                for q in (2, 3):
                    ins = pe.transpose(bank[7][:, (q - 2) * P:(q - 1) * P], prob[:, par, P_AT[q] + 2 * P:P_AT[q] + 3 * P], ident[:])
                ins.then_inc(s_turned_c, 1)

            def weigh_values(b, h, par):
                N = b * NH + h
                pe.wait_ge(s_pt_a, N + 2)
                pe.wait_ge(s_pt_b, N + 2)
                pe.wait_ge(s_pt_c, N + 1)
                pe.wait_ge(s_v_ev, N + 2)
                for k in range(NT):
                    ins = mm3(bank[7][:, k * P:W], lambda i: v_r[:, par, i, k, :], lambda i: prob_r[:, i, PT_AT[k]:PT_AT[k] + W - k * P],
                              k == 0, True, skip_group_check=True)
                ins.then_inc(s_z_done, 1)

            def out_tile(banks, t):
                return bank[banks[t // 2]][:, (t % 2) * D:(t % 2 + 1) * D]

            def attention_out(b):
                pe.wait_ge(s_z_ev, (b + 1) * NH + 1)
                for t in range(NT):
                    for h in range(NH):
                        mm(bank[t][:, 0:D], lhsT=z_t[:, h, t * P:(t + 1) * P], rhs=wo_sb[:, h, :], start=(h == 0), stop=False)
                    for k in range(KT):
                        ins = mm(bank[t][:, 0:D], lhsT=xn_t[:, k, t * P:(t + 1) * P], rhs=w0_t[:, k, :],
                                 start=False, stop=(k == KT - 1))
                    ins.then_inc(s_attn_out, 1)

            def ffn_hidden(b, f):
                m = P if f < FT - 1 else FR
                pe.wait_ge(s_ffn_hid, b * FT + f + 1)
                for w, bk, done in ((gw_sb, FFN_BANKS[f % 2][0], s_ffn_gate), (uw_sb, FFN_BANKS[f % 2][1], s_ffn_up)):
                    for k in range(KT):
                        ins = mm(bank[bk][0:m, :], lhsT=w[:, k, f * P:f * P + m], rhs=xn_t[:, k, :], start=(k == 0), stop=(k == KT - 1))
                    ins.then_inc(done, 1)

            def ffn_down(b):
                pe.wait_ge(s_ffn_hid, (b + 1) * FT + 2)
                for t in range(NT):
                    for f in range(FT):
                        m = P if f < FT - 1 else FR
                        ins = mm(out_tile(FFN_BANKS[1], t), lhsT=f_hid[0:m, f, t * P:(t + 1) * P], rhs=dw_sb[0:m, f, :],
                                 start=(f == 0), stop=(f == FT - 1))
                ins.then_inc(s_ffn_out, 1)

            def mamba_start(b):
                for t in range(NT):
                    for k in range(KT):
                        ins = mm(bank[2][:, t * MH:(t + 1) * MH], lhsT=xn_t[:, k, t * P:(t + 1) * P], rhs=wdt_sb[:, k, :],
                                 start=(k == 0), stop=(k == KT - 1))
                ins.then_inc(s_dt_done, 1)
                for i in range(2):
                    for k in range(KT):
                        ins = mm(bank[i][:], lhsT=wbc_sb[:, k, i * P:(i + 1) * P], rhs=xn_t[:, k, :], start=(k == 0), stop=(k == KT - 1))
                    ins.then_inc(s_bc_done, 1)
                ffn_hidden(b, 0)
                pe.wait_ge(s_da_ready, b + 1)
                for i, (a, c) in enumerate(FEEDS):
                    o = bank[2][:, i * MH:(i + 1) * MH]
                    ins = mm(o, lhsT=after[:], rhs=da[:, a, 0, :], start=True, stop=(c == a + 1))
                    for m in range(a + 1, c):
                        ins = mm(o, lhsT=ones[:], rhs=da[:, m, 0, :], start=False, stop=(m == c - 1))
                ins.then_inc(s_dec_done, 1)
                for t in range(NT):
                    ins = mm(bank[6][:, t * P:(t + 1) * P], lhsT=da[:, t, :, :].rearrange("p a h -> p (a h)"), rhs=upto[:],
                             start=True, stop=True)
                ins.then_inc(s_cum_done, 1)
                ffn_hidden(b, 1)
                pe.wait_ge(s_conv_silu, b * (NPAIR + 2) + 3)
                for t in range(NT):
                    ins = pe.transpose(bank[0][:, t * P:(t + 1) * P], b_t[:, t * P:(t + 1) * P], ident[:])
                ins.then_inc(s_b_turned, 1)
                for t in range(NT):
                    ins = mm(bank[1][:, t * P:(t + 1) * P], lhsT=b_t[:, t * P:(t + 1) * P], rhs=c_t[:, t * P:(t + 1) * P],
                             start=True, stop=True)
                ins.then_inc(s_cb_done, 1)
                pe.wait_ge(s_cum_ev, b + 1)
                pe.wait_ge(s_cum_split, b + 1)
                for t in range(NT):
                    ins = pe.transpose(bank[6][:, t * P:(t + 1) * P], cum[:, t * P:(t + 1) * P], ident[:])
                ins.then_inc(s_cum_turned, 1)
                ffn_hidden(b, 2)
                pe.wait_ge(s_xn_lo, b * 2 + 2)
                pe.wait_ge(s_cb_ev, b + 1)
                project_x(b, 0, 0)
                ffn_hidden(b, 3)
                ffn_hidden(b, 4)
                ffn_hidden(b, 5)
                pe.wait_ge(s_b_ev, b + 1)
                project_gate(b, 0, 0)
                pe.wait_ge(s_dec_ready, b + 1)
                pe.wait_ge(s_cum_neg_ready, b + 1)
                pe.wait_ge(s_ffn_hid, b * FT + 7)
                spread_cum(b, 0, 0)
                ffn_down(b)
                mask_cum(b, 0)

            def project_x(b, n, par):
                N = b * NPAIR + n
                pe.wait_ge(s_w_ready, b * SLOTS + NH + n + 3)
                pe.wait_ge(s_taps_done, N + b * 2 + 2)
                project(bank[1][:], par, 1).then_inc(s_xc_done, 1)

            def project_gate(b, n, par):
                pe.wait_ge(s_gate_ready, b * NPAIR + n + 1)
                project(bank[0][:], par, 0).then_inc(s_w_used, 1)

            def spread_cum(b, n, par):
                N = b * NPAIR + n
                pe.wait_ge(s_pick_ready, N + 1)
                pe.wait_ge(s_mix_exp1, N + 1)
                for h in range(2):
                    ins = mm(bank[3 + h][:], lhsT=pick[:, par, h:h + 1].to_broadcast([P, P]), rhs=cum_r[:],
                             start=True, stop=True)
                ins.then_inc(s_cum_spread, 1)

            def mask_cum(b, n):
                pe.wait_ge(s_grow_ev, b * NPAIR + n + 1)
                for h, done in ((0, s_cum0_done), (1, s_cum1_done)):
                    mm(bank[3 + h][:].rearrange("p (t i) -> p t i", t=NT), lhsT=causal_bf[:],
                       rhs=ident_bf[:].unsqueeze(1).to_broadcast([P, NT, P]), start=False, stop=True,
                       skip_group_check=True).then_inc(done, 1)

            def turn_x(b, n, par):
                N = b * NPAIR + n
                pe.wait_ge(s_conv_silu, N + b * 2 + 4)
                pe.wait_ge(s_off_scaled, N + 1)
                for t in range(NT):
                    ins = pe.transpose(bank[2][:, t * P:(t + 1) * P], xs[:, par, t * P:(t + 1) * P], ident[:])
                ins.then_inc(s_x_turned, 1)

            def make_states(b, n, par):
                N = b * NPAIR + n
                pe.wait_ge(s_xw_ready, N + 1)
                for c in range(1, NT):
                    into = [i for i, f in enumerate(FEEDS) if f[1] == c]
                    for i in into:
                        ins = mm(bank[2][:, (c - 1) * P:c * P], lhsT=b_sb[:, FEEDS[i][0], :], rhs=x_w[:, i, :],
                                 start=(i == into[0]), stop=(i == into[-1]))
                ins.then_inc(s_state_done, 1)

            def off_block(b, n, par):
                N = b * NPAIR + n
                pe.wait_ge(s_state_ev, N + 2)
                for c in range(1, NT):
                    ins = mm(bank[2][:, (c - 1) * P:c * P], lhsT=state[:, c - 1, :], rhs=c_t[:, c * P:(c + 1) * P], start=True, stop=True)
                ins.then_inc(s_off_done, 1)

            def in_block(b, n, par):
                N = b * NPAIR + n
                pe.wait_ge(s_mix_ready, N + 1)
                pe.wait_ge(s_xdt_ready, N + 1)
                pe.wait_ge(s_y_ready, N + 1)
                for c in range(NT):
                    for h in range(2):
                        ins = mm(bank[5][h * HD:(h + 1) * HD, c * P:(c + 1) * P], lhsT=x_dt[:, par, c, h * HD:(h + 1) * HD],
                                 rhs=mix[:, par, h, c * P:(c + 1) * P], start=True, stop=True)
                ins.then_inc(s_diag_done, 1)

            def project_out(b, n, par, first, last):
                N = b * NPAIR + n
                pe.wait_ge(s_hid_split, N + 2)
                pe.wait_ge(s_out_ready, N + 3)
                for t in range(NT):
                    ins = mm3(out_tile((6, 7), t), lambda i: hid_r[:, par, i, t * P:(t + 1) * P], lambda i: wo_r[:, par, i, :],
                              first and t % 2 == 0, last, skip_group_check=True)
                ins.then_inc(s_projected, 1)

            with pe.Fori(0, NB) as b:
                pe.wait_ge(s_y_done, b + 1)
                turn_norm(b * 3, range(NT)).then_inc(s_ln_turned, 1)
                pe.wait_ge(s_ln_xnt, b * 2 + 1)
                pe.wait_ge(s_xnt_half, b * 2 + 1)
                pe.wait_ge(s_xn_lo, b * 2 + 1)
                project_qk(b, 0, 0)
                project_v(b, 0, 0)
                score(b, 0, 0)

                def head(h, par, more):
                    if more:
                        project_qk(b, h + 1, 1 - par)
                    turn_probs(b, h, par)
                    if more:
                        project_v(b, h + 1, 1 - par)
                        score(b, h + 1, 1 - par)
                    weigh_values(b, h, par)

                with pe.Fori(0, NH // 2 - 1) as i:
                    for par in range(2):
                        head(i * 2 + par, par, True)
                head(NH - 2, 0, True)
                head(NH - 1, 1, False)
                attention_out(b)

                turn_norm(b * 3 + 1, range(NT - 1))
                turn_norm(b * 3 + 2, (NT - 1,)).then_inc(s_ln_turned, 1)
                pe.wait_ge(s_ln_xnt, b * 2 + 2)
                pe.wait_ge(s_xnt_half, b * 2 + 2)
                mamba_start(b)
                pe.wait_ge(s_res_ready, b + 1)

                def pair(n, par, more, first=False, second=False):
                    turn_x(b, n, par)
                    if more:
                        project_x(b, n + 1, 1 - par)
                        project_gate(b, n + 1, 1 - par)
                        spread_cum(b, n + 1, 1 - par)
                    make_states(b, n, par)
                    if more:
                        mask_cum(b, n + 1)
                    in_block(b, n, par)
                    off_block(b, n, par)
                    if not first:
                        project_out(b, n - 1, 1 - par, second, False)

                pair(0, 0, True, first=True)
                pair(1, 1, True, second=True)
                with pe.Fori(1, NPAIR // 2 - 1) as i:
                    for par in range(2):
                        pair(i * 2 + par, par, True)
                pair(NPAIR - 2, 0, True)
                pair(NPAIR - 1, 1, False)
                project_out(b, NPAIR - 1, 1, False, True)
                pe.wait_ge(s_summed, (b + 1) * (NPAIR + 1))
                for t in range(NT):
                    ins = mm(bank[4][:, t:t + 1], lhsT=sumsq[:, t * P:(t + 1) * P], rhs=ones[:, 0:1], start=True, stop=True)
                ins.then_inc(s_ss_done, 1)

        @block.scalar
        def _(act):
            for free, n in ACT_CREDITS:
                act.sem_inc(free, n)
            A = act.activation
            act.wait_ge(s_loads, 16 * N_LOADS)
            A(exp_a[:], exp_a[:], ACT.Exp).then_inc(s_setup_act, 1)

            def copy_out(dst, src, done):
                A(dst, src, ACT.Copy).then_inc(done, 1)

            def high_out(dst, src, ready, count, done):
                act.wait_ge(ready, count)
                A(dst, src, ACT.Copy).then_inc(done, 1)

            def qk_high(b, h):
                N = b * NH + h
                high_out(q_r[:, 0, :], bank[0][:], s_q_done, N + 1, s_q_hi)
                high_out(k_r[:, 0, :], bank[1][:], s_k_done, N + 1, s_k_hi)

            def v_high(b, h, par):
                high_out(v_r[:, par, 0, :, :].rearrange("p t e -> p (t e)"), bank[0][:], s_w_used, b * SLOTS + h + 3, s_v_hi)

            def w_high(slot, par, width):
                act.wait_ge(w_in[par], (slot - par + 2) * 8)
                act.wait_ge(s_w_used, slot + 1)
                A(w_r_flat[par][0][:, 0:width], raw[:, par, 0:width], ACT.Copy).then_inc(s_w_hi, 1)

            def exps(b, h, par):
                N = b * NH + h
                act.wait_ge(s_bias_done, N + 1)
                for q, bk, at in ((3, 2, 0), (2, 3, 0), (0, 3, 384), (1, 4, 0)):
                    w = (q + 1) * P
                    ins = A(prob[:, par, P_AT[q]:P_AT[q] + w], bank[bk][:, at:at + w], ACT.Exp,
                            bias=bias[:, par, q:q + 1], scale=SCALE, accum_out=total[:, par, q:q + 1])
                ins.then_inc(s_exp_done, 1)

            def probs_high(b, h):
                N = b * NH + h
                act.wait_ge(s_z_done, N + 1)
                high_out(prob_r[:, 0, 0:512], bank[5][:], s_turned_a, N + 1, s_pt_a_hi)
                high_out(prob_r[:, 0, 512:1024], bank[6][:], s_turned_b, N + 1, s_pt_b_hi)
                high_out(prob_r[:, 0, 1024:NP], bank[7][:, 0:256], s_turned_c, N + 1, s_pt_c_hi)

            def xn_high(k):
                act.wait_ge(s_ln_xnt, k + 1)
                act.wait_ge(s_xnt_half, k + 1)
                A(xn_r[:, 0, :, :], xn_t[:], ACT.Copy).then_inc(s_xn_hi, 1)

            def out_high(b, n, par):
                N = b * NPAIR + n
                act.wait_ge(out_in[par], (N - par + 2) * 8)
                act.wait_ge(s_projected, N + 1)
                A(wo_r[:, par, 0, :], raw_out[:, par, :], ACT.Copy, scale=norm_sb[:, bass.ds(n, 1)]).then_inc(s_out_hi, 1)

            def hid_high(b, n, par):
                N = b * NPAIR + n
                act.wait_ge(s_hid_ready, N + 2)
                act.wait_ge(s_projected, N + 1)
                A(hid_r[:, par, 0, :], hid, ACT.Copy).then_inc(s_hid_hi, 1)
                act.wait_ge(s_summed, N + b + 1)
                A(square, hid, ACT.Square).then_inc(s_squared, 1)

            def gate_tanh(b, n, par):
                N = b * NPAIR + n
                act.wait_ge(s_w_used, b * SLOTS + NH + n + 3)
                act.wait_ge(s_gate_ready, N + 1)
                A(gate_th[:], bank[0][:], ACT.Tanh, scale=0.5).then_inc(s_gate_tanh, 1)

            def tap_now(k, ch, src):
                act.wait_ge(s_conv_silu, k + 1)
                A(conv_acc[:], src, ACT.Identity, bias=conv_sb[:, ch, TAPS:TAPS + 1],
                  scale=conv_sb[:, ch, TAPS - 1:TAPS]).then_inc(s_tap0, 1)

            def conv_tanh(k):
                act.wait_ge(s_taps_done, k + 1)
                A(conv_th[:], conv_acc[:], ACT.Tanh).then_inc(s_conv_tanh, 1)

            def pair_conv_start(b, n):
                act.wait_ge(s_xc_done, b * NPAIR + n + 1)
                tap_now(b * (NPAIR + 2) + 2 + n, n if isinstance(n, int) else bass.ds(n, 1), bank[1][:])

            def ffn_tanh(b, f):
                m = P if f < FT - 1 else FR
                act.wait_ge(s_ffn_gate, b * FT + f + 1)
                act.wait_ge(s_ffn_silu, b * FT + f + 1)
                A(f_th[0:m, f % 2, :], bank[FFN_BANKS[f % 2][0]][0:m, :], ACT.Tanh, scale=gs_sb[0:m, f:f + 1]).then_inc(s_ffn_tanh, 1)

            act.wait_ge(s_setup_dve, 6)

            with act.Fori(0, NB) as b:
                act.wait_ge(s_ln_turned, b * 2 + 1)
                copy_out(xn_t[:, 0, :], bank[0][:], s_xnt_half)
                xn_high(b * 2)
                w_high(b * SLOTS, 0, 3 * D)
                w_high(b * SLOTS + 1, 1, 3 * D)
                qk_high(b, 0)
                v_high(b, 0, 0)
                exps(b, 0, 0)

                def head(h, par, more, ahead):
                    if more:
                        qk_high(b, h + 1)
                    probs_high(b, h)
                    if more:
                        v_high(b, h + 1, 1 - par)
                        if ahead:
                            w_high(b * SLOTS + h + 2, par, 3 * D)
                        exps(b, h + 1, 1 - par)

                with act.Fori(0, NH // 2 - 1) as i:
                    for par in range(2):
                        head(i * 2 + par, par, True, True)
                head(NH - 2, 0, True, False)
                head(NH - 1, 1, False, False)

                act.wait_ge(s_ln_turned, b * 2 + 2)
                copy_out(xn_t[:, 0, :], bank[0][:], s_xnt_half)
                K = b * (NPAIR + 2)
                act.wait_ge(s_dt_absed, b + 1)
                A(dt_sb[:], dt_tmp[:], ACT.Exp, scale=-1.0).then_inc(s_dt_exp, 1)
                act.wait_ge(s_bc_done, b * 2 + 1)
                tap_now(K, NPAIR, bank[0][:])
                act.wait_ge(s_dt_exp, b + 1)
                A(dt_tmp[:], dt_sb[:], ACT.Ln, bias=1.0).then_inc(s_dt_ln, 1)
                conv_tanh(K)
                ffn_tanh(b, 0)
                act.wait_ge(s_bc_done, b * 2 + 2)
                tap_now(K + 1, NPAIR + 1, bank[1][:])
                xn_high(b * 2 + 1)
                conv_tanh(K + 1)
                act.wait_ge(s_dec_done, b + 1)
                A(dec[:].rearrange("p f h -> p (f h)"), bank[2][:, 0:len(FEEDS) * MH], ACT.Exp).then_inc(s_dec_ready, 1)
                act.wait_ge(s_cum_done, b + 1)
                copy_out(cum_r[:], bank[6][:], s_cum_hi)
                ffn_tanh(b, 1)
                w_high(b * SLOTS + NH, 0, 2 * D)
                w_high(b * SLOTS + NH + 1, 1, 2 * D)
                act.wait_ge(s_b_turned, b + 1)
                copy_out(b_sb[:].rearrange("p t n -> p (t n)"), bank[0][:], s_b_ev)
                ffn_tanh(b, 2)
                pair_conv_start(b, 0)
                conv_tanh(K + 2)
                ffn_tanh(b, 3)
                ffn_tanh(b, 4)
                ffn_tanh(b, 5)
                gate_tanh(b, 0, 0)
                def decays(n, par):
                    N = b * NPAIR + n
                    act.wait_ge(s_cum_spread, N + 1)
                    for h in range(2):
                        ins = A(grow[h * HD:(h + 1) * HD, par, 0:W - P], bank[3 + h][h * HD:(h + 1) * HD, P:W], ACT.Exp)
                    ins.then_inc(s_grow_ev, 1)

                def mixes(n, par, h):
                    act.wait_ge((s_cum0_done, s_cum1_done)[h], b * NPAIR + n + 1)
                    for c in range(NT):
                        ins = A(mix[:, par, h, c * P:(c + 1) * P], bank[3 + h][:, c * P:(c + 1) * P], ACT.Exp,
                                bias=cum_neg[:, c, bass.ds(n * 2 + h, 1)])
                    ins.then_inc((s_mix_exp0, s_mix_exp1)[h], 1)

                decays(0, 0)
                mixes(0, 0, 0)
                mixes(0, 0, 1)

                def pair(n, par, more, ahead, first=False):
                    N = b * NPAIR + n
                    out_high(b, n, par)
                    if ahead:
                        w_high(b * SLOTS + NH + n + 2, par, 2 * D)
                    if more:
                        pair_conv_start(b, n + 1)
                        gate_tanh(b, n + 1, 1 - par)
                        decays(n + 1, 1 - par)
                    if not first:
                        hid_high(b, n - 1, 1 - par)
                    act.wait_ge(s_state_done, N + 2)
                    act.wait_ge(s_off_done, N + 1)
                    copy_out(state[:].rearrange("p c q -> p (c q)"), bank[2][:, 0:W - P], s_state_ev)
                    if more:
                        mixes(n + 1, 1 - par, 0)
                        conv_tanh(K + n + 3)
                        mixes(n + 1, 1 - par, 1)

                pair(0, 0, True, True, first=True)
                pair(1, 1, True, True)
                with act.Fori(1, NPAIR // 2 - 1) as i:
                    for par in range(2):
                        pair(i * 2 + par, par, True, True)
                pair(NPAIR - 2, 0, True, False)
                pair(NPAIR - 1, 1, False, False)
                hid_high(b, NPAIR - 1, 1)
        @block.vector
        def _(dve):
            for free, n in DVE_CREDITS:
                dve.sem_inc(free, n)
            stt = dve.scalar_tensor_tensor
            tt = dve.tensor_tensor
            ts = dve.tensor_scalar
            dve.wait_ge(s_loads, 16 * N_LOADS)
            dve.tensor_reduce(w0_abs[:], w0_sb[:], AX_X, ALU.add, apply_absolute_value=True).then_inc(s_setup_dve, 1)
            ts(w0_sign[:], w0_sb[:], 0.0, 2.0, ALU.is_ge, ALU.mult).then_inc(s_setup_dve, 1)
            dve.wait_ge(s_setup_dve, 2)
            ts(w0_sign[:], w0_sign[:], -1.0, 1.0 / D, ALU.add, ALU.mult).then_inc(s_setup_sign, 1)
            dve.wait_ge(s_setup_sign, 1)
            for o in range(KT):
                ins = stt(out=w0_t[:, o, :], in0=w0_sign[:, o, :], scalar=w0_abs[:, o:o + 1], in1=w0_sb[:, o, :], op0=ALU.mult, op1=ALU.subtract)
            ins.then_inc(s_setup_sign, 1)
            dve.wait_ge(s_setup_sign, 2)
            tt(w0_sb[:], w0_t[:], w0_sb[:], ALU.add).then_inc(s_setup_dve, 1)
            dve.wait_ge(s_setup_pe, 1)
            dve.tensor_copy(w0_t[:].rearrange("p k d -> p (k d)"), bank[0][:]).then_inc(s_setup_dve, 1)
            ts(conv_sb[:], conv_sb[:], 0.5, None, ALU.mult)
            ts(gs_sb[:], gs_sb[:], 0.5, None, ALU.mult).then_inc(s_setup_dve, 1)
            dve.wait_ge(s_setup_dve, 5)
            tt(us_sb[:], us_sb[:], gs_sb[:], ALU.mult)
            tt(dw_sb[:, 0:FT - 1, :], dw_sb[:, 0:FT - 1, :], ds_bc[:].unsqueeze(1).to_broadcast([P, FT - 1, D]), ALU.mult)
            tt(dw_sb[0:FR, FT - 1, :], dw_sb[0:FR, FT - 1, :], ds_bc[0:FR, :], ALU.mult).then_inc(s_setup_dve, 1)
            dve.wait_ge(s_setup_dve, 6)

            def low_of(dst, src, high, ready, count, done):
                dve.wait_ge(ready, count)
                tt(dst, src, high.bitcast(F32), ALU.subtract).then_inc(done, 1)

            def ln_stats(g, src, tiles):
                for t in tiles:
                    ins = dve.bn_stats(stats[:, t, :], src[:, t, :])
                ins.then_inc(s_ln_stats, 1)
                dve.wait_ge(s_ln_stats, g * 2 + 1)
                dve.memset(spacer[:], 0.0)
                for t in tiles:
                    ins = dve.bn_aggr(meanvar[:, t, :], stats[:, t, :])
                ins.then_inc(s_ln_stats, 1)
                dve.wait_ge(s_ln_stats, g * 2 + 2)
                ts(var_eps[:, tiles[0]:tiles[-1] + 1], meanvar[:, tiles[0]:tiles[-1] + 1, 1:2].rearrange("p t o -> p (t o)"),
                   EPS, None, ALU.add).then_inc(s_ln_var, 1)

            def ln_apply(g, src, tiles):
                dve.wait_ge(s_ln_rstd, g + 1)
                for t in tiles:
                    ins = ts(xn[:, t, :], src[:, t, :], meanvar[:, t, 0:1], rstd[:, t:t + 1], ALU.subtract, ALU.mult)
                ins.then_inc(s_ln_xn, 1)

            def ln_out(k):
                dve.wait_ge(s_ln_turned, k + 1)
                dve.tensor_copy(xn_t[:, 1, :], bank[1][:]).then_inc(s_ln_xnt, 1)

            def qk_low(b, h):
                N = b * NH + h
                low_of(q_r[:, 1, :], bank[0][:], q_r[:, 0, :], s_q_hi, N + 1, s_q_ev)
                low_of(k_r[:, 1, :], bank[1][:], k_r[:, 0, :], s_k_hi, N + 1, s_k_ev)

            def v_low(b, h, par):
                low_of(v_r[:, par, 1, :, :].rearrange("p t e -> p (t e)"), bank[0][:],
                       v_r[:, par, 0, :, :].rearrange("p t e -> p (t e)"), s_v_hi, b * NH + h + 1, s_v_ev)

            def probs_low(b, h):
                N = b * NH + h
                for lo, up, bk, ready, done in ((0, 512, 5, s_pt_a_hi, s_pt_a), (512, 1024, 6, s_pt_b_hi, s_pt_b), (1024, NP, 7, s_pt_c_hi, s_pt_c)):
                    low_of(prob_r[:, 1, lo:up], bank[bk][:, 0:up - lo], prob_r[:, 0, lo:up], ready, N + 1, done)

            def maxima(b, h, par):
                N = b * NH + h
                for j, (q, bk, at) in enumerate(((3, 2, 0), (2, 3, 0), (0, 3, 384), (1, 4, 0))):
                    w = (q + 1) * P
                    dve.wait_ge(s_scores_done, N * NT + (j + 1 if bk != 3 else 3))
                    ins = dve.tensor_reduce(neg_max[:, par, q:q + 1], bank[bk][:, at:at + w], AX_X, ALU.max, negate=True)
                ins.then_inc(s_max_done, 1)
                dve.wait_ge(s_max_done, N + 1)
                ts(bias[:, par, :], neg_max[:, par, :], SCALE, None, ALU.mult).then_inc(s_bias_done, 1)

            def normalise(b, h, par):
                N = b * NH + h
                dve.wait_ge(s_exp_done, N + 2)
                dve.reciprocal(inv_total[:, par, :], total[:, par, :]).then_inc(s_inv_done, 1)
                dve.wait_ge(s_inv_done, N + 1)
                for q in range(NT):
                    pr = prob[:, par, P_AT[q]:P_AT[q] + (q + 1) * P]
                    ins = ts(pr, pr, inv_total[:, par, q:q + 1], None, ALU.mult)
                ins.then_inc(s_norm_done, 1)

            def pair_gate(b, n, par):
                N = b * NPAIR + n
                dve.wait_ge(s_gate_tanh, N + 1)
                stt(out=gate[:, par, :], in0=gate_th[:], scalar=1.0, in1=bank[0][:], op0=ALU.add, op1=ALU.mult).then_inc(s_gate_ready, 1)

            def conv_tap(k, ch, src, back):
                dve.wait_ge((s_tap0, s_tap1, s_tap2)[back - 1], k + 1)
                stt(out=conv_acc[:, back:W], in0=src[:, 0:W - back], scalar=conv_sb[:, ch, TAPS - 1 - back:TAPS - back],
                    in1=conv_acc[:, back:W], op0=ALU.mult, op1=ALU.add).then_inc((s_tap1, s_tap2, s_taps_done)[back - 1], 1)

            def conv_taps(k, ch, src):
                for back in range(1, TAPS):
                    conv_tap(k, ch, src, back)

            def conv_end(k, dst):
                dve.wait_ge(s_conv_tanh, k + 1)
                stt(out=dst, in0=conv_th[:], scalar=1.0, in1=conv_acc[:], op0=ALU.add, op1=ALU.mult).then_inc(s_conv_silu, 1)

            def ffn_hid(b, f):
                m = P if f < FT - 1 else FR
                o, u = FFN_BANKS[f % 2]
                N = b * FT + f
                dve.wait_ge(s_ffn_tanh, N + 1)
                dve.wait_ge(s_ffn_hid, N + 1)
                stt(out=f_silu[0:m, f % 2, :], in0=f_th[0:m, f % 2, :], scalar=1.0, in1=bank[o][0:m, :], op0=ALU.add, op1=ALU.mult).then_inc(s_ffn_silu, 1)
                dve.wait_ge(s_ffn_silu, N + 3)
                dve.wait_ge(s_ffn_up, N + 1)
                stt(out=f_hid[0:m, f, :], in0=bank[u][0:m, :], scalar=us_sb[0:m, f:f + 1], in1=f_silu[0:m, f % 2, :], op0=ALU.mult, op1=ALU.mult).then_inc(s_ffn_hid, 1)

            def wide(t):
                return t[:].rearrange("p t h -> p (t h)")

            with dve.Fori(0, NB) as b:
                dve.wait_ge(s_x_in, (b + 1) * 16)
                ln_stats(b * 3, x_sb, range(NT))
                ln_apply(b * 3, x_sb, range(NT))
                ln_out(b * 2)
                low_of(xn_r[:, 1, :, :], xn_t[:], xn_r[:, 0, :, :], s_xn_hi, b * 2 + 1, s_xn_lo)
                qk_low(b, 0)
                v_low(b, 0, 0)
                maxima(b, 0, 0)
                normalise(b, 0, 0)

                def head(h, par, more):
                    N = b * NH + h
                    if more:
                        qk_low(b, h + 1)
                    probs_low(b, h)
                    if more:
                        v_low(b, h + 1, 1 - par)
                        maxima(b, h + 1, 1 - par)
                    dve.wait_ge(s_z_done, N + 2)
                    dst = z_t[:, h, :] if isinstance(h, int) else z_t[:, bass.ds(h, 1), :].rearrange("p h w -> p (h w)")
                    dve.tensor_copy(dst, bank[7][:]).then_inc(s_z_ev, 1)
                    if more:
                        normalise(b, h + 1, 1 - par)

                with dve.Fori(0, NH // 2 - 1) as i:
                    for par in range(2):
                        head(i * 2 + par, par, True)
                head(NH - 2, 0, True)
                head(NH - 1, 1, False)

                dve.wait_ge(s_x_bias, b + 1)
                dve.wait_ge(s_stored, b * 16 + 16)
                for t in range(NT):
                    dve.wait_ge(s_attn_out, b * NT + t + 1)
                    tt(x2[:, t, :], bank[t][:, 0:D], x_sb[:, t, :], ALU.add).then_inc(s_x2_done, 1)
                    if t == NT - 2:
                        dve.wait_ge(s_x2_done, b * NT + t + 2)
                        ln_stats(b * 3 + 1, x2, range(NT - 1))
                        ln_apply(b * 3 + 1, x2, range(NT - 1))
                dve.wait_ge(s_x2_done, (b + 1) * NT + 1)
                ln_stats(b * 3 + 2, x2, (NT - 1,))
                ln_apply(b * 3 + 2, x2, (NT - 1,))
                ln_out(b * 2 + 1)
                K = b * (NPAIR + 2)
                dve.wait_ge(s_dt_done, b + 1)
                tt(dt_raw[:], bank[2][:, 0:NT * MH].rearrange("p (t h) -> p t h", t=NT),
                   dtb_bc[:].unsqueeze(1).to_broadcast([P, NT, MH]), ALU.add).then_inc(s_dt_biased, 1)
                dve.wait_ge(s_dt_biased, b + 1)
                stt(out=wide(dt_tmp), in0=wide(dt_raw), scalar=-1.0, in1=wide(dt_raw), op0=ALU.mult, op1=ALU.max).then_inc(s_dt_absed, 1)
                conv_taps(K, NPAIR, bank[0])
                dve.wait_ge(s_dt_ln, b + 1)
                stt(out=wide(dt_sb), in0=wide(dt_raw), scalar=0.0, in1=wide(dt_tmp), op0=ALU.max, op1=ALU.add).then_inc(s_dt_ready, 1)
                dve.wait_ge(s_dt_ready, b + 1)
                for i in range(2):
                    ins = stt(out=da[:, :, i, :], in0=dt_sb[:], scalar=-1.0, in1=exp_a[:].unsqueeze(1).to_broadcast([P, NT, MH]),
                              op0=ALU.mult, op1=ALU.mult)
                ins.then_inc(s_da_ready, 1)
                conv_end(K, b_t[:])
                ffn_hid(b, 0)
                conv_taps(K + 1, NPAIR + 1, bank[1])
                conv_end(K + 1, c_t[:])
                dve.wait_ge(s_cum_hi, b + 1)
                dve.tensor_copy(cum, bank[6][:]).then_inc(s_cum_ev, 1)
                low_of(cum_r[MH:P, :], bank[6][MH:P, :], cum_r[MH:P, :], s_cum_hi, b + 1, s_cum_split)
                ffn_hid(b, 1)
                dve.wait_ge(s_cb_done, b + 1)
                dve.tensor_copy(cb[:].rearrange("p t i -> p (t i)"), bank[1][:]).then_inc(s_cb_ev, 1)
                dve.wait_ge(s_cum_turned, b + 1)
                ts(cum_neg[:], bank[6][:].rearrange("p (t h) -> p t h", t=NT)[:, :, 0:MH], -1.0, None, ALU.mult).then_inc(s_cum_neg_ready, 1)
                ffn_hid(b, 2)
                conv_taps(K + 2, 0, bank[1])
                conv_end(K + 2, xs[:, 0, :])
                for f in range(3, FT):
                    ffn_hid(b, f)
                pair_gate(b, 0, 0)
                dve.wait_ge(s_ffn_out, b + 1)
                for i in range(2):
                    part = x2[:, 2 * i:2 * i + 2, :].rearrange("p t d -> p (t d)")
                    ins = tt(part, bank[FFN_BANKS[1][i]][:], part, ALU.add)
                ins.then_inc(s_res_ready, 1)

                def out_low(n, par):
                    dve.wait_ge(s_out_hi, b * NPAIR + n + 1)
                    stt(out=wo_r[:, par, 1, :], in0=raw_out[:, par, :], scalar=norm_sb[:, bass.ds(n, 1)],
                        in1=wo_r[:, par, 0, :].bitcast(F32), op0=ALU.mult, op1=ALU.subtract).then_inc(s_out_ready, 1)

                def mixed(n, par, h):
                    return tt(mix[:, par, h, :], mix[:, par, h, :], cb[:].rearrange("p t i -> p (t i)"), ALU.mult)

                def tail(n, par):
                    N = b * NPAIR + n

                    def off():
                        dve.wait_ge(s_off_done, N + 2)
                        dve.wait_ge(s_grow_ev, N + 1)
                        tt(y_in[:, P:W], bank[2][:, 0:W - P], grow[:, par, 0:W - P], ALU.mult).then_inc(s_off_scaled, 1)

                    def skip():
                        dve.wait_ge(s_off_scaled, N + 2)
                        stt(out=y, in0=xs[:, par, :], scalar=d_sb[:, n:n + 1] if isinstance(n, int) else d_sb[:, bass.ds(n, 1)],
                            in1=y_in[:], op0=ALU.mult, op1=ALU.add).then_inc(s_skip_done, 1)

                    def total_y():
                        dve.wait_ge(s_diag_done, N + 1)
                        dve.wait_ge(s_skip_done, N + 1)
                        tt(y, bank[5][:], y, ALU.add).then_inc(s_y_ready, 1)

                    def gated():
                        dve.wait_ge(s_y_ready, N + 2)
                        dve.wait_ge(s_squared, N + 1)
                        dve.wait_ge(s_hid_split, N + 1)
                        tt(hid, y, gate[:, par, :], ALU.mult).then_inc(s_hid_ready, 1)

                    return off, skip, total_y, gated

                def pair(n, par, more, first=False):
                    N = b * NPAIR + n
                    ch = n + 1 if isinstance(n, int) else bass.ds(n + 1, 1)
                    if not first:
                        off, skip, total_y, gated = tail(n - 1, 1 - par)
                        off()
                        skip()
                    dve.wait_ge(s_conv_silu, K + n + 4)
                    dve.wait_ge(s_x_turned, N + 1)
                    tt(x_dt[:, par, :, :].rearrange("p t (h q) -> p t h q", h=2),
                       bank[2][:].rearrange("p (t h q) -> p t h q", t=NT, h=2),
                       dt_sb[:, :, bass.ds(n * 2, 2)].unsqueeze(3).to_broadcast([P, NT, 2, HD]), ALU.mult).then_inc(s_xdt_ready, 1)
                    if not first:
                        total_y()
                    dve.wait_ge(s_mix_exp0, N + 1)
                    mixed(n, par, 0)
                    if not first:
                        gated()
                    if more:
                        conv_tap(K + n + 3, ch, bank[1], 1)
                    dve.wait_ge(s_mix_exp1, N + 2)
                    mixed(n, par, 1).then_inc(s_mix_ready, 1)
                    if more:
                        conv_tap(K + n + 3, ch, bank[1], 2)
                        if not first:
                            dve.wait_ge(s_hid_ready, N + 1)
                        pair_gate(b, n + 1, 1 - par)
                        conv_tap(K + n + 3, ch, bank[1], 3)
                    out_low(n, par)
                    if more:
                        conv_end(K + n + 3, xs[:, 1 - par, :])

                pair(0, 0, True, first=True)
                pair(1, 1, True)
                with dve.Fori(1, NPAIR // 2 - 1) as i:
                    for par in range(2):
                        pair(i * 2 + par, par, True)
                pair(NPAIR - 2, 0, True)
                pair(NPAIR - 1, 1, False)
                for step in tail(NPAIR - 1, 1):
                    step()
                dve.wait_ge(s_ss_done, b + 2)
                ts(ms_eps[:], bank[4][:, 0:NT], 1.0 / (NPAIR * P), 4 * EPS, ALU.mult, ALU.add).then_inc(s_ms_ready, 1)
                dve.wait_ge(s_res_ready, b + 1)
                dve.wait_ge(s_rms_ready, b + 1)
                dve.wait_ge(s_projected, (b + 1) * NPAIR + 2)
                for t in range(NT):
                    ins = stt(out=x2[:, t, :], in0=bank[6 + t // 2][:, (t % 2) * D:(t % 2 + 1) * D], scalar=rms[:, t:t + 1],
                              in1=x2[:, t, :], op0=ALU.mult, op1=ALU.add)
                ins.then_inc(s_y_done, 1)


def kernel(**inputs):
    import numpy as np
    import concourse.bacc as bacc
    from concourse.bass_utils import run_bass_kernel_spmd as run

    a = {k: np.asarray(v) for k, v in inputs.items()}

    def tiles(w_t):
        return w_t.reshape(-1, P, w_t.shape[1]).transpose(1, 0, 2)

    NH, DH, D = a["L0_attn_W_Q"].shape
    qkv = np.stack([a[f"L0_attn_W_{c}"] for c in "QKV"])
    qkv = qkv.reshape(3, NH, DH, D // P, P).transpose(1, 4, 0, 3, 2)
    w_in = a["L1_attn_in_proj_w"]
    inner = a["L1_attn_norm_w"].shape[0]
    pairs = inner // P
    both = np.stack([w_in[:, 0:inner], w_in[:, inner:2 * inner]])
    both = both.reshape(2, D // P, P, pairs, P).transpose(3, 2, 0, 1, 4)
    conv = np.concatenate([a["L1_attn_conv_w"], a["L1_attn_conv_b"][:, None]], axis=1)
    F = a["L1_ffn_gate_w"].shape[0]
    ft = -(-F // P)

    def column(v):
        c = np.zeros((ft * P,), v.dtype)
        c[:F] = v
        return c.reshape(ft, P).T

    per_head = inner // a["L1_attn_D_param"].shape[0]
    arrays = {
        "x": a["L0_attn_x"],
        "wqkv": qkv.reshape(NH, P, -1),
        "wo_t": a["L0_attn_W_O"].T.reshape(NH, DH, D).transpose(1, 0, 2),
        "w0": tiles(a["L0_ffn_weight"]),
        "b0": a["L0_ffn_bias"],
        "w_pair": both.reshape(pairs, P, -1),
        "w_out": a["L1_attn_out_proj_w"].reshape(pairs, P, -1),
        "w_bc": tiles(w_in[:, 2 * inner:2 * inner + 2 * P]),
        "w_dt": tiles(w_in[:, 2 * inner + 2 * P:]),
        "conv_par": conv.reshape(pairs + 2, P, -1).transpose(1, 0, 2),
        "dt_bias": a["L1_attn_dt_bias"],
        "a_log": a["L1_attn_A_log"],
        "d_col": np.repeat(a["L1_attn_D_param"], per_head).reshape(pairs, P).T,
        "norm_col": a["L1_attn_norm_w"].reshape(pairs, P).T,
        "gate_t": tiles(a["L1_ffn_gate_w"].T),
        "up_t": tiles(a["L1_ffn_up_w"].T),
        "down_t": a["L1_ffn_down_w"].T,
        "gate_s": column(a["L1_ffn_gate_s"]),
        "up_s": column(a["L1_ffn_up_s"]),
        "down_s": a["L1_ffn_down_s"],
    }
    nc = bacc.Bacc("TRN2", target_bir_lowering=False, num_devices=1)
    fed, aps = {}, {}
    for name, v in arrays.items():
        v = np.ascontiguousarray(v)
        fed[f"in_{name}"] = v
        aps[name] = nc.dram_tensor(f"in_{name}", v.shape, mybir.dt.from_np(v.dtype), kind="ExternalInput").ap()
    aps["out"] = nc.dram_tensor("out_0", arrays["x"].shape, F32, kind="ExternalOutput").ap()
    two_layers(nc, **aps)
    return run(nc, [fed], core_ids=[0]).results[0]["out_0"]
```

```python
from contextlib import ExitStack

import concourse.bass as bass
from concourse import mybir

F32 = mybir.dt.float32
BF16 = mybir.dt.bfloat16
F32R = mybir.dt.float32r
ALU = mybir.AluOpType
ACT = mybir.ActivationFunctionType
AX_X = mybir.AxisListType.X

P = 128
EPS = 1e-5
TAPS = 4


def two_layers(nc, x, wqkv, wo_t, w0, b0, w_pair, w_out, w_bc, w_dt, conv_par, dt_bias, a_log,
               d_col, norm_col, gate_t, up_t, down_t, gate_s, up_s, down_s, out):
    NB, S, D = x.shape
    NH = wqkv.shape[0]
    NT = S // P
    KT = D // P
    NPAIR = w_pair.shape[0]
    MH = dt_bias.shape[0]
    HD = P // 2
    F = gate_t.shape[2]
    FT = -(-F // P)
    FR = F - (FT - 1) * P
    SCALE = float(P) ** -0.5
    W = NT * P
    assert FT == 6 and 2 * MH == P and W == 512 and D == 256 and NH % 2 == 0 and NPAIR % 2 == 0 and NT == 4

    P_AT = {3: 0, 2: 512, 0: 896, 1: 1024}
    PT_AT = {0: 0, 1: 512, 3: 896, 2: 1024}
    NP = 1280
    with ExitStack() as ctx:
        def sb(name, shape, dt=F32):
            return ctx.enter_context(nc.sbuf_tensor(name, shape, dt))

        def sem(name):
            return ctx.enter_context(nc.semaphore(name))

        bank = [ctx.enter_context(nc.psum_tensor(f"bank{i}", [P, 512], F32)) for i in range(8)]

        ident = sb("ident", [P, P])
        ident_bf = sb("ident_bf", [P, P], BF16)
        causal_bf = sb("causal_bf", [P, P], BF16)
        upto = sb("upto", [P, P])
        after = sb("after", [P, P])
        ones = sb("ones", [P, P])
        minus_half = sb("minus_half", [P, NT])
        wo_sb = sb("wo_sb", [P, NH, D])
        w0_sb = sb("w0_sb", [P, KT, D])
        w0_abs = sb("w0_abs", [P, KT])
        w0_sign = sb("w0_sign", [P, KT, D])
        w0_t = sb("w0_t", [P, KT, D])
        b0_bc = sb("b0_bc", [P, D])
        wbc_sb = sb("wbc_sb", [P, KT, 2 * P])
        wdt_sb = sb("wdt_sb", [P, KT, MH])
        conv_sb = sb("conv_sb", [P, NPAIR + 2, TAPS + 1])
        dtb_bc = sb("dtb_bc", [P, MH])
        exp_a = sb("exp_a", [P, MH])
        d_sb = sb("d_sb", [P, NPAIR])
        norm_sb = sb("norm_sb", [P, NPAIR])
        gw_sb = sb("gw_sb", [P, KT, F])
        uw_sb = sb("uw_sb", [P, KT, F])
        dw_sb = sb("dw_sb", [P, FT, D])
        gs_sb = sb("gs_sb", [P, FT])
        us_sb = sb("us_sb", [P, FT])
        ds_bc = sb("ds_bc", [P, D])

        x_sb = sb("x_sb", [P, NT, D])
        xn = sb("xn", [P, NT, D])
        xn_t = sb("xn_t", [P, KT, W])
        spacer = sb("spacer", [P, 1])
        stats = sb("stats", [P, NT, 6])
        meanvar = sb("meanvar", [P, NT, 2])
        var_eps = sb("var_eps", [P, NT])
        rstd = sb("rstd", [P, NT])
        raw = sb("raw", [P, 2, 3 * KT * P])
        w_r = sb("w_r", [P, 2, 2, 3, KT, P], F32R)
        w_r_flat = [[w_r[:, a, i, :, :, :].rearrange("p m k e -> p (m k e)") for i in range(2)] for a in range(2)]
        raw_out = sb("raw_out", [P, 2, D])
        wo_r = sb("wo_r", [P, 2, 2, D], F32R)
        xn_r = sb("xn_r", [P, 2, KT, W], F32R)
        neg_max = sb("neg_max", [P, 2, NT])
        bias = sb("bias", [P, 2, NT])
        total = sb("total", [P, 2, NT])
        inv_total = sb("inv_total", [P, 2, NT])
        shared = sb("shared", [P, NH * W])
        z_t = shared[:].rearrange("p (h w) -> p h w", h=NH)
        n_mix, n_xw, n_ffn = 4 * NT * P, (NT - 1) * P, FT * W
        mix = shared[:, 0:n_mix].rearrange("p (a h w) -> p a h w", a=2, h=2)
        x_w = shared[:, n_mix:n_mix + n_xw].rearrange("p (c q) -> p c q", c=NT - 1)
        f_hid = shared[:, n_mix + n_xw:n_mix + n_xw + n_ffn].rearrange("p (f w) -> p f w", f=FT)
        f_at = n_mix + n_xw + n_ffn
        f_th = shared[:, f_at:f_at + 2 * W].rearrange("p (a w) -> p a w", a=2)
        f_silu = shared[:, f_at + 2 * W:f_at + 4 * W].rearrange("p (a w) -> p a w", a=2)
        x2 = sb("x2", [P, NT, D])

        place = sb("place", [P, 11 * W])
        prob = place[:, 0:2 * NP].rearrange("p (a n) -> p a n", a=2)
        xs = place[:, 0:2 * W].rearrange("p (a w) -> p a w", a=2)
        gate = place[:, 2 * W:4 * W].rearrange("p (a w) -> p a w", a=2)
        x_dt = place[:, 4 * W:6 * W].rearrange("p (a t q) -> p a t q", a=2, t=NT)
        hid, y, square = (place[:, i * W:(i + 1) * W] for i in (6, 9, 10))
        grow = place[:, 7 * W:9 * W].rearrange("p (a w) -> p a w", a=2)
        place_r = sb("place_r", [P, 8 * W + 2 * NP], F32R)
        q_r = place_r[:, 0:2 * W].rearrange("p (i w) -> p i w", i=2)
        k_r = place_r[:, 2 * W:4 * W].rearrange("p (i w) -> p i w", i=2)
        v_r = place_r[:, 4 * W:8 * W].rearrange("p (a i t e) -> p a i t e", a=2, i=2, t=NT)
        prob_r = place_r[:, 8 * W:8 * W + 2 * NP].rearrange("p (i n) -> p i n", i=2)
        hid_r = place_r[:, 8 * W:12 * W].rearrange("p (a i w) -> p a i w", a=2, i=2)

        conv_acc = sb("conv_acc", [P, W])
        conv_th = sb("conv_th", [P, W])
        gate_th = sb("gate_th", [P, W])
        b_t = sb("b_t", [P, W])
        c_t = sb("c_t", [P, W])
        b_sb = sb("b_sb", [P, NT, P])
        cb = sb("cb", [P, NT, P])
        dt_raw = sb("dt_raw", [P, NT, MH])
        dt_tmp = sb("dt_tmp", [P, NT, MH])
        dt_sb = sb("dt_sb", [P, NT, MH])
        da = sb("da", [P, NT, 2, MH])
        dec = sb("dec", [P, 2 * NT - 3, MH])
        cum = place[:, 9 * W:10 * W]
        cum_r = sb("cum_r", [2 * MH, W], F32R)
        pick = sb("pick", [P, 2, 2], F32R)
        cum_neg = sb("cum_neg", [P, NT, MH])
        state = sb("state", [P, NT - 1, P])
        carry = sb("carry", [P, P])
        y_in = sb("y_in", [P, W - P])
        sumsq = sb("sumsq", [P, W])
        ms_eps = sb("ms_eps", [P, NT])
        rms = sb("rms", [P, NT])

        s_loads = sem("loads")
        s_late = sem("late")
        s_consts = sem("consts")
        s_x_in = sem("x_in")
        s_stored = sem("stored")
        s_xnt_half = sem("xnt_half")
        s_setup_sign = sem("setup_sign")
        s_setup_act = sem("setup_act")
        s_setup_dve = sem("setup_dve")
        s_setup_pe = sem("setup_pe")
        s_ln_stats = sem("ln_stats")
        s_ln_var = sem("ln_var")
        s_ln_rstd = sem("ln_rstd")
        s_ln_xn = sem("ln_xn")
        s_ln_turned = sem("ln_turned")
        s_ln_xnt = sem("ln_xnt")
        s_x_bias = sem("x_bias")
        s_q_done = sem("q_done")
        s_v_done = sem("v_done")
        s_k_done = sem("k_done")
        s_q_ev = sem("q_ev")
        s_k_ev = sem("k_ev")
        s_v_ev = sem("v_ev")
        s_scores_done = sem("scores_done")
        s_max_done = sem("max_done")
        s_bias_done = sem("bias_done")
        s_exp_done = sem("exp_done")
        s_inv_done = sem("inv_done")
        s_norm_done = sem("norm_done")
        s_turned_a = sem("turned_a")
        s_turned_b = sem("turned_b")
        s_turned_c = sem("turned_c")
        s_pt_a = sem("pt_a")
        s_pt_b = sem("pt_b")
        s_pt_c = sem("pt_c")
        s_z_done = sem("z_done")
        s_z_ev = sem("z_ev")
        s_attn_out = sem("attn_out")
        s_x2_done = sem("x2_done")
        s_dt_done = sem("dt_done")
        s_dt_biased = sem("dt_biased")
        s_dt_absed = sem("dt_absed")
        s_dt_exp = sem("dt_exp")
        s_dt_ln = sem("dt_ln")
        s_dt_ready = sem("dt_ready")
        s_da_ready = sem("da_ready")
        s_bc_done = sem("bc_done")
        s_tap0 = sem("tap0")
        s_tap1 = sem("tap1")
        s_tap2 = sem("tap2")
        s_taps_done = sem("taps_done")
        s_conv_tanh = sem("conv_tanh")
        s_conv_silu = sem("conv_silu")
        s_b_turned = sem("b_turned")
        s_b_ev = sem("b_ev")
        s_cb_done = sem("cb_done")
        s_cb_ev = sem("cb_ev")
        s_dec_done = sem("dec_done")
        s_dec_ready = sem("dec_ready")
        s_xc_done = sem("xc_done")
        s_gate_tanh = sem("gate_tanh")
        s_gate_ready = sem("gate_ready")
        s_mix_exp0 = sem("mix_exp0")
        s_mix_exp1 = sem("mix_exp1")
        s_mix_ready = sem("mix_ready")
        s_carried = sem("carried")
        s_x_turned = sem("x_turned")
        s_xdt_ready = sem("xdt_ready")
        s_xw_ready = sem("xw_ready")
        s_state_done = sem("state_done")
        s_state_ev = sem("state_ev")
        s_grow_ev = sem("grow_ev")
        s_off_done = sem("off_done")
        s_off_scaled = sem("off_scaled")
        s_base_done = sem("base_done")
        s_diag_done = sem("diag_done")
        s_y_ready = sem("y_ready")
        s_hid_ready = sem("hid_ready")
        s_squared = sem("squared")
        s_summed = sem("summed")
        s_projected = sem("projected")
        s_ss_done = sem("ss_done")
        s_ms_ready = sem("ms_ready")
        s_rms_ready = sem("rms_ready")
        s_ffn_gate = sem("ffn_gate")
        s_ffn_up = sem("ffn_up")
        s_ffn_tanh = sem("ffn_tanh")
        s_ffn_silu = sem("ffn_silu")
        s_ffn_hid = sem("ffn_hid")
        s_ffn_out = sem("ffn_out")
        s_res_ready = sem("res_ready")
        s_y_done = sem("y_done")
        s_xn_hi = sem("xn_hi")
        s_xn_lo = sem("xn_lo")
        s_w_hi = sem("w_hi")
        s_w_ready = sem("w_ready")
        s_w_used = sem("w_used")
        s_out_hi = sem("out_hi")
        s_out_ready = sem("out_ready")
        s_q_hi = sem("q_hi")
        s_k_hi = sem("k_hi")
        s_v_hi = sem("v_hi")
        s_pt_a_hi = sem("pt_a_hi")
        s_pt_b_hi = sem("pt_b_hi")
        s_pt_c_hi = sem("pt_c_hi")
        s_cum_done = sem("cum_done")
        s_cum_ev = sem("cum_ev")
        s_cum_hi = sem("cum_hi")
        s_cum_split = sem("cum_split")
        s_cum_turned = sem("cum_turned")
        s_cum_neg_ready = sem("cum_neg_ready")
        s_pick_ready = sem("pick_ready")
        s_cum_spread = sem("cum_spread")
        s_cum0_done = sem("cum0_done")
        s_cum1_done = sem("cum1_done")
        s_hid_hi = sem("hid_hi")
        s_hid_split = sem("hid_split")
        s_w_in0 = sem("w_in0")
        s_w_in1 = sem("w_in1")
        s_out_in0 = sem("out_in0")
        s_out_in1 = sem("out_in1")
        w_in, out_in = (s_w_in0, s_w_in1), (s_out_in0, s_out_in1)

        PE_CREDITS = ((s_z_done, 1), (s_state_done, 1), (s_off_done, 1), (s_projected, 2), (s_ss_done, 1))
        ACT_CREDITS = ((s_exp_done, 1), (s_state_ev, 1), (s_mix_exp1, 1))
        DVE_CREDITS = ((s_k_ev, 1), (s_v_ev, 1), (s_pt_a, 1), (s_pt_b, 1), (s_z_ev, 1), (s_x2_done, 1), (s_gate_ready, 1),
                       (s_conv_silu, 1), (s_off_scaled, 1), (s_base_done, 1), (s_hid_ready, 1),
                       (s_ffn_silu, 2), (s_ffn_hid, 2), (s_y_done, 1), (s_out_ready, 2))
        POOL_CREDITS = ((s_hid_split, 1), (s_squared, 1), (s_w_ready, 2), (s_stored, 16))
        SLOTS = NH + NPAIR

        def v_half(bk):
            return bank[bk][:].rearrange("p (t a e) -> p a t e", t=NT // 2, a=2)

        block = ctx.enter_context(nc.Block())
        FFN_BANKS = ((3, 4), (5, 7))
        N_EARLY, N_LATE = 8, 9
        NCONST = 8

        @block.sync
        def _(sp):
            early = [
                (w0_sb[:], w0), (conv_sb[:], conv_par), (exp_a[:], a_log.unsqueeze(0).to_broadcast([P, MH])),
                (gs_sb[:], gate_s), (us_sb[:], up_s), (ds_bc[:], down_s.unsqueeze(0).to_broadcast([P, D])),
                (dw_sb[:, 0:FT - 1, :], down_t[0:(FT - 1) * P, :].rearrange("(f p) d -> p f d", p=P)),
                (dw_sb[0:FR, FT - 1, :], down_t[(FT - 1) * P:F, :]),
            ]
            late = [
                (b0_bc[:], b0.unsqueeze(0).to_broadcast([P, D])), (wo_sb[:], wo_t), (wbc_sb[:], w_bc), (wdt_sb[:], w_dt),
                (dtb_bc[:], dt_bias.unsqueeze(0).to_broadcast([P, MH])), (d_sb[:], d_col), (norm_sb[:], norm_col),
                (gw_sb[:], gate_t), (uw_sb[:], up_t),
            ]
            assert len(early) == N_EARLY and len(late) == N_LATE

            def x_load(b):
                sp.wait_ge(s_x2_done, b * NT + 1)
                sp.dma_start(x_sb[:], x[bass.ds(b, 1), :, :].rearrange("b (t p) d -> p (b t) d", p=P)).then_inc(s_x_in, 16)

            def head_load(b, h, par):
                sp.wait_ge(s_w_ready, b * SLOTS + h + 1)
                sp.dma_start(raw[:, par, :], wqkv[bass.ds(h, 1), :, :].rearrange("h p w -> p (h w)")).then_inc(w_in[par], 16)

            def pair_load(b, n, par):
                sp.wait_ge(s_w_ready, b * SLOTS + NH + n + 1)
                sp.dma_start(raw[:, par, 0:2 * D], w_pair[bass.ds(n, 1), :, :].rearrange("h p w -> p (h w)")).then_inc(w_in[par], 16)

            def out_load(b, n, par):
                sp.wait_ge(s_out_ready, b * NPAIR + n + 1)
                sp.dma_start(raw_out[:, par, :], w_out[bass.ds(n, 1), :, :].rearrange("h p d -> p (h d)")).then_inc(out_in[par], 16)

            def sequence(b, last):
                with sp.Fori(1, NH // 2) as i:
                    for par in range(2):
                        head_load(b, i * 2 + par, par)
                if not last:
                    x_load(b + 1)
                for n in range(2):
                    pair_load(b, n, n)
                with sp.Fori(0, NPAIR // 2 - 1) as i:
                    for par in range(2):
                        pair_load(b, i * 2 + par + 2, par)
                        out_load(b, i * 2 + par, par)
                for par in range(2):
                    if not last:
                        head_load(b + 1, par, par)
                    out_load(b, NPAIR - 2 + par, par)
                sp.wait_ge(s_y_done, b + 2)
                sp.dma_start(out[bass.ds(b, 1), :, :].rearrange("b (t p) d -> p (b t) d", p=P), x2[:]).then_inc(s_stored, 16)

            x_load(0)
            for h in range(2):
                head_load(0, h, h)
            for dst, src in early:
                sp.dma_start(dst, src).then_inc(s_loads, 16)
            for dst, src in late:
                sp.dma_start(dst, src).then_inc(s_late, 16)
            with sp.Fori(0, NB - 1) as b:
                sequence(b, False)
            sequence(NB - 1, True)
            sp.wait_ge(s_stored, 16 * NB + 16)

        @block.gpsimd
        def _(pool):
            for free, n in POOL_CREDITS:
                pool.sem_inc(free, n)
            pool.memset(ident[:], 0.0).then_inc(s_consts, 1)
            pool.memset(upto[:], 1.0).then_inc(s_consts, 1)
            pool.memset(after[:], 1.0).then_inc(s_consts, 1)
            pool.memset(ones[:], 1.0).then_inc(s_consts, 1)
            pool.memset(causal_bf[:], 0.0).then_inc(s_consts, 1)
            pool.memset(minus_half[:], -0.5).then_inc(s_consts, 1)
            pool.memset(ident_bf[:], 0.0).then_inc(s_consts, 1)
            pool.wait_ge(s_consts, 7)
            for t in (ident, ident_bf):
                pool.affine_select(out=t[:], in_=t[:], compare_op=ALU.not_equal, fill=1.0, base=0,
                                   pattern=[[-1, P]], channel_multiplier=1)
            pool.affine_select(out=upto[:], in_=upto[:], compare_op=ALU.is_ge, fill=0.0, base=0,
                               pattern=[[1, P]], channel_multiplier=-1)
            pool.affine_select(out=after[:], in_=after[:], compare_op=ALU.is_ge, fill=0.0, base=-1,
                               pattern=[[-1, P]], channel_multiplier=1)
            pool.affine_select(out=causal_bf[:], in_=causal_bf[:], compare_op=ALU.is_ge, fill=-1e10, base=0,
                               pattern=[[-1, P]], channel_multiplier=1).then_inc(s_consts, 1)

            def rstd_of(g, t0, t1):
                pool.wait_ge(s_ln_var, g + 1)
                pool.tensor_tensor(rstd[:, t0:t1], var_eps[:, t0:t1], minus_half[:, t0:t1], ALU.pow).then_inc(s_ln_rstd, 1)

            def split_low(slot, par, width):
                pool.wait_ge(s_w_hi, slot + 1)
                pool.tensor_tensor(w_r_flat[par][1][:, 0:width], raw[:, par, 0:width],
                                   w_r_flat[par][0][:, 0:width].bitcast(F32), ALU.subtract).then_inc(s_w_ready, 1)

            def weigh_x(b, n, par):
                N = b * NPAIR + n
                pool.wait_ge(s_xdt_ready, N + 1)
                pool.wait_ge(s_state_done, N + 1)
                pool.tensor_tensor(x_w.rearrange("p c (h q) -> p c h q", h=2),
                                   x_dt[:, par, 0:NT - 1, :].rearrange("p c (h q) -> p c h q", h=2),
                                   dec[:, 0:NT - 1, bass.ds(n * 2, 2)].unsqueeze(3).to_broadcast([P, NT - 1, 2, HD]),
                                   ALU.mult).then_inc(s_xw_ready, 1)

            def carry_states(b, n):
                N = b * NPAIR + n
                pool.wait_ge(s_state_ev, N + 2)
                for c in range(1, NT - 1):
                    if c > 1:
                        pool.wait_ge(s_carried, N * 4 + c * 2 - 2)
                    pool.tensor_tensor(carry[:].rearrange("p (h q) -> p h q", h=2),
                                       state[:, c - 1, :].rearrange("p (h q) -> p h q", h=2),
                                       dec[:, NT - 2 + c, bass.ds(n * 2, 2)].unsqueeze(2).to_broadcast([P, 2, HD]),
                                       ALU.mult).then_inc(s_carried, 1)
                    pool.wait_ge(s_carried, N * 4 + c * 2 - 1)
                    pool.tensor_tensor(state[:, c, :], state[:, c, :], carry[:], ALU.add).then_inc(s_carried, 1)

            def pick_heads(b, n, par):
                pool.tensor_tensor(pick[:, par, :], ident[:, bass.ds(n * 2, 2)], ident[:, bass.ds(n * 2 + MH, 2)],
                                   ALU.add).then_inc(s_pick_ready, 1)

            def hid_low(b, n, par):
                pool.wait_ge(s_hid_hi, b * NPAIR + n + 1)
                pool.tensor_tensor(hid_r[:, par, 1, :], hid, hid_r[:, par, 0, :].bitcast(F32), ALU.subtract).then_inc(s_hid_split, 1)

            def add_squares(b, n):
                N = b * NPAIR + n
                pool.wait_ge(s_squared, N + 2)
                pool.wait_ge(s_summed, N + b + 1)
                pool.tensor_tensor(sumsq[:], sumsq[:], square, ALU.add).then_inc(s_summed, 1)

            def normalised(b, first=False):
                rstd_of(b * 3, 0, NT)
                if not first:
                    x_bias(b)

            def x_bias(b):
                pool.wait_ge(s_late, 16 * N_LATE)
                pool.wait_ge(s_ln_xn, b * 3 + 1)
                pool.tensor_tensor(x_sb[:], x_sb[:], b0_bc[:].unsqueeze(1).to_broadcast([P, NT, D]), ALU.add).then_inc(s_x_bias, 1)

            def xn_low(k):
                pool.wait_ge(s_xn_hi, k + 1)
                for d in range(KT):
                    pool.tensor_tensor(xn_r[:, 1, d, :], xn_t[:, d, :], xn_r[:, 0, d, :].bitcast(F32), ALU.subtract).then_inc(s_xn_lo, 1)

            def sequence(b, last):
                with pool.Fori(1, NH // 2) as i:
                    for par in range(2):
                        split_low(b * SLOTS + i * 2 + par, par, 3 * D)
                pool.wait_ge(s_ss_done, b + 1)
                rstd_of(b * 3 + 1, 0, NT - 1)
                pool.memset(sumsq[:], 0.0).then_inc(s_summed, 1)
                rstd_of(b * 3 + 2, NT - 1, NT)
                pick_heads(b, 0, 0)
                pick_heads(b, 1, 1)
                xn_low(b * 2 + 1)
                split_low(b * SLOTS + NH, 0, 2 * D)
                split_low(b * SLOTS + NH + 1, 1, 2 * D)
                if not last:
                    normalised(b + 1)

                def pair(n, par, ahead, first=False):
                    weigh_x(b, n, par)
                    if ahead:
                        pick_heads(b, n + 2, par)
                        split_low(b * SLOTS + NH + n + 2, par, 2 * D)
                    elif not last:
                        split_low((b + 1) * SLOTS + par, par, 3 * D)
                        if par == 0:
                            xn_low(b * 2 + 2)
                    carry_states(b, n)
                    if not first:
                        hid_low(b, n - 1, 1 - par)
                        add_squares(b, n - 1)

                pool.wait_ge(s_dec_ready, b + 1)
                pair(0, 0, True, first=True)
                pair(1, 1, True)
                with pool.Fori(1, NPAIR // 2 - 1) as i:
                    for par in range(2):
                        pair(i * 2 + par, par, True)
                pair(NPAIR - 2, 0, False)
                pair(NPAIR - 1, 1, False)
                hid_low(b, NPAIR - 1, 1)
                add_squares(b, NPAIR - 1)
                pool.wait_ge(s_ms_ready, b + 1)
                pool.tensor_tensor(rms[:], ms_eps[:], minus_half[:], ALU.pow).then_inc(s_rms_ready, 1)

            normalised(0, first=True)
            xn_low(0)
            for h in range(2):
                split_low(h, h, 3 * D)
            x_bias(0)
            with pool.Fori(0, NB - 1) as b:
                sequence(b, False)
            sequence(NB - 1, True)

        @block.tensor
        def _(pe):
            for free, n in PE_CREDITS:
                pe.sem_inc(free, n)
            mm = pe.matmul

            def mm3(out, w, m, start, stop, **kw):
                for i, (a, b) in enumerate(((0, 1), (1, 0), (0, 0))):
                    ins = mm(out, lhsT=w(a), rhs=m(b), start=(start and i == 0), stop=(stop and i == 2), **kw)
                return ins

            pe.wait_ge(s_consts, NCONST)
            def turn_norm(g, tiles, banks):
                pe.wait_ge(s_ln_xn, g + 1)
                for d in range(KT):
                    for t in tiles:
                        ins = pe.transpose(bank[banks[d]][:, t * P:(t + 1) * P], xn[:, t, d * P:(d + 1) * P], ident[:])
                return ins

            def project(o, par, m, lows=None):
                for k in range(KT):
                    if lows is not None:
                        pe.wait_ge(s_xn_lo, lows + k + 1)
                    ins = mm3(o, lambda i: w_r[:, par, i, m, k, :], lambda i: xn_r[:, i, k, :], k == 0, k == KT - 1)
                return ins

            def project_qk(b, h, par, lows=None):
                N = b * NH + h
                pe.wait_ge(s_w_ready, b * SLOTS + h + 3)
                pe.wait_ge(s_v_ev, N + 1 - par)
                project(bank[0][:], par, 0, lows).then_inc(s_q_done, 1)
                pe.wait_ge(s_k_ev, N + 1)
                project(bank[1][:], par, 1).then_inc(s_k_done, 1)

            def project_v(b, j, par, bk):
                pe.wait_ge(s_w_ready, b * SLOTS + j + 4 - par)
                pe.wait_ge(s_q_ev, b * NH + j + 1)
                for x in range(NT // 2):
                    t = par * (NT // 2) + x
                    for k in range(KT):
                        ins = mm3(bank[bk][:, x * D:(x + 1) * D].rearrange("p (a e) -> p a e", a=2),
                                  lambda i: xn_r[:, i, k, t * P:(t + 1) * P], lambda i: w_r[:, :, i, 2, k, :], k == 0, k == KT - 1)
                ins.then_inc(s_v_done, 1)

            def score(b, h, par):
                N = b * NH + h
                pe.wait_ge(s_q_ev, N + 1)
                pe.wait_ge(s_k_ev, N + 2)
                pe.wait_ge(s_exp_done, N + 1)
                for q, bk, at in ((3, 2, 0), (2, 3, 0), (0, 3, 384), (1, 4, 0)):
                    w = (q + 1) * P
                    mm3(bank[bk][:, at:at + w], lambda i: q_r[:, i, q * P:(q + 1) * P], lambda i: k_r[:, i, 0:w], True, True)
                    mm(bank[bk][:, at + w - P:at + w], lhsT=ident_bf[:], rhs=causal_bf[:], start=False, stop=True,
                       skip_group_check=True).then_inc(s_scores_done, 1)

            def turn_probs(b, h, par):
                N = b * NH + h
                pe.wait_ge(s_norm_done, N + 1)
                pe.wait_ge(s_y_done, b + 1)
                pe.wait_ge(s_pt_a, N + 1)
                if par == 0:
                    pe.wait_ge(s_v_ev, N + 2)
                for q in range(NT):
                    ins = pe.transpose(bank[5][:, q * P:(q + 1) * P], prob[:, par, P_AT[q]:P_AT[q] + P], ident[:])
                ins.then_inc(s_turned_a, 1)
                pe.wait_ge(s_pt_b, N + 1)
                for k, q in ((1, 1), (1, 2), (1, 3), (3, 3)):
                    at = PT_AT[k] - PT_AT[1] + (q - k) * P
                    ins = pe.transpose(bank[6][:, at:at + P], prob[:, par, P_AT[q] + k * P:P_AT[q] + (k + 1) * P], ident[:])
                ins.then_inc(s_turned_b, 1)
                pe.wait_ge(s_z_ev, N + 1)
                for q in (2, 3):
                    ins = pe.transpose(bank[7][:, (q - 2) * P:(q - 1) * P], prob[:, par, P_AT[q] + 2 * P:P_AT[q] + 3 * P], ident[:])
                ins.then_inc(s_turned_c, 1)

            def weigh_values(b, h, par):
                N = b * NH + h
                pe.wait_ge(s_pt_a, N + 2)
                pe.wait_ge(s_pt_b, N + 2)
                pe.wait_ge(s_pt_c, N + 1)
                pe.wait_ge(s_v_ev, N + 3 - par)
                for k in range(NT):
                    ins = mm3(bank[7][:, k * P:W], lambda i: v_r[:, par, i, k, :], lambda i: prob_r[:, i, PT_AT[k]:PT_AT[k] + W - k * P],
                              k == 0, True, skip_group_check=True)
                ins.then_inc(s_z_done, 1)

            def out_tile(banks, t):
                return bank[banks[t // 2]][:, (t % 2) * D:(t % 2 + 1) * D]

            def out_heads(t, heads):
                for h in heads:
                    mm(bank[t][:, 0:D], lhsT=z_t[:, h, t * P:(t + 1) * P], rhs=wo_sb[:, h, :], start=(h == 0), stop=False)

            def attention_out(b):
                for t, first in ((2, 0), (0, NH - 2), (1, NH - 2), (3, 0)):
                    out_heads(t, range(first, NH - 2))
                    pe.wait_ge(s_z_ev, (b + 1) * NH + 1)
                    out_heads(t, range(NH - 2, NH))
                    for k in range(KT):
                        ins = mm(bank[t][:, 0:D], lhsT=xn_t[:, k, t * P:(t + 1) * P], rhs=w0_t[:, k, :],
                                 start=False, stop=(k == KT - 1))
                    ins.then_inc(s_attn_out, 1)

            def ffn_hidden(b, f):
                m = P if f < FT - 1 else FR
                pe.wait_ge(s_ffn_hid, b * FT + f + 1)
                for w, bk, done in ((gw_sb, FFN_BANKS[f % 2][0], s_ffn_gate), (uw_sb, FFN_BANKS[f % 2][1], s_ffn_up)):
                    for k in range(KT):
                        ins = mm(bank[bk][0:m, :], lhsT=w[:, k, f * P:f * P + m], rhs=xn_t[:, k, :], start=(k == 0), stop=(k == KT - 1))
                    ins.then_inc(done, 1)

            def ffn_down(b):
                pe.wait_ge(s_ffn_hid, (b + 1) * FT + 2)
                for t in range(NT):
                    for f in range(FT):
                        m = P if f < FT - 1 else FR
                        ins = mm(out_tile(FFN_BANKS[1], t), lhsT=f_hid[0:m, f, t * P:(t + 1) * P], rhs=dw_sb[0:m, f, :],
                                 start=(f == 0), stop=(f == FT - 1))
                ins.then_inc(s_ffn_out, 1)

            def mamba_start(b):
                for t in range(NT):
                    for k in range(KT):
                        ins = mm(bank[2][:, t * MH:(t + 1) * MH], lhsT=xn_t[:, k, t * P:(t + 1) * P], rhs=wdt_sb[:, k, :],
                                 start=(k == 0), stop=(k == KT - 1))
                ins.then_inc(s_dt_done, 1)
                for i in range(2):
                    for k in range(KT):
                        ins = mm(bank[i][:], lhsT=wbc_sb[:, k, i * P:(i + 1) * P], rhs=xn_t[:, k, :], start=(k == 0), stop=(k == KT - 1))
                    ins.then_inc(s_bc_done, 1)
                ffn_hidden(b, 0)
                pe.wait_ge(s_da_ready, b + 1)
                for i, (part, c) in enumerate([(after, c) for c in range(NT - 1)] + [(ones, c) for c in range(1, NT - 1)]):
                    ins = mm(bank[2][:, i * MH:(i + 1) * MH], lhsT=part[:], rhs=da[:, c, 0, :], start=True, stop=True)
                ins.then_inc(s_dec_done, 1)
                for t in range(NT):
                    ins = mm(bank[6][:, t * P:(t + 1) * P], lhsT=da[:, t, :, :].rearrange("p a h -> p (a h)"), rhs=upto[:],
                             start=True, stop=True)
                ins.then_inc(s_cum_done, 1)
                ffn_hidden(b, 1)
                pe.wait_ge(s_conv_silu, b * (NPAIR + 2) + 3)
                for t in range(NT):
                    ins = pe.transpose(bank[0][:, t * P:(t + 1) * P], b_t[:, t * P:(t + 1) * P], ident[:])
                ins.then_inc(s_b_turned, 1)
                for t in range(NT):
                    ins = mm(bank[1][:, t * P:(t + 1) * P], lhsT=b_t[:, t * P:(t + 1) * P], rhs=c_t[:, t * P:(t + 1) * P],
                             start=True, stop=True)
                ins.then_inc(s_cb_done, 1)
                pe.wait_ge(s_cum_ev, b + 1)
                pe.wait_ge(s_cum_split, b + 1)
                for t in range(NT):
                    ins = pe.transpose(bank[6][:, t * P:(t + 1) * P], cum[:, t * P:(t + 1) * P], ident[:])
                ins.then_inc(s_cum_turned, 1)
                ffn_hidden(b, 2)
                pe.wait_ge(s_xn_lo, (b * 2 + 2) * KT)
                pe.wait_ge(s_cb_ev, b + 1)
                project_x(b, 0, 0)
                ffn_hidden(b, 3)
                ffn_hidden(b, 4)
                ffn_hidden(b, 5)
                pe.wait_ge(s_b_ev, b + 1)
                project_gate(b, 0, 0)
                pe.wait_ge(s_dec_ready, b + 1)
                pe.wait_ge(s_cum_neg_ready, b + 1)
                pe.wait_ge(s_ffn_hid, b * FT + 7)
                spread_cum(b, 0, 0)
                ffn_down(b)
                mask_cum(b, 0)

            def project_x(b, n, par):
                N = b * NPAIR + n
                pe.wait_ge(s_w_ready, b * SLOTS + NH + n + 3)
                pe.wait_ge(s_taps_done, N + b * 2 + 2)
                project(bank[1][:], par, 1).then_inc(s_xc_done, 1)

            def project_gate(b, n, par):
                pe.wait_ge(s_gate_ready, b * NPAIR + n + 1)
                project(bank[0][:], par, 0).then_inc(s_w_used, 1)

            def spread_cum(b, n, par):
                N = b * NPAIR + n
                pe.wait_ge(s_pick_ready, N + 1)
                pe.wait_ge(s_mix_exp1, N + 1)
                for h in range(2):
                    ins = mm(bank[3 + h][:], lhsT=pick[:, par, h:h + 1].to_broadcast([P, P]), rhs=cum_r[:],
                             start=True, stop=True)
                ins.then_inc(s_cum_spread, 1)

            def mask_cum(b, n):
                pe.wait_ge(s_grow_ev, b * NPAIR + n + 1)
                for h, done in ((0, s_cum0_done), (1, s_cum1_done)):
                    mm(bank[3 + h][:].rearrange("p (t i) -> p t i", t=NT), lhsT=causal_bf[:],
                       rhs=ident_bf[:].unsqueeze(1).to_broadcast([P, NT, P]), start=False, stop=True,
                       skip_group_check=True).then_inc(done, 1)

            def turn_x(b, n, par):
                N = b * NPAIR + n
                pe.wait_ge(s_conv_silu, N + b * 2 + 4)
                pe.wait_ge(s_mix_exp0, N + 1)
                for t in range(NT):
                    ins = pe.transpose(bank[3][:, t * P:(t + 1) * P], xs[:, par, t * P:(t + 1) * P], ident[:])
                ins.then_inc(s_x_turned, 1)

            def make_states(b, n, par):
                N = b * NPAIR + n
                pe.wait_ge(s_xw_ready, N + 1)
                pe.wait_ge(s_off_scaled, N + 1)
                for c in range(NT - 1):
                    ins = mm(bank[2][:, c * P:(c + 1) * P], lhsT=b_sb[:, c, :], rhs=x_w[:, c, :], start=True, stop=True)
                ins.then_inc(s_state_done, 1)

            def off_block(b, n, par):
                N = b * NPAIR + n
                pe.wait_ge(s_carried, (N + 1) * 4)
                for c in range(1, NT):
                    ins = mm(bank[2][:, (c - 1) * P:c * P], lhsT=state[:, c - 1, :], rhs=c_t[:, c * P:(c + 1) * P], start=True, stop=True)
                ins.then_inc(s_off_done, 1)

            def in_block(b, n, par):
                N = b * NPAIR + n
                pe.wait_ge(s_mix_ready, N + 1)
                pe.wait_ge(s_xdt_ready, N + 1)
                pe.wait_ge(s_base_done, N + 1)
                for c in range(NT):
                    for h in range(2):
                        ins = mm(bank[5][h * HD:(h + 1) * HD, c * P:(c + 1) * P], lhsT=x_dt[:, par, c, h * HD:(h + 1) * HD],
                                 rhs=mix[:, par, h, c * P:(c + 1) * P], start=True, stop=True)
                ins.then_inc(s_diag_done, 1)

            def project_out(b, n, par, first, last):
                N = b * NPAIR + n
                pe.wait_ge(s_hid_split, N + 2)
                pe.wait_ge(s_out_ready, N + 3)
                for t in range(NT):
                    ins = mm3(out_tile((6, 7), t), lambda i: hid_r[:, par, i, t * P:(t + 1) * P], lambda i: wo_r[:, par, i, :],
                              first and t % 2 == 0, last, skip_group_check=True)
                ins.then_inc(s_projected, 1)

            def first_qk(b):
                project_qk(b, 0, 0, lows=b * 2 * KT)

            def sequence(b, last):
                def head(h, par, more):
                    if more:
                        project_qk(b, h + 1, 1 - par)
                    turn_probs(b, h, par)
                    if par == 0:
                        project_v(b, h + 1, 1, 0)
                    if more:
                        score(b, h + 1, 1 - par)
                    weigh_values(b, h, par)
                    if more and par == 1:
                        project_v(b, h + 1, 0, 5)

                with pe.Fori(0, NH // 2 - 1) as i:
                    for par in range(2):
                        head(i * 2 + par, par, True)
                head(NH - 2, 0, True)
                pe.wait_ge(s_late, 16 * N_LATE)
                pe.wait_ge(s_v_ev, (b + 1) * NH + 1)
                pe.wait_ge(s_z_ev, (b + 1) * NH - 1)
                out_heads(0, range(NH - 2))
                turn_probs(b, NH - 1, 1)
                pe.wait_ge(s_k_ev, (b + 1) * NH + 1)
                out_heads(1, range(NH - 2))
                weigh_values(b, NH - 1, 1)
                attention_out(b)

                turn_norm(b * 3 + 1, range(NT - 1), (0, 1))
                turn_norm(b * 3 + 2, (NT - 1,), (0, 1)).then_inc(s_ln_turned, 1)
                pe.wait_ge(s_ln_xnt, b * 2 + 2)
                pe.wait_ge(s_xnt_half, b * 2 + 2)
                mamba_start(b)
                pe.wait_ge(s_res_ready, b + 1)
                if not last:
                    turn_norm(b * 3 + 3, range(NT), (6, 7)).then_inc(s_ln_turned, 1)

                def pair(n, par, more, before=2):
                    turn_x(b, n, par)
                    if not more and not last:
                        pe.wait_ge(s_gate_ready, (b + 1) * NPAIR + 1)
                        pe.wait_ge(s_taps_done, (b + 1) * (NPAIR + 2))
                        first_qk(b + 1)
                    if more:
                        project_x(b, n + 1, 1 - par)
                    if before > 0:
                        off_block(b, n - 1, 1 - par)
                    if more:
                        pe.wait_ge(s_xdt_ready, b * NPAIR + n + 1)
                        spread_cum(b, n + 1, 1 - par)
                    if before > 1:
                        project_out(b, n - 2, par, isinstance(n, int) and n == 2, False)
                    if more:
                        mask_cum(b, n + 1)
                        project_gate(b, n + 1, 1 - par)
                    make_states(b, n, par)
                    in_block(b, n, par)

                pair(0, 0, True, before=0)
                pair(1, 1, True, before=1)
                if not last:
                    pe.wait_ge(s_ln_xnt, b * 2 + 3)
                    pe.wait_ge(s_xnt_half, b * 2 + 3)
                pair(2, 0, True)
                pair(3, 1, True)
                with pe.Fori(2, NPAIR // 2 - 1) as i:
                    for par in range(2):
                        pair(i * 2 + par, par, True)
                pair(NPAIR - 2, 0, True)
                pair(NPAIR - 1, 1, False)
                if not last:
                    project_v(b + 1, 0, 0, 0)
                off_block(b, NPAIR - 1, 1)
                project_out(b, NPAIR - 2, 0, False, False)
                if not last:
                    pe.wait_ge(s_off_scaled, (b + 1) * NPAIR + 1)
                    score(b + 1, 0, 0)
                    pe.wait_ge(s_v_ev, (b + 1) * NH + 2)
                project_out(b, NPAIR - 1, 1, False, True)
                pe.wait_ge(s_summed, (b + 1) * (NPAIR + 1))
                pe.wait_ge(s_base_done, (b + 1) * NPAIR + 1)
                for t in range(NT):
                    ins = mm(bank[5][:, t:t + 1], lhsT=sumsq[:, t * P:(t + 1) * P], rhs=ones[:, 0:1], start=True, stop=True)
                ins.then_inc(s_ss_done, 1)

            turn_norm(0, range(NT), (6, 7)).then_inc(s_ln_turned, 1)
            first_qk(0)
            project_v(0, 0, 0, 0)
            score(0, 0, 0)
            pe.wait_ge(s_v_ev, 2)
            pe.wait_ge(s_setup_dve, 3)
            for o in range(KT):
                for k in range(KT):
                    ins = pe.transpose(bank[5][:, k * D + o * P:k * D + (o + 1) * P], w0_sb[:, o, k * P:(k + 1) * P], ident[:])
            ins.then_inc(s_setup_pe, 1)
            pe.wait_ge(s_setup_dve, 4)
            with pe.Fori(0, NB - 1) as b:
                sequence(b, False)
            sequence(NB - 1, True)

        @block.scalar
        def _(act):
            for free, n in ACT_CREDITS:
                act.sem_inc(free, n)
            A = act.activation
            def copy_out(dst, src, done):
                A(dst, src, ACT.Copy).then_inc(done, 1)

            def high_out(dst, src, ready, count, done):
                act.wait_ge(ready, count)
                A(dst, src, ACT.Copy).then_inc(done, 1)

            def qk_high(b, h):
                N = b * NH + h
                high_out(q_r[:, 0, :], bank[0][:], s_q_done, N + 1, s_q_hi)
                high_out(k_r[:, 0, :], bank[1][:], s_k_done, N + 1, s_k_hi)

            def v_high(b, j, par, bk):
                high_out(v_r[:, :, 0, par * 2:par * 2 + 2, :], v_half(bk), s_v_done, b * NH + j + 1, s_v_hi)

            def w_high(slot, par, width):
                act.wait_ge(w_in[par], (slot - par + 2) * 8)
                A(w_r_flat[par][0][:, 0:width], raw[:, par, 0:width], ACT.Copy).then_inc(s_w_hi, 1)

            def exps(b, h, par):
                N = b * NH + h
                act.wait_ge(s_bias_done, N + 1)
                for q, bk, at in ((3, 2, 0), (2, 3, 0), (0, 3, 384), (1, 4, 0)):
                    w = (q + 1) * P
                    ins = A(prob[:, par, P_AT[q]:P_AT[q] + w], bank[bk][:, at:at + w], ACT.Exp,
                            bias=bias[:, par, q:q + 1], scale=SCALE, accum_out=total[:, par, q:q + 1])
                ins.then_inc(s_exp_done, 1)

            def probs_high(b, h):
                N = b * NH + h
                act.wait_ge(s_z_done, N + 1)
                high_out(prob_r[:, 0, 0:512], bank[5][:], s_turned_a, N + 1, s_pt_a_hi)
                high_out(prob_r[:, 0, 512:1024], bank[6][:], s_turned_b, N + 1, s_pt_b_hi)
                high_out(prob_r[:, 0, 1024:NP], bank[7][:, 0:256], s_turned_c, N + 1, s_pt_c_hi)

            def xn_high(k):
                act.wait_ge(s_ln_xnt, k + 1)
                act.wait_ge(s_xnt_half, k + 1)
                A(xn_r[:, 0, :, :], xn_t[:], ACT.Copy).then_inc(s_xn_hi, 1)

            def out_high(b, n, par):
                N = b * NPAIR + n
                act.wait_ge(out_in[par], (N - par + 2) * 8)
                act.wait_ge(s_projected, N + 1)
                A(wo_r[:, par, 0, :], raw_out[:, par, :], ACT.Copy, scale=norm_sb[:, bass.ds(n, 1)]).then_inc(s_out_hi, 1)

            def hid_high(b, n, par):
                N = b * NPAIR + n
                act.wait_ge(s_hid_ready, N + 2)
                act.wait_ge(s_projected, N + 1)
                A(hid_r[:, par, 0, :], hid, ACT.Copy).then_inc(s_hid_hi, 1)

            def squares(b, n):
                N = b * NPAIR + n
                act.wait_ge(s_hid_ready, N + 2)
                act.wait_ge(s_summed, N + b + 1)
                A(square, hid, ACT.Square).then_inc(s_squared, 1)

            def gate_tanh(b, n, par):
                N = b * NPAIR + n
                act.wait_ge(s_w_used, b * NPAIR + n + 1)
                act.wait_ge(s_gate_ready, N + 1)
                A(gate_th[:], bank[0][:], ACT.Tanh, scale=0.5).then_inc(s_gate_tanh, 1)

            def tap_now(k, ch, src):
                act.wait_ge(s_conv_silu, k + 1)
                A(conv_acc[:], src, ACT.Identity, bias=conv_sb[:, ch, TAPS:TAPS + 1],
                  scale=conv_sb[:, ch, TAPS - 1:TAPS]).then_inc(s_tap0, 1)

            def conv_tanh(k):
                act.wait_ge(s_taps_done, k + 1)
                A(conv_th[:], conv_acc[:], ACT.Tanh).then_inc(s_conv_tanh, 1)

            def pair_conv_start(b, n):
                act.wait_ge(s_xc_done, b * NPAIR + n + 1)
                tap_now(b * (NPAIR + 2) + 2 + n, n if isinstance(n, int) else bass.ds(n, 1), bank[1][:])

            def ffn_tanh(b, f):
                m = P if f < FT - 1 else FR
                act.wait_ge(s_ffn_gate, b * FT + f + 1)
                act.wait_ge(s_ffn_silu, b * FT + f + 1)
                A(f_th[0:m, f % 2, :], bank[FFN_BANKS[f % 2][0]][0:m, :], ACT.Tanh, scale=gs_sb[0:m, f:f + 1]).then_inc(s_ffn_tanh, 1)

            def xn_half(k, bk):
                act.wait_ge(s_ln_turned, k + 1)
                copy_out(xn_t[:, 0, :], bank[bk][:], s_xnt_half)

            def sequence(b, last):
                def head(h, par, more, ahead):
                    if ahead and par == 1:
                        act.wait_ge(s_v_done, b * NH + h + 1)
                        w_high(b * SLOTS + h + 2, par, 3 * D)
                    if more:
                        qk_high(b, h + 1)
                    probs_high(b, h)
                    if par == 0:
                        v_high(b, h + 1, 1, 0)
                    if ahead and par == 0:
                        act.wait_ge(s_v_done, b * NH + h + 2)
                        w_high(b * SLOTS + h + 2, par, 3 * D)
                    if more:
                        exps(b, h + 1, 1 - par)
                        if par == 1:
                            v_high(b, h + 1, 0, 5)

                with act.Fori(0, NH // 2 - 1) as i:
                    for par in range(2):
                        head(i * 2 + par, par, True, True)
                head(NH - 2, 0, True, False)
                head(NH - 1, 1, False, False)

                act.wait_ge(s_late, 16 * N_LATE)
                xn_half(b * 2 + 1, 0)
                K = b * (NPAIR + 2)
                act.wait_ge(s_dt_absed, b + 1)
                A(dt_sb[:], dt_tmp[:], ACT.Exp, scale=-1.0).then_inc(s_dt_exp, 1)
                act.wait_ge(s_bc_done, b * 2 + 1)
                tap_now(K, NPAIR, bank[0][:])
                act.wait_ge(s_dt_exp, b + 1)
                A(dt_tmp[:], dt_sb[:], ACT.Ln, bias=1.0).then_inc(s_dt_ln, 1)
                conv_tanh(K)
                ffn_tanh(b, 0)
                act.wait_ge(s_bc_done, b * 2 + 2)
                tap_now(K + 1, NPAIR + 1, bank[1][:])
                xn_high(b * 2 + 1)
                conv_tanh(K + 1)
                act.wait_ge(s_dec_done, b + 1)
                A(dec[:].rearrange("p c h -> p (c h)"), bank[2][:, 0:(2 * NT - 3) * MH], ACT.Exp).then_inc(s_dec_ready, 1)
                act.wait_ge(s_cum_done, b + 1)
                copy_out(cum_r[:], bank[6][:], s_cum_hi)
                ffn_tanh(b, 1)
                act.wait_ge(s_v_done, (b + 1) * NH)
                w_high(b * SLOTS + NH, 0, 2 * D)
                w_high(b * SLOTS + NH + 1, 1, 2 * D)
                act.wait_ge(s_b_turned, b + 1)
                copy_out(b_sb[:].rearrange("p t n -> p (t n)"), bank[0][:], s_b_ev)
                ffn_tanh(b, 2)
                pair_conv_start(b, 0)
                conv_tanh(K + 2)
                ffn_tanh(b, 3)
                ffn_tanh(b, 4)
                ffn_tanh(b, 5)
                gate_tanh(b, 0, 0)

                def decays(n, par):
                    N = b * NPAIR + n
                    act.wait_ge(s_cum_spread, N + 1)
                    for h in range(2):
                        ins = A(grow[h * HD:(h + 1) * HD, par, 0:W - P], bank[3 + h][h * HD:(h + 1) * HD, P:W], ACT.Exp)
                    ins.then_inc(s_grow_ev, 1)

                def mixes(n, par, h):
                    act.wait_ge((s_cum0_done, s_cum1_done)[h], b * NPAIR + n + 1)
                    for c in range(NT):
                        ins = A(mix[:, par, h, c * P:(c + 1) * P], bank[3 + h][:, c * P:(c + 1) * P], ACT.Exp,
                                bias=cum_neg[:, c, bass.ds(n * 2 + h, 1)])
                    ins.then_inc((s_mix_exp0, s_mix_exp1)[h], 1)

                decays(0, 0)
                mixes(0, 0, 0)
                mixes(0, 0, 1)
                if not last:
                    xn_half(b * 2 + 2, 6)

                def pair(n, par, more, ahead, first=False):
                    N = b * NPAIR + n
                    if more:
                        pair_conv_start(b, n + 1)
                    if ahead:
                        act.wait_ge(s_w_used, N + 1)
                        w_high(b * SLOTS + NH + n + 2, par, 2 * D)
                    elif not last:
                        act.wait_ge(s_w_used, N + 1)
                        w_high((b + 1) * SLOTS + par, par, 3 * D)
                        if par == 1:
                            qk_high(b + 1, 0)
                    if more:
                        act.wait_ge(s_off_scaled, N + 1)
                        decays(n + 1, 1 - par)
                        if not ahead and not last:
                            act.wait_ge(s_w_used, N + 2)
                            xn_high(b * 2 + 2)
                        mixes(n + 1, 1 - par, 0)
                    if not first:
                        hid_high(b, n - 1, 1 - par)
                    if more:
                        conv_tanh(K + n + 3)
                    act.wait_ge(s_state_done, N + 2)
                    act.wait_ge(s_off_done, N + 1)
                    copy_out(state[:].rearrange("p c q -> p (c q)"), bank[2][:, 0:W - P], s_state_ev)
                    if more:
                        gate_tanh(b, n + 1, 1 - par)
                    out_high(b, n, par)
                    if more:
                        mixes(n + 1, 1 - par, 1)
                    if not first:
                        squares(b, n - 1)

                pair(0, 0, True, True, first=True)
                pair(1, 1, True, True)
                with act.Fori(1, NPAIR // 2 - 1) as i:
                    for par in range(2):
                        pair(i * 2 + par, par, True, True)
                pair(NPAIR - 2, 0, True, False)
                pair(NPAIR - 1, 1, False, False)
                if not last:
                    v_high(b + 1, 0, 0, 0)
                hid_high(b, NPAIR - 1, 1)
                squares(b, NPAIR - 1)
                if not last:
                    exps(b + 1, 0, 0)

            xn_half(0, 6)
            xn_high(0)
            for h in range(2):
                w_high(h, h, 3 * D)
            qk_high(0, 0)
            v_high(0, 0, 0, 0)
            exps(0, 0, 0)
            act.wait_ge(s_loads, 16 * N_EARLY)
            A(exp_a[:], exp_a[:], ACT.Exp).then_inc(s_setup_act, 1)
            act.wait_ge(s_setup_dve, 6)
            with act.Fori(0, NB - 1) as b:
                sequence(b, False)
            sequence(NB - 1, True)

        @block.vector
        def _(dve):
            for free, n in DVE_CREDITS:
                dve.sem_inc(free, n)
            stt = dve.scalar_tensor_tensor
            tt = dve.tensor_tensor
            ts = dve.tensor_scalar
            def low_of(dst, src, high, ready, count, done):
                dve.wait_ge(ready, count)
                tt(dst, src, high.bitcast(F32), ALU.subtract).then_inc(done, 1)

            def ln_stats(g, src, tiles):
                for t in tiles:
                    ins = dve.bn_stats(stats[:, t, :], src[:, t, :])
                ins.then_inc(s_ln_stats, 1)
                dve.wait_ge(s_ln_stats, g * 2 + 1)
                dve.memset(spacer[:], 0.0)
                for t in tiles:
                    ins = dve.bn_aggr(meanvar[:, t, :], stats[:, t, :])
                ins.then_inc(s_ln_stats, 1)
                dve.wait_ge(s_ln_stats, g * 2 + 2)
                ts(var_eps[:, tiles[0]:tiles[-1] + 1], meanvar[:, tiles[0]:tiles[-1] + 1, 1:2].rearrange("p t o -> p (t o)"),
                   EPS, None, ALU.add).then_inc(s_ln_var, 1)

            def ln_apply(g, src, tiles):
                dve.wait_ge(s_ln_rstd, g + 1)
                for t in tiles:
                    ins = ts(xn[:, t, :], src[:, t, :], meanvar[:, t, 0:1], rstd[:, t:t + 1], ALU.subtract, ALU.mult)
                ins.then_inc(s_ln_xn, 1)

            def ln_out(k, bk):
                dve.wait_ge(s_ln_turned, k + 1)
                dve.tensor_copy(xn_t[:, 1, :], bank[bk][:]).then_inc(s_ln_xnt, 1)

            def qk_low(b, h):
                N = b * NH + h
                low_of(q_r[:, 1, :], bank[0][:], q_r[:, 0, :], s_q_hi, N + 1, s_q_ev)
                low_of(k_r[:, 1, :], bank[1][:], k_r[:, 0, :], s_k_hi, N + 1, s_k_ev)

            def v_low(b, j, par, bk):
                low_of(v_r[:, :, 1, par * 2:par * 2 + 2, :], v_half(bk), v_r[:, :, 0, par * 2:par * 2 + 2, :],
                       s_v_hi, b * NH + j + 1, s_v_ev)

            def probs_low(b, h):
                N = b * NH + h
                for lo, up, bk, ready, done in ((0, 512, 5, s_pt_a_hi, s_pt_a), (512, 1024, 6, s_pt_b_hi, s_pt_b), (1024, NP, 7, s_pt_c_hi, s_pt_c)):
                    low_of(prob_r[:, 1, lo:up], bank[bk][:, 0:up - lo], prob_r[:, 0, lo:up], ready, N + 1, done)

            def maxima(b, h, par):
                N = b * NH + h
                for j, (q, bk, at) in enumerate(((3, 2, 0), (2, 3, 0), (0, 3, 384), (1, 4, 0))):
                    w = (q + 1) * P
                    dve.wait_ge(s_scores_done, N * NT + (j + 1 if bk != 3 else 3))
                    ins = dve.tensor_reduce(neg_max[:, par, q:q + 1], bank[bk][:, at:at + w], AX_X, ALU.max, negate=True)
                ins.then_inc(s_max_done, 1)
                dve.wait_ge(s_max_done, N + 1)
                ts(bias[:, par, :], neg_max[:, par, :], SCALE, None, ALU.mult).then_inc(s_bias_done, 1)

            def normalise(b, h, par):
                N = b * NH + h
                dve.wait_ge(s_exp_done, N + 2)
                dve.reciprocal(inv_total[:, par, :], total[:, par, :]).then_inc(s_inv_done, 1)
                dve.wait_ge(s_inv_done, N + 1)
                for q in range(NT):
                    pr = prob[:, par, P_AT[q]:P_AT[q] + (q + 1) * P]
                    ins = ts(pr, pr, inv_total[:, par, q:q + 1], None, ALU.mult)
                ins.then_inc(s_norm_done, 1)

            def pair_gate(b, n, par):
                N = b * NPAIR + n
                dve.wait_ge(s_gate_tanh, N + 1)
                stt(out=gate[:, par, :], in0=gate_th[:], scalar=1.0, in1=bank[0][:], op0=ALU.add, op1=ALU.mult).then_inc(s_gate_ready, 1)

            def conv_tap(k, ch, src, back):
                dve.wait_ge((s_tap0, s_tap1, s_tap2)[back - 1], k + 1)
                stt(out=conv_acc[:, back:W], in0=src[:, 0:W - back], scalar=conv_sb[:, ch, TAPS - 1 - back:TAPS - back],
                    in1=conv_acc[:, back:W], op0=ALU.mult, op1=ALU.add).then_inc((s_tap1, s_tap2, s_taps_done)[back - 1], 1)

            def conv_taps(k, ch, src):
                for back in range(1, TAPS):
                    conv_tap(k, ch, src, back)

            def conv_end(k, dst):
                dve.wait_ge(s_conv_tanh, k + 1)
                stt(out=dst, in0=conv_th[:], scalar=1.0, in1=conv_acc[:], op0=ALU.add, op1=ALU.mult).then_inc(s_conv_silu, 1)

            def ffn_hid(b, f):
                m = P if f < FT - 1 else FR
                o, u = FFN_BANKS[f % 2]
                N = b * FT + f
                dve.wait_ge(s_ffn_tanh, N + 1)
                dve.wait_ge(s_ffn_hid, N + 1)
                stt(out=f_silu[0:m, f % 2, :], in0=f_th[0:m, f % 2, :], scalar=1.0, in1=bank[o][0:m, :], op0=ALU.add, op1=ALU.mult).then_inc(s_ffn_silu, 1)
                dve.wait_ge(s_ffn_silu, N + 3)
                dve.wait_ge(s_ffn_up, N + 1)
                stt(out=f_hid[0:m, f, :], in0=bank[u][0:m, :], scalar=us_sb[0:m, f:f + 1], in1=f_silu[0:m, f % 2, :], op0=ALU.mult, op1=ALU.mult).then_inc(s_ffn_hid, 1)

            def wide(t):
                return t[:].rearrange("p t h -> p (t h)")

            def first_layernorm(b):
                dve.wait_ge(s_x_in, (b + 1) * 16)
                ln_stats(b * 3, x_sb, range(NT))
                ln_apply(b * 3, x_sb, range(NT))

            def sequence(b, last):
                def head(h, par, more):
                    N = b * NH + h
                    if more:
                        qk_low(b, h + 1)
                    probs_low(b, h)
                    if par == 0:
                        v_low(b, h + 1, 1, 0)
                    if more:
                        maxima(b, h + 1, 1 - par)
                    dve.wait_ge(s_z_done, N + 2)
                    dst = z_t[:, h, :] if isinstance(h, int) else z_t[:, bass.ds(h, 1), :].rearrange("p h w -> p (h w)")
                    dve.tensor_copy(dst, bank[7][:]).then_inc(s_z_ev, 1)
                    if more:
                        normalise(b, h + 1, 1 - par)
                        if par == 1:
                            v_low(b, h + 1, 0, 5)

                with dve.Fori(0, NH // 2 - 1) as i:
                    for par in range(2):
                        head(i * 2 + par, par, True)
                head(NH - 2, 0, True)
                head(NH - 1, 1, False)

                dve.wait_ge(s_late, 16 * N_LATE)
                dve.wait_ge(s_x_bias, b + 1)
                dve.wait_ge(s_stored, b * 16 + 16)
                for i, t in enumerate((2, 0, 1, 3)):
                    dve.wait_ge(s_attn_out, b * NT + i + 1)
                    tt(x2[:, t, :], bank[t][:, 0:D], x_sb[:, t, :], ALU.add).then_inc(s_x2_done, 1)
                    if t == 1:
                        dve.wait_ge(s_x2_done, b * NT + i + 2)
                        ln_stats(b * 3 + 1, x2, range(NT - 1))
                        ln_apply(b * 3 + 1, x2, range(NT - 1))
                dve.wait_ge(s_x2_done, (b + 1) * NT + 1)
                ln_stats(b * 3 + 2, x2, (NT - 1,))
                ln_apply(b * 3 + 2, x2, (NT - 1,))
                ln_out(b * 2 + 1, 1)
                K = b * (NPAIR + 2)
                dve.wait_ge(s_dt_done, b + 1)
                tt(dt_raw[:], bank[2][:, 0:NT * MH].rearrange("p (t h) -> p t h", t=NT),
                   dtb_bc[:].unsqueeze(1).to_broadcast([P, NT, MH]), ALU.add).then_inc(s_dt_biased, 1)
                dve.wait_ge(s_dt_biased, b + 1)
                stt(out=wide(dt_tmp), in0=wide(dt_raw), scalar=-1.0, in1=wide(dt_raw), op0=ALU.mult, op1=ALU.max).then_inc(s_dt_absed, 1)
                conv_taps(K, NPAIR, bank[0])
                dve.wait_ge(s_dt_ln, b + 1)
                stt(out=wide(dt_sb), in0=wide(dt_raw), scalar=0.0, in1=wide(dt_tmp), op0=ALU.max, op1=ALU.add).then_inc(s_dt_ready, 1)
                dve.wait_ge(s_dt_ready, b + 1)
                for i in range(2):
                    ins = stt(out=da[:, :, i, :], in0=dt_sb[:], scalar=-1.0, in1=exp_a[:].unsqueeze(1).to_broadcast([P, NT, MH]),
                              op0=ALU.mult, op1=ALU.mult)
                ins.then_inc(s_da_ready, 1)
                conv_end(K, b_t[:])
                ffn_hid(b, 0)
                conv_taps(K + 1, NPAIR + 1, bank[1])
                conv_end(K + 1, c_t[:])
                dve.wait_ge(s_cum_hi, b + 1)
                dve.tensor_copy(cum, bank[6][:]).then_inc(s_cum_ev, 1)
                low_of(cum_r[MH:P, :], bank[6][MH:P, :], cum_r[MH:P, :], s_cum_hi, b + 1, s_cum_split)
                ffn_hid(b, 1)
                dve.wait_ge(s_cb_done, b + 1)
                dve.tensor_copy(cb[:].rearrange("p t i -> p (t i)"), bank[1][:]).then_inc(s_cb_ev, 1)
                dve.wait_ge(s_cum_turned, b + 1)
                ts(cum_neg[:], bank[6][:].rearrange("p (t h) -> p t h", t=NT)[:, :, 0:MH], -1.0, None, ALU.mult).then_inc(s_cum_neg_ready, 1)
                ffn_hid(b, 2)
                conv_taps(K + 2, 0, bank[1])
                conv_end(K + 2, xs[:, 0, :])
                for f in range(3, FT):
                    ffn_hid(b, f)
                pair_gate(b, 0, 0)
                if not last:
                    first_layernorm(b + 1)
                dve.wait_ge(s_ffn_out, b + 1)
                for i in range(2):
                    part = x2[:, 2 * i:2 * i + 2, :].rearrange("p t d -> p (t d)")
                    ins = tt(part, bank[FFN_BANKS[1][i]][:], part, ALU.add)
                ins.then_inc(s_res_ready, 1)
                if not last:
                    ln_out(b * 2 + 2, 7)

                def out_low(n, par):
                    dve.wait_ge(s_out_hi, b * NPAIR + n + 1)
                    stt(out=wo_r[:, par, 1, :], in0=raw_out[:, par, :], scalar=norm_sb[:, bass.ds(n, 1)],
                        in1=wo_r[:, par, 0, :].bitcast(F32), op0=ALU.mult, op1=ALU.subtract).then_inc(s_out_ready, 1)

                def tail(n, par):
                    N = b * NPAIR + n

                    def base():
                        dve.wait_ge(s_diag_done, N + 1)
                        stt(out=y, in0=xs[:, par, :], scalar=d_sb[:, n:n + 1] if isinstance(n, int) else d_sb[:, bass.ds(n, 1)],
                            in1=bank[5][:], op0=ALU.mult, op1=ALU.add).then_inc(s_base_done, 1)

                    def off():
                        dve.wait_ge(s_off_done, N + 2)
                        dve.wait_ge(s_grow_ev, N + 1)
                        tt(y_in[:], bank[2][:, 0:W - P], grow[:, par, 0:W - P], ALU.mult).then_inc(s_off_scaled, 1)

                    def total_y():
                        dve.wait_ge(s_off_scaled, N + 2)
                        dve.wait_ge(s_base_done, N + 2)
                        tt(y[:, P:W], y[:, P:W], y_in[:], ALU.add).then_inc(s_y_ready, 1)

                    def gated():
                        dve.wait_ge(s_y_ready, N + 1)
                        dve.wait_ge(s_squared, N + 1)
                        dve.wait_ge(s_hid_split, N + 1)
                        tt(hid, y, gate[:, par, :], ALU.mult).then_inc(s_hid_ready, 1)

                    return base, off, total_y, gated

                def mixed(par, h):
                    return tt(mix[:, par, h, :], mix[:, par, h, :], cb[:].rearrange("p t i -> p (t i)"), ALU.mult)

                def pair(n, par, more, first=False):
                    N = b * NPAIR + n
                    ch = n + 1 if isinstance(n, int) else bass.ds(n + 1, 1)
                    if not first:
                        base, off, total_y, gated = tail(n - 1, 1 - par)
                        dve.wait_ge(s_hid_ready, N)
                        base()
                    dve.wait_ge(s_conv_silu, K + n + 4)
                    dve.wait_ge(s_x_turned, N + 1)
                    tt(x_dt[:, par, :, :].rearrange("p t (h q) -> p t h q", h=2),
                       bank[3][:].rearrange("p (t h q) -> p t h q", t=NT, h=2),
                       dt_sb[:, :, bass.ds(n * 2, 2)].unsqueeze(3).to_broadcast([P, NT, 2, HD]), ALU.mult).then_inc(s_xdt_ready, 1)
                    dve.wait_ge(s_mix_exp0, N + 1)
                    mixed(par, 0)
                    dve.wait_ge(s_mix_exp1, N + 2)
                    mixed(par, 1).then_inc(s_mix_ready, 1)
                    if not first:
                        off()
                    if more:
                        conv_tap(K + n + 3, ch, bank[1], 1)
                    if not first:
                        total_y()
                    if more:
                        conv_tap(K + n + 3, ch, bank[1], 2)
                    if not first:
                        gated()
                    if more:
                        conv_tap(K + n + 3, ch, bank[1], 3)
                    elif not last:
                        qk_low(b + 1, 0)
                    if not first:
                        out_low(n - 1, 1 - par)
                    if more:
                        conv_end(K + n + 3, xs[:, 1 - par, :])
                        if not first:
                            dve.wait_ge(s_hid_ready, N + 1)
                        pair_gate(b, n + 1, 1 - par)

                pair(0, 0, True, first=True)
                pair(1, 1, True)
                with dve.Fori(1, NPAIR // 2 - 1) as i:
                    for par in range(2):
                        pair(i * 2 + par, par, True)
                pair(NPAIR - 2, 0, True)
                pair(NPAIR - 1, 1, False)
                out_low(NPAIR - 1, 1)
                if not last:
                    v_low(b + 1, 0, 0, 0)
                for step in tail(NPAIR - 1, 1):
                    step()
                if not last:
                    maxima(b + 1, 0, 0)
                dve.wait_ge(s_ss_done, b + 2)
                ts(ms_eps[:], bank[5][:, 0:NT], 1.0 / (NPAIR * P), 4 * EPS, ALU.mult, ALU.add).then_inc(s_ms_ready, 1)
                if not last:
                    normalise(b + 1, 0, 0)
                dve.wait_ge(s_res_ready, b + 1)
                dve.wait_ge(s_rms_ready, b + 1)
                dve.wait_ge(s_projected, (b + 1) * NPAIR + 2)
                for t in range(NT):
                    ins = stt(out=x2[:, t, :], in0=bank[6 + t // 2][:, (t % 2) * D:(t % 2 + 1) * D], scalar=rms[:, t:t + 1],
                              in1=x2[:, t, :], op0=ALU.mult, op1=ALU.add)
                ins.then_inc(s_y_done, 1)

            first_layernorm(0)
            ln_out(0, 7)
            qk_low(0, 0)
            v_low(0, 0, 0, 0)
            maxima(0, 0, 0)
            normalise(0, 0, 0)
            dve.wait_ge(s_loads, 16 * N_EARLY)
            dve.wait_ge(s_setup_act, 1)
            dve.tensor_reduce(w0_abs[:], w0_sb[:], AX_X, ALU.add, apply_absolute_value=True).then_inc(s_setup_dve, 1)
            ts(w0_sign[:], w0_sb[:], 0.0, 2.0, ALU.is_ge, ALU.mult).then_inc(s_setup_dve, 1)
            dve.wait_ge(s_setup_dve, 2)
            ts(w0_sign[:], w0_sign[:], -1.0, 1.0 / D, ALU.add, ALU.mult).then_inc(s_setup_sign, 1)
            dve.wait_ge(s_setup_sign, 1)
            for o in range(KT):
                ins = stt(out=w0_t[:, o, :], in0=w0_sign[:, o, :], scalar=w0_abs[:, o:o + 1], in1=w0_sb[:, o, :], op0=ALU.mult, op1=ALU.subtract)
            ins.then_inc(s_setup_sign, 1)
            dve.wait_ge(s_setup_sign, 2)
            tt(w0_sb[:], w0_t[:], w0_sb[:], ALU.add).then_inc(s_setup_dve, 1)
            dve.wait_ge(s_setup_pe, 1)
            dve.tensor_copy(w0_t[:].rearrange("p k d -> p (k d)"), bank[5][:]).then_inc(s_setup_dve, 1)
            ts(conv_sb[:], conv_sb[:], 0.5, None, ALU.mult)
            ts(gs_sb[:], gs_sb[:], 0.5, None, ALU.mult).then_inc(s_setup_dve, 1)
            dve.wait_ge(s_setup_dve, 5)
            tt(us_sb[:], us_sb[:], gs_sb[:], ALU.mult)
            tt(dw_sb[:, 0:FT - 1, :], dw_sb[:, 0:FT - 1, :], ds_bc[:].unsqueeze(1).to_broadcast([P, FT - 1, D]), ALU.mult)
            tt(dw_sb[0:FR, FT - 1, :], dw_sb[0:FR, FT - 1, :], ds_bc[0:FR, :], ALU.mult).then_inc(s_setup_dve, 1)
            dve.wait_ge(s_setup_dve, 6)
            with dve.Fori(0, NB - 1) as b:
                sequence(b, False)
            sequence(NB - 1, True)


def kernel(**inputs):
    import numpy as np
    import concourse.bacc as bacc
    from concourse.bass_utils import run_bass_kernel_spmd as run

    a = {k: np.asarray(v) for k, v in inputs.items()}

    def tiles(w_t):
        return w_t.reshape(-1, P, w_t.shape[1]).transpose(1, 0, 2)

    NH, DH, D = a["L0_attn_W_Q"].shape
    qkv = np.stack([a[f"L0_attn_W_{c}"] for c in "QKV"])
    qkv = qkv.reshape(3, NH, DH, D // P, P).transpose(1, 4, 0, 3, 2)
    w_in = a["L1_attn_in_proj_w"]
    inner = a["L1_attn_norm_w"].shape[0]
    pairs = inner // P
    both = np.stack([w_in[:, 0:inner], w_in[:, inner:2 * inner]])
    both = both.reshape(2, D // P, P, pairs, P).transpose(3, 2, 0, 1, 4)
    conv = np.concatenate([a["L1_attn_conv_w"], a["L1_attn_conv_b"][:, None]], axis=1)
    F = a["L1_ffn_gate_w"].shape[0]
    ft = -(-F // P)

    def column(v):
        c = np.zeros((ft * P,), v.dtype)
        c[:F] = v
        return c.reshape(ft, P).T

    per_head = inner // a["L1_attn_D_param"].shape[0]
    arrays = {
        "x": a["L0_attn_x"],
        "wqkv": qkv.reshape(NH, P, -1),
        "wo_t": a["L0_attn_W_O"].T.reshape(NH, DH, D).transpose(1, 0, 2),
        "w0": tiles(a["L0_ffn_weight"]),
        "b0": a["L0_ffn_bias"],
        "w_pair": both.reshape(pairs, P, -1),
        "w_out": a["L1_attn_out_proj_w"].reshape(pairs, P, -1),
        "w_bc": tiles(w_in[:, 2 * inner:2 * inner + 2 * P]),
        "w_dt": tiles(w_in[:, 2 * inner + 2 * P:]),
        "conv_par": conv.reshape(pairs + 2, P, -1).transpose(1, 0, 2),
        "dt_bias": a["L1_attn_dt_bias"],
        "a_log": a["L1_attn_A_log"],
        "d_col": np.repeat(a["L1_attn_D_param"], per_head).reshape(pairs, P).T,
        "norm_col": a["L1_attn_norm_w"].reshape(pairs, P).T,
        "gate_t": tiles(a["L1_ffn_gate_w"].T),
        "up_t": tiles(a["L1_ffn_up_w"].T),
        "down_t": a["L1_ffn_down_w"].T,
        "gate_s": column(a["L1_ffn_gate_s"]),
        "up_s": column(a["L1_ffn_up_s"]),
        "down_s": a["L1_ffn_down_s"],
    }
    nc = bacc.Bacc("TRN2", target_bir_lowering=False, num_devices=1)
    fed, aps = {}, {}
    for name, v in arrays.items():
        v = np.ascontiguousarray(v)
        fed[f"in_{name}"] = v
        aps[name] = nc.dram_tensor(f"in_{name}", v.shape, mybir.dt.from_np(v.dtype), kind="ExternalInput").ap()
    aps["out"] = nc.dram_tensor("out_0", arrays["x"].shape, F32, kind="ExternalOutput").ap()
    two_layers(nc, **aps)
    return run(nc, [fed], core_ids=[0]).results[0]["out_0"]
```
